# Optimizing a Trainium2 kernel written in Bass

```python
import numpy as np
import jax
import jax.numpy as jnp

def _softmax(x, axis=-1):
    return jax.nn.softmax(x, axis=axis)

def _gelu(x):
    return jax.nn.gelu(x, approximate=True)

def _silu(x):
    return jax.nn.silu(x)

def _sigmoid(x):
    return jax.nn.sigmoid(x)

def _layernorm(x, axis=-1, eps=1e-05):
    m = jnp.mean(x, axis=axis, keepdims=True)
    v = jnp.var(x, axis=axis, keepdims=True)
    return (x - m) / jnp.sqrt(v + eps)

def _scatter_add(tgt, idx, src, axis=0):
    return tgt.at[idx].add(src)

def _segment_sum(src, seg, n):
    return jax.ops.segment_sum(src, seg, n)
kernel_name = 'mk_adaln_d1_jaxref_r8_51a8cb'

def setup_inputs(seed: int=0):
    np.random.seed(seed)
    _w = jnp.asarray

    def _L0_attn_setup():
        import jax, jax.numpy as jnp
        import numpy as np
        import math
        D = 256
        H = 16
        HKV = 4
        HD = 128
        S = 32
        TOPK = 8
        RD = 32
        EPS = 1e-05

        def rms(x, w):
            var = jnp.mean(jnp.square(x), axis=-1, keepdims=True)
            return x * jax.lax.rsqrt(var + EPS) * w

        def hsa_forward(hidden_states, w_k, w_v, w_lmk, w_q_retr, w_q, w_o, g_chunk_norm, g_k_norm, g_pre_retr, g_q_retr, g_lmk, g_pre, g_q_norm):
            B, L, _ = hidden_states.shape
            residual = hidden_states
            x = rms(hidden_states, g_pre)
            C = L // S
            xc = rms(x, g_chunk_norm).reshape(B, C, S, D)
            k = (xc @ w_k.T).reshape(B, C, S, HKV, HD)
            v = (xc @ w_v.T).reshape(B, C, S, HKV, HD)
            k = rms(k, g_k_norm)
            landmarks = xc.mean(axis=2) @ w_lmk.T
            xr = rms(x, g_pre_retr)
            qr = rms(xr @ w_q_retr.T, g_q_retr)
            lmk = rms(landmarks, g_lmk)
            scores = jnp.einsum('bld,bcd->blc', qr, lmk) / math.sqrt(RD)
            pos = jnp.arange(L)[None, :, None]
            chunk_ends = (jnp.arange(C) + 1)[None, None, :] * S
            causal = pos >= chunk_ends
            scores = jnp.where(causal, scores, -jnp.inf)
            topk = min(TOPK, C)
            _, idx = jax.lax.top_k(scores, topk)
            idx = jnp.sort(idx, axis=-1)
            sel = jnp.take_along_axis(scores, idx, axis=-1)
            all_inf = jnp.all(sel == -jnp.inf, axis=-1, keepdims=True)
            sel = jnp.where(all_inf, 0.0, sel)
            rw = jax.nn.softmax(sel, axis=-1)
            rw = jnp.where(all_inf, 0.0, rw)
            q = (x @ w_q.T).reshape(B, L, H, HD)
            q = rms(q, g_q_norm)
            tok_idx = (idx[..., None] * S + jnp.arange(S)).reshape(B, L, topk * S)
            tok_idx = jnp.clip(tok_idx, 0, C * S - 1)
            kf = k.reshape(B, C * S, HKV, HD).transpose(0, 2, 1, 3)[:, None]
            vf = v.reshape(B, C * S, HKV, HD).transpose(0, 2, 1, 3)[:, None]
            ii = tok_idx[:, :, None, :, None]
            sel_k = jnp.take_along_axis(kf, ii, axis=3)
            sel_v = jnp.take_along_axis(vf, ii, axis=3)
            G = H // HKV
            qg = q.reshape(B, L, HKV, G, HD)
            att = jnp.einsum('blhgd,blhkd->blhgk', qg, sel_k) / math.sqrt(HD)
            att = att.reshape(B, L, HKV, G, topk, S)
            p = jax.nn.softmax(att, axis=-1)
            p = p * rw[:, :, None, None, :, None]
            sv = sel_v.reshape(B, L, HKV, topk, S, HD)
            out = jnp.einsum('blhgks,blhksd->blhgd', p, sv)
            out = out.reshape(B, L, H * HD) @ w_o.T
            return residual + out
        key = jax.random.key(seed)
        ks = jax.random.split(key, 8)
        std = 0.02
        f = lambda k, shp: jax.random.normal(k, shp, jnp.float32) * std
        return {'hidden_states': jax.random.normal(ks[0], (1, 128, D), jnp.float32), 'w_k': f(ks[1], (HKV * HD, D)), 'w_v': f(ks[2], (HKV * HD, D)), 'w_lmk': f(ks[3], (RD, D)), 'w_q_retr': f(ks[4], (RD, D)), 'w_q': f(ks[5], (H * HD, D)), 'w_o': f(ks[6], (D, H * HD)), 'g_chunk_norm': jnp.ones((D,), jnp.float32), 'g_k_norm': jnp.ones((HD,), jnp.float32), 'g_pre_retr': jnp.ones((D,), jnp.float32), 'g_q_retr': jnp.ones((RD,), jnp.float32), 'g_lmk': jnp.ones((RD,), jnp.float32), 'g_pre': jnp.ones((D,), jnp.float32), 'g_q_norm': jnp.ones((HD,), jnp.float32)}
    _L0_attn_in = _L0_attn_setup()

    def _L0_ffn_setup():
        import jax, jax.numpy as jnp
        import numpy as np
        B, S, D = (2, 256, 256)
        E, H, TOP_K = (8, 176, 2)
        SH = 176
        ROUTED_SCALE = 2.5
        key = jax.random.key(seed)
        ks = jax.random.split(key, 8)
        std = 0.02
        return {'x': jax.random.normal(ks[0], (B, S, D), jnp.float32), 'gate_w': jax.random.normal(ks[1], (E, D), jnp.float32) * std, 'w1': jax.random.normal(ks[2], (E, D, H), jnp.float32) * std, 'w3': jax.random.normal(ks[3], (E, D, H), jnp.float32) * std, 'w2': jax.random.normal(ks[4], (E, H, D), jnp.float32) * std, 'sw1': jax.random.normal(ks[5], (D, SH), jnp.float32) * std, 'sw3': jax.random.normal(ks[6], (D, SH), jnp.float32) * std, 'sw2': jax.random.normal(ks[7], (SH, D), jnp.float32) * std}
    _L0_ffn_in = _L0_ffn_setup()
    _L0_c = _w((lambda *s: np.random.randn(*s).astype(np.float32) * 0.05)(4, 256))
    _L0_wmod = _w((lambda *s: np.random.randn(*s).astype(np.float32) * 0.05)(256, 6 * 256) * 256 ** (-0.5))
    _d = {'L0_attn_hidden_states': _L0_attn_in['hidden_states'], 'L0_attn_w_k': _L0_attn_in['w_k'], 'L0_attn_w_v': _L0_attn_in['w_v'], 'L0_attn_w_lmk': _L0_attn_in['w_lmk'], 'L0_attn_w_q_retr': _L0_attn_in['w_q_retr'], 'L0_attn_w_q': _L0_attn_in['w_q'], 'L0_attn_w_o': _L0_attn_in['w_o'], 'L0_attn_g_chunk_norm': _L0_attn_in['g_chunk_norm'], 'L0_attn_g_k_norm': _L0_attn_in['g_k_norm'], 'L0_attn_g_pre_retr': _L0_attn_in['g_pre_retr'], 'L0_attn_g_q_retr': _L0_attn_in['g_q_retr'], 'L0_attn_g_lmk': _L0_attn_in['g_lmk'], 'L0_attn_g_pre': _L0_attn_in['g_pre'], 'L0_attn_g_q_norm': _L0_attn_in['g_q_norm'], 'L0_ffn_gate_w': _L0_ffn_in['gate_w'], 'L0_ffn_w1': _L0_ffn_in['w1'], 'L0_ffn_w2': _L0_ffn_in['w2'], 'L0_ffn_w3': _L0_ffn_in['w3'], 'L0_ffn_sw1': _L0_ffn_in['sw1'], 'L0_ffn_sw2': _L0_ffn_in['sw2'], 'L0_ffn_sw3': _L0_ffn_in['sw3'], 'L0_c': _L0_c, 'L0_wmod': _L0_wmod}
    _x0 = _d['L0_attn_hidden_states']
    _d['L0_attn_hidden_states'] = jax.random.normal(jax.random.fold_in(jax.random.key(seed), 1), (4, 256, 256), dtype=_x0.dtype)
    del _x0
    return _d

def reference(L0_attn_hidden_states, L0_attn_w_k, L0_attn_w_v, L0_attn_w_lmk, L0_attn_w_q_retr, L0_attn_w_q, L0_attn_w_o, L0_attn_g_chunk_norm, L0_attn_g_k_norm, L0_attn_g_pre_retr, L0_attn_g_q_retr, L0_attn_g_lmk, L0_attn_g_pre, L0_attn_g_q_norm, L0_ffn_gate_w, L0_ffn_w1, L0_ffn_w2, L0_ffn_w3, L0_ffn_sw1, L0_ffn_sw2, L0_ffn_sw3, L0_c, L0_wmod):

    def _L0_attn_ref(hidden_states, w_k, w_v, w_lmk, w_q_retr, w_q, w_o, g_chunk_norm, g_k_norm, g_pre_retr, g_q_retr, g_lmk, g_pre, g_q_norm):
        import jax, jax.numpy as jnp
        import numpy as np
        import math
        D = 256
        H = 16
        HKV = 4
        HD = 128
        S = 32
        TOPK = 8
        RD = 32
        EPS = 1e-05

        def rms(x, w):
            var = jnp.mean(jnp.square(x), axis=-1, keepdims=True)
            return x * jax.lax.rsqrt(var + EPS) * w

        def hsa_forward(hidden_states, w_k, w_v, w_lmk, w_q_retr, w_q, w_o, g_chunk_norm, g_k_norm, g_pre_retr, g_q_retr, g_lmk, g_pre, g_q_norm):
            B, L, _ = hidden_states.shape
            residual = hidden_states
            x = rms(hidden_states, g_pre)
            C = L // S
            xc = rms(x, g_chunk_norm).reshape(B, C, S, D)
            k = (xc @ w_k.T).reshape(B, C, S, HKV, HD)
            v = (xc @ w_v.T).reshape(B, C, S, HKV, HD)
            k = rms(k, g_k_norm)
            landmarks = xc.mean(axis=2) @ w_lmk.T
            xr = rms(x, g_pre_retr)
            qr = rms(xr @ w_q_retr.T, g_q_retr)
            lmk = rms(landmarks, g_lmk)
            scores = jnp.einsum('bld,bcd->blc', qr, lmk) / math.sqrt(RD)
            pos = jnp.arange(L)[None, :, None]
            chunk_ends = (jnp.arange(C) + 1)[None, None, :] * S
            causal = pos >= chunk_ends
            scores = jnp.where(causal, scores, -jnp.inf)
            topk = min(TOPK, C)
            _, idx = jax.lax.top_k(scores, topk)
            idx = jnp.sort(idx, axis=-1)
            sel = jnp.take_along_axis(scores, idx, axis=-1)
            all_inf = jnp.all(sel == -jnp.inf, axis=-1, keepdims=True)
            sel = jnp.where(all_inf, 0.0, sel)
            rw = jax.nn.softmax(sel, axis=-1)
            rw = jnp.where(all_inf, 0.0, rw)
            q = (x @ w_q.T).reshape(B, L, H, HD)
            q = rms(q, g_q_norm)
            tok_idx = (idx[..., None] * S + jnp.arange(S)).reshape(B, L, topk * S)
            tok_idx = jnp.clip(tok_idx, 0, C * S - 1)
            kf = k.reshape(B, C * S, HKV, HD).transpose(0, 2, 1, 3)[:, None]
            vf = v.reshape(B, C * S, HKV, HD).transpose(0, 2, 1, 3)[:, None]
            ii = tok_idx[:, :, None, :, None]
            sel_k = jnp.take_along_axis(kf, ii, axis=3)
            sel_v = jnp.take_along_axis(vf, ii, axis=3)
            G = H // HKV
            qg = q.reshape(B, L, HKV, G, HD)
            att = jnp.einsum('blhgd,blhkd->blhgk', qg, sel_k) / math.sqrt(HD)
            att = att.reshape(B, L, HKV, G, topk, S)
            p = jax.nn.softmax(att, axis=-1)
            p = p * rw[:, :, None, None, :, None]
            sv = sel_v.reshape(B, L, HKV, topk, S, HD)
            out = jnp.einsum('blhgks,blhksd->blhgd', p, sv)
            out = out.reshape(B, L, H * HD) @ w_o.T
            return residual + out
        return hsa_forward(hidden_states, w_k, w_v, w_lmk, w_q_retr, w_q, w_o, g_chunk_norm, g_k_norm, g_pre_retr, g_q_retr, g_lmk, g_pre, g_q_norm)

    def _L0_ffn_ref(x, gate_w, w1, w2, w3, sw1, sw2, sw3):
        import jax, jax.numpy as jnp
        import numpy as np
        B, S, D = (2, 256, 256)
        E, H, TOP_K = (8, 176, 2)
        SH = 176
        ROUTED_SCALE = 2.5
        b, s, d = x.shape
        xt = x.reshape(b * s, d)
        scores = jax.nn.sigmoid(xt @ gate_w.T)
        top_scores, top_idx = jax.lax.top_k(scores, TOP_K)
        top_scores = top_scores / (jnp.sum(top_scores, axis=-1, keepdims=True) + 1e-20)
        top_scores = top_scores * ROUTED_SCALE
        combine = jnp.sum(jax.nn.one_hot(top_idx, E, dtype=xt.dtype) * top_scores[..., None], axis=1)
        h = jnp.einsum('td,edh->eth', xt, w1)
        u = jnp.einsum('td,edh->eth', xt, w3)
        y = jnp.einsum('eth,ehd->etd', jax.nn.silu(h) * u, w2)
        routed = jnp.einsum('etd,te->td', y, combine)
        shared = jax.nn.silu(xt @ sw1) * (xt @ sw3) @ sw2
        return (routed + shared).reshape(b, s, d)
    x = L0_attn_hidden_states
    mod = (_silu(L0_c) @ L0_wmod).reshape(L0_c.shape[0], 6, 1, -1)
    sa, ca, ga, sb, cb, gb = (mod[:, 0], mod[:, 1], mod[:, 2], mod[:, 3], mod[:, 4], mod[:, 5])
    ga = (2 * (ga >= 0) - 1) * jnp.maximum(jnp.abs(ga), 0.25)
    gb = (2 * (gb >= 0) - 1) * jnp.maximum(jnp.abs(gb), 0.25)
    h = _layernorm(x, axis=-1) * (1 + ca) + sa
    x = x + ga * _L0_attn_ref(h, L0_attn_w_k, L0_attn_w_v, L0_attn_w_lmk, L0_attn_w_q_retr, L0_attn_w_q, L0_attn_w_o, L0_attn_g_chunk_norm, L0_attn_g_k_norm, L0_attn_g_pre_retr, L0_attn_g_q_retr, L0_attn_g_lmk, L0_attn_g_pre, L0_attn_g_q_norm)
    h = _layernorm(x, axis=-1) * (1 + cb) + sb
    x = x + gb * _L0_ffn_ref(h, L0_ffn_gate_w, L0_ffn_w1, L0_ffn_w2, L0_ffn_w3, L0_ffn_sw1, L0_ffn_sw2, L0_ffn_sw3)
    return x

_drawn_inputs = setup_inputs


def setup_inputs(seed=0):
    import zlib

    import numpy as np

    out = dict(_drawn_inputs(seed))
    spreads = {'L0_attn_g_chunk_norm': (1.0, 0.6),
     'L0_attn_g_k_norm': (1.0, 0.6),
     'L0_attn_g_pre_retr': (1.0, 0.6),
     'L0_attn_g_q_retr': (1.0, 0.6),
     'L0_attn_g_lmk': (1.0, 0.6),
     'L0_attn_g_pre': (1.0, 0.6),
     'L0_attn_g_q_norm': (1.0, 0.6)}
    factors = {'L0_attn_w_k': 4.928,
     'L0_attn_w_v': 3.981,
     'L0_attn_w_lmk': 8.0,
     'L0_attn_w_q_retr': 8.0,
     'L0_attn_w_q': 4.858,
     'L0_attn_w_o': 3.979,
     'L0_ffn_gate_w': 8.0,
     'L0_ffn_w1': 8.0,
     'L0_ffn_w2': 8.0,
     'L0_ffn_w3': 8.0,
     'L0_ffn_sw1': 8.0,
     'L0_ffn_sw2': 8.0,
     'L0_ffn_sw3': 8.0}
    for name, (base, spread) in spreads.items():
        noise = np.random.default_rng([zlib.crc32(name.encode()), seed]).standard_normal(out[name].shape)
        drawn = base * np.exp(spread * noise) if base else spread * noise
        out[name] = jnp.asarray(drawn.astype(out[name].dtype))
    for name, factor in factors.items():
        out[name] = (out[name] * factor).astype(out[name].dtype)
    return out
```

```python
from contextlib import ExitStack

import concourse.bass as bass
from concourse import mybir

F32 = mybir.dt.float32
F32R = mybir.dt.float32r
I32 = mybir.dt.int32
ALU = mybir.AluOpType
ACT = mybir.ActivationFunctionType
AX = mybir.AxisListType.X

P = 128
B = 4
L = 256
D = 256
KF = D // P
NT = L // P
H = 16
HKV = 4
G = H // HKV
HD = 128
S = 32
C = L // S
RD = 32
NI = C - 1
TQ = NI * S
EPS = 1e-5
E = 8
HE = 176
NHID = (E + 1) * HE
NJ = (NHID + P - 1) // P
NJP = NJ + 1
POOL_CONSTS = 28
GAINS = 7
W_LO = 2 * 3 + 2 + 1
MOD_STEPS = 11
ROUTED = 2.5
KVW = HKV * HD
NKV = 2 * KVW + 2 * RD
HALF = 512
RSQRT_MAGIC = float(0x5F3759DF)

BANK_A = (7, 6, 3)
BANK_B = (5, 4, 2, 1)
PAIR0 = {}
NPAIR = 0
for _i in BANK_A + BANK_B:
    PAIR0[_i] = NPAIR
    NPAIR += _i
PAIRS_A = sum(BANK_A)
COLS = NPAIR * S


class Steps:

    def __init__(self, nc_sem, names):
        self.sem, self.names, self.at_name = nc_sem, names, 0

    def does(self, name):
        assert self.names[self.at_name] == name, (self.names[self.at_name], name)
        self.at_name = (self.at_name + 1) % len(self.names)
        return self.sem, 1

    def at(self, unit, name, off=0):
        return self.sem, unit * len(self.names) + ((off + 1) * len(self.names) + self.names.index(name) + 1)

    def start(self, eng):
        eng.sem_inc(self.sem, len(self.names))


def newton(name):
    return [f"{name}.{n}" for n in range(11)]


def build(nc, x, xT, wq, wk, wv, wr, wl, wo, gains_d, gains_hd, gains_rd, gateT, cT, wmod, wffn, out):
    with ExitStack() as top:
        def sem(name):
            return top.enter_context(nc.semaphore(name))

        def sb(ctx, name, shape, dt=F32):
            return ctx.enter_context(nc.sbuf_tensor(name, shape, dt))

        ps = top.enter_context(nc.psum_tensor("banks", [P, 8, 512], F32))
        RING = (0, 1)
        SA, SB = 2, 3
        R0, R1, R2 = 4, 5, 6
        OB = 7

        ident = sb(top, "ident", [P, P])
        x2T = sb(top, "x2T", [P, KF, B, L])
        h2T = sb(top, "h2T", [P, KF, B, L])
        cw = sb(top, "cw", [64, B, L], F32R)
        modT = sb(top, "modT", [P, B, 12])

        att = ExitStack()

        def at_(name, shape, dt=F32):
            return sb(att, name, shape, dt)

        wq_hi, wq_lo = at_("wq_hi", [P, KF, H * HD], F32R), at_("wq_lo", [P, KF, H * HD], F32R)
        wkv_hi, wkv_lo = at_("wkv_hi", [P, KF, NKV], F32R), at_("wkv_lo", [P, KF, NKV], F32R)
        wo_hi, wo_lo = at_("wo_hi", [P, H, D], F32R), at_("wo_lo", [P, H, D], F32R)
        pick = at_("pick", [P, 4, P])
        chunk_mean = at_("chunk_mean", [P, NT, C])
        rank = at_("rank", [P, NT, E])
        causal = at_("causal", [P, NI, C])
        gd = at_("gd", [P, 3, KF])
        ghd = at_("ghd", [P, 2])
        grd = at_("grd", [RD, 2])
        g_att, g_retr = at_("g_att", [P, KF]), at_("g_retr", [P, KF])
        g_sq = at_("g_sq", [P, KF])
        statv = at_("statv", [P, KF, 2])
        gqk, grl = at_("gqk", [P, 1]), at_("grl", [RD, 1])
        gate_sb = at_("gate_sb", [P, KF, E])
        ones = at_("ones", [P, 1])
        mod_in, mod_out = at_("mod_in", [P, 6]), at_("mod_out", [P, 6])
        xin, xTin, xn = at_("xin", [P, NT, D]), at_("xTin", [P, KF, L]), at_("xn", [P, NT, D])
        hT = at_("hT", [P, KF, L])
        hT_hi, hT_lo = at_("hT_hi", [P, KF, L], F32R), at_("hT_lo", [P, KF, L], F32R)
        squares = at_("squares", [P, KF * L])
        hsq, ksq = squares[:, :].rearrange("p (k l) -> p k l", l=L), squares
        bn6, mv, var, rstd = at_("bn6", [P, NT, 6]), at_("mv", [P, NT, 2]), at_("var", [P, NT]), at_("rstd", [P, NT])
        bn6o, mvo, varo, rstdo = at_("bn6o", [P, NT, 6]), at_("mvo", [P, NT, 2]), at_("varo", [P, NT]), at_("rstdo", [P, NT])
        tok = at_("tok", [P, 2, NT])
        qeps, stok, epsT = at_("qeps", [P, NI]), at_("stok", [P, NT]), at_("epsT", [P, NT])
        kraw = at_("kraw", [P, NT, KVW])
        kss = at_("kss", [P, NT, HKV])
        nv, nr = at_("nv", [P, 10]), at_("nr", [P, 10])
        rraw, rsq, rss = at_("rraw", [P, NT, 2 * RD]), at_("rsq", [P, NT, RD]), at_("rss", [P, NT])
        rqn, lmn = at_("rqn", [P, NT, RD]), at_("lmn", [P, NT, RD])
        lsum, lsq, lnorm = at_("lsum", [C, RD]), at_("lsq", [C, RD]), at_("lnorm", [C, RD])
        lss, lvar, lrs = at_("lss", [C, 1]), at_("lvar", [C, 1]), at_("lrs", [C, 1])
        lmkT, qrT = at_("lmkT", [RD, C]), at_("qrT", [RD, NI, G, S])
        rsc, rex = at_("rsc", [P, NI, C]), at_("rex", [P, NI, C])
        rmx, rsum, rrec = at_("rmx", [P, NI]), at_("rsum", [P, NI]), at_("rrec", [P, NI])
        rw = at_("rw", [P, NPAIR])
        qvar, rnq = at_("qvar", [P, HKV, NI]), at_("rnq", [P, HKV, NI])
        nw1, nw2 = at_("nw1", [P, HKV * NI]), at_("nw2", [P, HKV * NI])
        smax, ssum, srec, wpair = (at_(n, [P, 2, NPAIR]) for n in ("smax", "ssum", "srec", "wpair"))
        gth, gsc, gk1, gk2, gs1, gs2, gsc2 = (at_(n, [P, NT, E]) for n in ("gth", "gsc", "gk1", "gk2", "gs1", "gs2", "gsc2"))
        gm1, gm2, gx1, gx2, gden, grec = (at_(n, [P, NT]) for n in ("gm1", "gm2", "gx1", "gx2", "gden", "grec"))
        cfull, c_hi = at_("cfull", [P, NT, E + 1]), at_("c_hi", [P, NT, E + 1], F32R)
        cpad = at_("cpad", [P, NT, 64])

        stage = ExitStack()
        wmod_sb = sb(stage, "wmod_sb", [P, KF, 6 * D])
        cT_sb, silu_c = sb(stage, "cT_sb", [P, KF, B]), sb(stage, "silu_c", [P, KF, B])
        gsgn, gabs = sb(stage, "gsgn", [P, B, 2]), sb(stage, "gabs", [P, B, 2])
        wkv_raw = sb(stage, "wkv_raw", [P, KF, NKV])
        wq_raw = sb(stage, "wq_raw", [P, KF, H * HD])
        wo_raw = sb(stage, "wo_raw", [P, H, D])
        stage.close()
        qo_hi = at_("qo_hi", [P, HKV, NI, G, S], F32R)
        qo_lo = at_("qo_lo", [P, HKV, NI, G, S], F32R)
        q_sq = at_("q_sq", [P, NI, G, S])
        v_hi, v_lo = at_("v_hi", [P, NT, KVW], F32R), at_("v_lo", [P, NT, KVW], F32R)
        kT_hi, kT_lo = at_("kT_hi", [P, HKV, TQ], F32R), at_("kT_lo", [P, HKV, TQ], F32R)
        x2cur, tail = at_("x2cur", [P, KF, L]), at_("tail", [P, KF * L])
        xn2, h2cur = (tail[:, :].rearrange("p (a b) -> p a b", a=2) for _ in range(2))
        d_sc = at_("d_sc", [P, 2, COLS])
        prob = at_("prob", [P, NI, L])
        pt_hi, pt_lo = at_("pt_hi", [P, 10, P], F32R), at_("pt_lo", [P, 10, P], F32R)
        att.close()

        ffn = ExitStack()

        def ff(name, shape, dt=F32):
            return sb(ffn, name, shape, dt)

        NW = 7
        f_x_hi, f_x_lo = ff("f_x_hi", [P, KF, B * L], F32R), ff("f_x_lo", [P, KF, B * L], F32R)
        w_raw = ff("w_raw", [P, 2, NW, P])
        w_hi, w_lo = ff("w_hi", [P, 2, NW, P], F32R), ff("w_lo", [P, 2, NW - 1, P], F32R)
        f_th, f_a, f_g = (ff(n, [P, 2, HALF]) for n in ("f_th", "f_a", "f_g"))
        f_g_hi, f_g_lo = ff("f_g_hi", [P, 2, HALF], F32R), ff("f_g_lo", [P, 2, HALF], F32R)
        f_out = ff("f_out", [P, KF, B, L])
        ffn.close()

        ld_x, ld_xT, ld_gain, ld_c, ld_mod, ld_kv, ld_q, ld_o, ld_gate = (
            sem(n) for n in ("ld_x", "ld_xT", "ld_gain", "ld_c", "ld_mod", "ld_kv", "ld_q", "ld_o", "ld_gate"))
        ld_w = [sem("ld_w0"), sem("ld_w1")]
        st_out = sem("st_out")
        pool_const, gains_ready, silu_steps, mod_product, mod_steps, w_hi_ready, w_lo_ready = (
            sem(n) for n in ("pool_const", "gains_ready", "silu_steps", "mod_product", "mod_steps", "w_hi_ready", "w_lo_ready"))

        def steps(name, names):
            return Steps(sem(name), names)

        pe_head = steps("pe_head", ["hT", "stat", "rows"])
        pe_kv = steps("pe_kv", ["K0", "V0", "K1", "V1", "R"])
        pe_kT = steps("pe_kT", ["kTa", "kTb"])
        pe_retr = steps("pe_retr", ["lmean", "qrT", "scores"])
        pe_q = steps("pe_q", [f"{n}{u}" for u in range(HKV) for n in ("qa", "qb", "ss")])
        pe_tail = steps("pe_tail", ["x", "h", "gate", "cT"])
        pe_qk = steps("pe_qk", ["A", "B"])
        pe_pt = steps("pe_pt", ["0", "1", "2"])
        pe_pv = steps("pe_pv", ["0", "1"])
        pe_o = steps("pe_o", [f"o{u}" for u in range(HKV)])

        v_ln = steps("v_ln", ["bn0", "bn1", "mod", "ag0", "ag1", "var", *newton("rs"), "xn0", "xn1"])
        v_h = steps("v_h", ["hT0", "hT1", "lo", "base0", "base1"])
        v_stat = steps("v_stat", ["tok", "epsT", "qeps", *newton("s")])
        v_kv = steps("v_kv", ["kss0", "vlo0", "kss1", "vlo1", "rraw", "rsq", "rss", "nvk", "nvr", *newton("nr"), "rqn", "lmn"])
        v_kT = steps("v_kT", ["a", "b"])
        v_retr = steps("v_retr", ["lsum", "lsq", "lss", "lvar", *newton("lrs"), "lnorm", "qrT", "lmkT", "masked", "max",
                                  "sub", "sum", "rec"])
        v_q = steps("v_q", [f"{n}{u}" for u in range(HKV) for n in ("qa", "qb", "ss")] + newton("rnq"))
        v_sc = steps("v_sc", ["maxA", "subA", "maxB", "subB"])
        v_w = steps("v_w", ["sum", "rec", "w"])
        v_pt = steps("v_pt", ["0", "1", "2"])
        v_ot = steps("v_ot", ["0", "1"])
        v_x2 = steps("v_x2", ["mod", "copy", "x0", "x1", "bn0", "bn1", "mod2", "ag0", "ag1", "var", *newton("rs"), "xn0", "xn1", "h0", "h1"])
        v_gate = steps("v_gate", ["sc", "m1", "e1", "k1", "x1", "s1", "sc2", "m2", "e2", "k2", "x2", "s2", "den",
                                  "rec", "sel", "num", "c", "hi", "pad", "lo", "cT"])

        a_head = steps("a_head", ["hi", "sq"])
        a_kv = steps("a_kv", ["kraw0", "ksq0", "vhi0", "kraw1", "ksq1", "vhi1"])
        a_kT = steps("a_kT", ["a", "b"])
        a_retr = steps("a_retr", ["exp"])
        a_q = steps("a_q", [f"{n}{m}{u}" for u in range(HKV) for m in "ab" for n in ("sq", "hi")])
        a_exp = steps("a_exp", [f"e{i}" for i in BANK_A + BANK_B])
        a_pt = steps("a_pt", ["0", "1", "2"])
        a_ot = steps("a_ot", ["0", "1"])
        a_gate = steps("a_gate", ["tanh"])

        g_kn = steps("g_kn", ["0", "1"])
        g_rw = steps("g_rw", [f"r{i}" for i in range(1, C)])
        g_pr = steps("g_pr", [f"p{i}" for i in range(NI, 0, -1)])
        g_keep = steps("g_keep", ["x2", "h2"])

        f_whi, f_wlo = steps("f_whi", ["w"]), steps("f_wlo", ["w"])
        f_pe_h, f_pe_y = steps("f_pe_h", ["h", "u", "c"]), steps("f_pe_y", ["y"])
        f_act = steps("f_act", ["th"])
        f_ghi = steps("f_ghi", ["hi"])
        f_dve = steps("f_dve", ["a", "b", "g"])
        f_glo = steps("f_glo", ["lo"])
        f_xhi, f_xlo, f_fin = sem("f_xhi"), sem("f_xlo"), sem("f_fin")

        ring = [("hT", v_h, "hT1"), ("stat", v_stat, "qeps"),
                ("K0", a_kv, "ksq0"), ("V0", v_kv, "vlo0"), ("K1", a_kv, "ksq1"), ("V1", v_kv, "vlo1"),
                ("R", v_kv, "rraw"), ("qa0", v_q, "qa0"), ("qb0", v_q, "qb0"), ("kTa", v_kT, "a"), ("kTb", v_kT, "b"),
                ("ss0", v_q, "ss0"), ("lmean", v_retr, "lsum"), ("qa1", v_q, "qa1"), ("qb1", v_q, "qb1"), ("qrT", v_retr, "lmkT"),
                ("ss1", v_q, "ss1"),
                ("qa2", v_q, "qa2"), ("qb2", v_q, "qb2"), ("scores", v_retr, "masked"), ("ss2", v_q, "ss2"),
                ("qa3", v_q, "qa3"), ("qb3", v_q, "qb3"), ("ss3", v_q, "ss3")]
        ring_names = [r[0] for r in ring]
        assert len(ring) % 2 == 0

        def bank(name):
            return ps[:, RING[ring_names.index(name) % 2], :]

        def bank_free(b, name):
            n = ring_names.index(name) - 2
            _, stage_, step = ring[n]
            return stage_.at(b, step, 0 if n >= 0 else -1)

        block = top.enter_context(nc.Block())

        @block.sync
        def _(sp):
            sp.dma_start(cT_sb[:, :, :], cT.rearrange("(k p) b -> p k b", p=P)).then_inc(ld_c, 16)
            sp.dma_start(gd[:, :, :], gains_d).then_inc(ld_gain, 16)
            sp.dma_start(ghd[:, :], gains_hd).then_inc(ld_gain, 16)
            sp.dma_start(grd[:, :], gains_rd).then_inc(ld_gain, 16)
            sp.dma_start(wmod_sb[:, :, :], wmod.rearrange("(k p) n -> p k n", p=P)).then_inc(ld_mod, 16)
            for w, n0, n in ((wk, 0, KVW), (wv, KVW, KVW), (wr, 2 * KVW, RD), (wl, 2 * KVW + RD, RD)):
                sp.dma_start(wkv_raw[:, :, n0:n0 + n], w.rearrange("(k p) n -> p k n", p=P)).then_inc(ld_kv, 16)
            sp.dma_start(wq_raw[:, :, :], wq.rearrange("(k p) n -> p k n", p=P)).then_inc(ld_q, 16)
            sp.dma_start(wo_raw[:, :, :], wo.rearrange("(h p) n -> p h n", p=P)).then_inc(ld_o, 16)
            sp.dma_start(gate_sb[:, :, :], gateT.rearrange("(k p) e -> p k e", p=P)).then_inc(ld_gate, 16)
            with sp.Fori(0, B) as b:
                sp.wait_ge(*v_ln.at(b, "xn1", -1))
                sp.dma_start(xin[:, :, :], x[bass.ds(b, 1), :, :].rearrange("o (t p) d -> p (o t) d", p=P)).then_inc(ld_x, 16)
                sp.wait_ge(*v_h.at(b, "base1", -1))
                sp.dma_start(xTin[:, :, :], xT[:, bass.ds(b, 1), :].rearrange("(k p) o l -> p k (o l)", p=P)).then_inc(ld_xT, 16)
            sp.wait_ge(*g_keep.at(B - 1, "h2"))
            sp.wait_ge(*v_gate.at(B - 1, "cT"))
            for j in range(2):
                sp.dma_start(w_raw[:, j, :, :], wffn[j, :, :, :]).then_inc(ld_w[j], 16)
            with sp.Fori(0, (NJP - 2) // 2) as n:
                for j in range(2):
                    sp.wait_ge(*f_whi.at(n * 2 + j, "w"))
                    sp.wait_ge(*f_wlo.at(n * 2 + j, "w"))
                    sp.dma_start(w_raw[:, j, :, :], wffn[bass.ds(n * 2 + 2 + j, 1), :, :, :].rearrange("o p s n -> p (o s) n"))\
                      .then_inc(ld_w[j], 16)
            for n in range(KF * 2):
                k, half = n % 2, n // 2
                sp.wait_ge(f_fin, 2 * (n + 1))
                sp.dma_start(out[k * P:(k + 1) * P, 2 * half:2 * half + 2, :], f_out[:, k, 2 * half:2 * half + 2, :]).then_inc(st_out, 16)
            sp.wait_ge(st_out, 16 * KF * 2)

        @block.gpsimd
        def _(pool):
            for st in (g_kn, g_rw, g_pr, g_keep, f_glo):
                st.start(pool)
            n = 0

            def const(ins):
                nonlocal n
                ins.then_inc(pool_const, 1)
                n += 1
                pool.wait_ge(pool_const, n)

            const(pool.memset(ident[:, :], 0.0))
            const(pool.affine_select(out=ident[:, :], in_=ident[:, :], compare_op=ALU.not_equal, fill=1.0,
                                     base=0, pattern=[[-1, P]], channel_multiplier=1))
            const(pool.memset(ones[:, :], 1.0))
            for m in range(4):
                const(pool.tensor_copy(pick[:, m, :].rearrange("p (r q) -> p r q", q=S),
                                       ident[:, m * S:(m + 1) * S].unsqueeze(1).broadcast_to([P, G, S])))
            const(pool.memset(chunk_mean[:, :, :], 1.0 / S))
            const(pool.affine_select(out=chunk_mean[:, :, :], in_=chunk_mean[:, :, :], compare_op=ALU.is_ge, fill=0.0,
                                     base=0, pattern=[[P, NT], [-S, C]], channel_multiplier=1))
            const(pool.affine_select(out=chunk_mean[:, :, :], in_=chunk_mean[:, :, :], compare_op=ALU.is_ge, fill=0.0,
                                     base=S - 1, pattern=[[-P, NT], [S, C]], channel_multiplier=-1))
            for e in range(E):
                const(pool.memset(rank[:, :, e:e + 1], float(E - e)))
            const(pool.memset(causal[:, :, :], 0.0))
            for i in range(1, C):
                const(pool.memset(causal[:, i - 1, i:C], -1e30))
            const(pool.memset(cpad[:, :, :], 0.0))
            const(pool.memset(cfull[:, :, E:E + 1], 0.5))
            assert n == POOL_CONSTS, n
            pool.wait_ge(w_lo_ready, W_LO)
            const(pool.memset(prob[:, :, :], 0.0))

            def unit(b, u):
                k = b * HKV + u
                pool.wait_ge(*v_w.at(k, "w"))
                pool.wait_ge(*pe_pt.at(k, "2", -1))
                for i in range(NI, 0, -1):
                    dst = prob[:, i - 1, 0:S * i].rearrange("p (c k) -> p c k", k=S)
                    src = d_sc[:, u % 2, S * PAIR0[i]:S * (PAIR0[i] + i)].rearrange("p (c k) -> p c k", k=S)
                    w = wpair[:, u % 2, PAIR0[i]:PAIR0[i] + i].unsqueeze(2).broadcast_to([P, i, S])
                    pool.tensor_tensor(dst, src, w, ALU.mult).then_inc(*g_pr.does(f"p{i}"))

            with pool.Fori(0, B) as b:
                pool.wait_ge(*v_kv.at(b, "nr.10"))
                pool.wait_ge(*a_kv.at(b, "kraw1"))
                for t in range(NT):
                    kk = kraw[:, t, :].rearrange("p (g d) -> p g d", d=HD)
                    r = nr[:, t * HKV:(t + 1) * HKV].unsqueeze(2).broadcast_to([P, HKV, HD])
                    pool.tensor_tensor(kk, kk, r, ALU.mult).then_inc(*g_kn.does(str(t)))
                pool.wait_ge(*v_retr.at(b, "rec"))
                pool.wait_ge(*v_w.at(b * HKV, "w", -1))
                for i in range(1, C):
                    pool.tensor_tensor(rw[:, PAIR0[i]:PAIR0[i] + i], rex[:, i - 1, 0:i], rrec[:, i - 1:i].broadcast_to([P, i]), ALU.mult).then_inc(*g_rw.does(f"r{i}"))
                for u in range(HKV):
                    unit(b, u)
                pool.wait_ge(*v_x2.at(b, "x1"))
                pool.tensor_copy(x2T[:, :, bass.ds(b, 1), :].rearrange("p k o l -> p k (o l)"), x2cur[:, :, :])\
                    .then_inc(*g_keep.does("x2"))
                pool.wait_ge(*v_x2.at(b, "h1"))
                pool.tensor_copy(h2T[:, :, bass.ds(b, 1), :].rearrange("p k o l -> p k (o l)"), h2cur[:, :, :])\
                    .then_inc(*g_keep.does("h2"))

            def g_lo(t, i, first=False):
                pool.wait_ge(*f_ghi.at(t, "hi"))
                if not first:
                    pool.wait_ge(*f_pe_y.at(t, "y", -2))
                pool.tensor_tensor(f_g_lo[:, i, :], f_g[:, i, :], f_g_hi[:, i, :].bitcast(F32), ALU.subtract)\
                    .then_inc(*f_glo.does("lo"))

            for i in range(2):
                g_lo(i, i, True)
            with pool.Fori(1, NJ) as j:
                for i in range(2):
                    g_lo(j * 2 + i, i)

        @block.scalar
        def _(act):
            for st in (a_head, a_kv, a_kT, a_retr, a_q, a_exp, a_pt, a_ot, a_gate, f_whi, f_act, f_ghi):
                st.start(act)
            act.wait_ge(ld_c, 16)
            act.activation(silu_c[:, :, :], cT_sb[:, :, :], ACT.Tanh, scale=0.5).then_inc(silu_steps, 1)
            act.wait_ge(gains_ready, GAINS)
            act.wait_ge(ld_kv, 64)
            for k in range(KF):
                for n0, n1, g in W_PARTS(g_att, g_retr):
                    act.activation(wkv_hi[:, k, n0:n1], wkv_raw[:, k, n0:n1], ACT.Copy, scale=g[:, k:k + 1]).then_inc(w_hi_ready, 1)
            act.wait_ge(ld_q, 16)
            for k in range(KF):
                act.activation(wq_hi[:, k, :], wq_raw[:, k, :], ACT.Copy, scale=gd[:, 0, k:k + 1]).then_inc(w_hi_ready, 1)
            act.wait_ge(ld_o, 16)
            act.activation(wo_hi[:, :, :], wo_raw[:, :, :], ACT.Copy).then_inc(w_hi_ready, 1)

            def exps(b, u):
                k = b * HKV + u
                act.wait_ge(*v_q.at(b, "rnq.10"))
                for i in BANK_A + BANK_B:
                    act.wait_ge(*v_sc.at(k, "subA" if i in BANK_A else "subB"))
                    seg = d_sc[:, u % 2, S * PAIR0[i]:S * (PAIR0[i] + i)]
                    act.activation(seg, seg, ACT.Exp, scale=rnq[:, u, i - 1:i]).then_inc(*a_exp.does(f"e{i}"))

            def pt_high(b, u):
                k = b * HKV + u
                for n, (bk, rows, c0, c1) in enumerate(((R0, P, 3, 7), (R1, P, 0, 3), (R2, TQ - P, 7, 10))):
                    act.wait_ge(*pe_pt.at(k, str(n)))
                    act.wait_ge(*pe_pv.at(k, "1", -1))
                    act.activation(pt_hi[0:rows, c0:c1, :].rearrange("p c r -> p (c r)"), ps[0:rows, bk, 0:(c1 - c0) * P],
                                   ACT.Copy).then_inc(*a_pt.does(str(n)))

            def out_high(b, u):
                k = b * HKV + u
                for n, (bk, i0, i1) in enumerate(((R0, 3, 7), (R1, 0, 3))):
                    act.wait_ge(*pe_pv.at(k, str(n)))
                    act.activation(qo_hi[:, u, i0:i1, :, :].rearrange("p i h q -> p (i h q)"), ps[:, bk, 0:(i1 - i0) * P],
                                   ACT.Copy).then_inc(*a_ot.does(str(n)))

            act.wait_ge(w_lo_ready, W_LO)
            act.wait_ge(mod_steps, MOD_STEPS)
            with act.Fori(0, B) as b:
                act.wait_ge(*v_h.at(b, "hT1"))
                act.wait_ge(*pe_q.at(b, "qb3", -1))
                act.activation(hT_hi[:, :, :], hT[:, :, :], ACT.Copy).then_inc(*a_head.does("hi"))
                act.activation(hsq[:, :, :], hT[:, :, :], ACT.Square).then_inc(*a_head.does("sq"))
                for t in range(NT):
                    act.wait_ge(*pe_kv.at(b, f"K{t}"))
                    act.wait_ge(*pe_kT.at(b, "kTb", -1))
                    act.activation(kraw[:, t, :], bank(f"K{t}"), ACT.Copy).then_inc(*a_kv.does(f"kraw{t}"))
                    if t:
                        act.wait_ge(*v_kv.at(b, "kss0"))
                    act.activation(ksq[:, :], bank(f"K{t}"), ACT.Square).then_inc(*a_kv.does(f"ksq{t}"))
                    act.wait_ge(*pe_kv.at(b, f"V{t}"))
                    act.wait_ge(*v_stat.at(b, "s.10"))
                    act.wait_ge(*pe_pv.at(b * HKV, "1", -1))
                    act.activation(v_hi[:, t, :], bank(f"V{t}"), ACT.Copy, scale=stok[:, t:t + 1]).then_inc(*a_kv.does(f"vhi{t}"))

                def queries(u):
                    for m, name in enumerate("ab"):
                        act.wait_ge(*pe_q.at(b, f"q{name}{u}"))
                        act.wait_ge(*pe_o.at(b, f"o{u}", -1))
                        if m == 0:
                            if u:
                                act.wait_ge(*pe_q.at(b, f"ss{u - 1}"))
                            else:
                                act.wait_ge(*pe_q.at(b, "ss3", -1))
                        src = bank(f"q{name}{u}")[:, 0:2 * TQ].rearrange("p (h i q) -> p i h q", h=2, q=S)
                        act.activation(q_sq[:, :, 2 * m:2 * m + 2, :], src, ACT.Square).then_inc(*a_q.does(f"sq{name}{u}"))
                        act.activation(qo_hi[:, u, :, 2 * m:2 * m + 2, :], src, ACT.Copy).then_inc(*a_q.does(f"hi{name}{u}"))

                queries(0)
                for n, name in enumerate(("a", "b")):
                    act.wait_ge(*pe_kT.at(b, f"kT{name}"))
                    act.wait_ge(*pe_qk.at(b * HKV, "B", -1))
                    act.activation(kT_hi[:, 2 * n:2 * n + 2, :], bank(f"kT{name}").rearrange("p (g l) -> p g l", l=L)[:, :, 0:TQ],
                                   ACT.Copy, scale=gqk[:, 0:1]).then_inc(*a_kT.does(name))
                queries(1)
                queries(2)
                act.wait_ge(*v_retr.at(b, "sub"))
                act.activation(rex[:, :, :], rsc[:, :, :], ACT.Exp).then_inc(*a_retr.does("exp"))
                queries(3)
                exps(b, 0)
                exps(b, 1)
                pt_high(b, 0)
                out_high(b, 0)
                exps(b, 2)
                pt_high(b, 1)
                out_high(b, 1)
                exps(b, 3)
                pt_high(b, 2)
                out_high(b, 2)
                pt_high(b, 3)
                out_high(b, 3)
                act.wait_ge(*pe_tail.at(b, "gate"))
                act.activation(gth[:, :, :], ps[:, OB, 0:NT * E].rearrange("p (t e) -> p t e", e=E), ACT.Tanh, scale=0.5)\
                    .then_inc(*a_gate.does("tanh"))

            act.wait_ge(*g_keep.at(B - 1, "h2"))
            act.wait_ge(*v_gate.at(B - 1, "cT"))
            for k in range(KF):
                act.activation(f_x_hi[:, k, :], h2T[:, k, :, :].rearrange("p b l -> p (b l)"), ACT.Copy).then_inc(f_xhi, 1)

            def w_high(i, count):
                act.wait_ge(ld_w[i], count)
                act.activation(w_hi[:, i, :, :], w_raw[:, i, :, :], ACT.Copy).then_inc(*f_whi.does("w"))

            def gate(t, i, first=False):
                act.wait_ge(*f_pe_h.at(t, "h"))
                if not first:
                    act.wait_ge(*f_dve.at(t, "a", -2))
                act.activation(f_th[:, i, :], ps[:, 0, :], ACT.Tanh, scale=0.5).then_inc(*f_act.does("th"))
                act.wait_ge(*f_dve.at(t, "g"))
                if not first:
                    act.wait_ge(*f_pe_y.at(t, "y", -2))
                    act.wait_ge(*f_glo.at(t, "lo", -2))
                act.activation(f_g_hi[:, i, :], f_g[:, i, :], ACT.Copy).then_inc(*f_ghi.does("hi"))

            w_high(0, 16)
            w_high(1, 16)
            gate(0, 0, True)
            gate(1, 1, True)
            with act.Fori(0, (NJ - 1) // 2) as n:
                gate(n * 4 + 2, 0)
                act.wait_ge(*f_pe_y.at(n * 4, "y", 1))
                w_high(0, n * 16 + 32)
                gate(n * 4 + 3, 1)
                gate(n * 4 + 4, 0)
                act.wait_ge(*f_pe_y.at(n * 4, "y", 3))
                w_high(1, n * 16 + 32)
                gate(n * 4 + 5, 1)

        @block.vector
        def _(dve):
            for st in (v_ln, v_h, v_stat, v_kv, v_kT, v_retr, v_q, v_sc, v_w, v_pt, v_ot, v_x2, v_gate, f_wlo, f_dve):
                st.start(dve)

            def step(st, b, name, ins, wait=True):
                ins.then_inc(*st.does(name))
                if wait:
                    dve.wait_ge(*st.at(b, name))

            def rsqrt(st, b, name, y, v):
                rows, cols = v.shape[0], v.shape[-1]
                t1, t2 = nw1[0:rows, 0:cols], nw2[0:rows, 0:cols]
                step(st, b, f"{name}.0", dve.tensor_scalar(t1.bitcast(I32), v.bitcast(I32), 1, None, ALU.logical_shift_right))
                step(st, b, f"{name}.1", dve.tensor_scalar(y.bitcast(I32), t1.bitcast(I32), -1.0, RSQRT_MAGIC, ALU.mult, ALU.add))
                for n in range(3):
                    step(st, b, f"{name}.{3 * n + 2}", dve.scalar_tensor_tensor(out=t1, in0=y, scalar=-0.5, in1=y, op0=ALU.mult, op1=ALU.mult))
                    step(st, b, f"{name}.{3 * n + 3}", dve.tensor_tensor(t2, t1, v, ALU.mult))
                    step(st, b, f"{name}.{3 * n + 4}", dve.scalar_tensor_tensor(out=y, in0=t2, scalar=1.5, in1=y, op0=ALU.add, op1=ALU.mult))

            dve.wait_ge(ld_gain, 48)
            dve.tensor_tensor(g_att[:, :], gd[:, 0, :], gd[:, 1, :], ALU.mult).then_inc(gains_ready, 1)
            dve.tensor_tensor(g_retr[:, :], gd[:, 0, :], gd[:, 2, :], ALU.mult).then_inc(gains_ready, 1)
            dve.tensor_tensor(g_sq[:, :], gd[:, 0, :], gd[:, 0, :], ALU.mult).then_inc(gains_ready, 1)
            dve.scalar_tensor_tensor(out=gqk[:, :], in0=ghd[:, 0:1], scalar=float(HD) ** -0.5, in1=ghd[:, 1:2],
                                     op0=ALU.mult, op1=ALU.mult).then_inc(gains_ready, 1)
            dve.scalar_tensor_tensor(out=grl[:, :], in0=grd[:, 0:1], scalar=float(RD) ** -0.5, in1=grd[:, 1:2],
                                     op0=ALU.mult, op1=ALU.mult).then_inc(gains_ready, 1)
            dve.memset(statv[:, :, 0:1], EPS / D).then_inc(gains_ready, 1)
            dve.wait_ge(gains_ready, 6)
            dve.tensor_scalar(statv[:, :, 1], g_sq[:, :], 1.0 / D, EPS / D, ALU.mult, ALU.add).then_inc(gains_ready, 1)

            dve.wait_ge(silu_steps, 1)
            dve.scalar_tensor_tensor(out=silu_c[:, :, :], in0=silu_c[:, :, :], scalar=1.0, in1=cT_sb[:, :, :],
                                     op0=ALU.add, op1=ALU.mult).then_inc(silu_steps, 1)
            dve.wait_ge(mod_product, 1)
            n = 0

            def mod(ins):
                nonlocal n
                ins.then_inc(mod_steps, 1)
                n += 1
                dve.wait_ge(mod_steps, n)

            mod(dve.tensor_scalar(modT[:, :, :].rearrange("p b n -> p n b"),
                                  ps[:, OB, 0:12 * B].rearrange("p (n b) -> p n b", b=B), 0.5, None, ALU.mult))
            for n0 in (2, 8):
                mod(dve.tensor_scalar(modT[:, :, n0:n0 + 2], modT[:, :, n0:n0 + 2], 1.0, None, ALU.add))
            for n0 in (4, 10):
                seg = modT[:, :, n0:n0 + 2]
                mod(dve.tensor_scalar(gsgn[:, :, :], seg, 0.0, 2.0, ALU.is_ge, ALU.mult))
                mod(dve.scalar_tensor_tensor(out=gabs[:, :, :], in0=gsgn[:, :, :], scalar=-1.0, in1=seg, op0=ALU.add, op1=ALU.mult))
                mod(dve.tensor_scalar(gabs[:, :, :], gabs[:, :, :], 0.25, None, ALU.max))
                mod(dve.scalar_tensor_tensor(out=seg, in0=gsgn[:, :, :], scalar=-1.0, in1=gabs[:, :, :], op0=ALU.add, op1=ALU.mult))
            assert n == MOD_STEPS, n

            n = 0
            for k in range(KF):
                for n0, n1, g in W_PARTS(g_att, g_retr):
                    n += 1
                    dve.wait_ge(w_hi_ready, n)
                    dve.scalar_tensor_tensor(out=wkv_lo[:, k, n0:n1], in0=wkv_raw[:, k, n0:n1], scalar=g[:, k:k + 1],
                                             in1=wkv_hi[:, k, n0:n1].bitcast(F32), op0=ALU.mult, op1=ALU.subtract).then_inc(w_lo_ready, 1)
            for k in range(KF):
                n += 1
                dve.wait_ge(w_hi_ready, n)
                dve.scalar_tensor_tensor(out=wq_lo[:, k, :], in0=wq_raw[:, k, :], scalar=gd[:, 0, k:k + 1],
                                         in1=wq_hi[:, k, :].bitcast(F32), op0=ALU.mult, op1=ALU.subtract).then_inc(w_lo_ready, 1)
            n += 1
            dve.wait_ge(w_hi_ready, n)
            dve.tensor_tensor(wo_lo[:, :, :], wo_raw[:, :, :], wo_hi[:, :, :].bitcast(F32), ALU.subtract).then_inc(w_lo_ready, 1)
            assert n == W_LO

            dve.wait_ge(pool_const, POOL_CONSTS + 1)
            with dve.Fori(0, B) as b:
                dve.wait_ge(ld_x, b * 16 + 16)
                for t in range(NT):
                    step(v_ln, b, f"bn{t}", dve.bn_stats(bn6[:, t, :], xin[:, t, :]), wait=False)
                dve.wait_ge(*v_ln.at(b, "bn1"))
                step(v_ln, b, "mod", dve.tensor_scalar(mod_in[:, :], modT[:, bass.ds(b, 1), 0:6].rearrange("p o n -> p (o n)"), 1.0, None, ALU.mult), wait=False)
                for t in range(NT):
                    step(v_ln, b, f"ag{t}", dve.bn_aggr(mv[:, t, :], bn6[:, t, :]), wait=t == NT - 1)
                step(v_ln, b, "var", dve.tensor_scalar(var[:, :], mv[:, :, 1], EPS, None, ALU.add))
                rsqrt(v_ln, b, "rs", rstd[:, :], var[:, :])
                for t in range(NT):
                    step(v_ln, b, f"xn{t}", dve.tensor_scalar(xn[:, t, :], xin[:, t, :], mv[:, t, 0:1], rstd[:, t:t + 1],
                                                              ALU.subtract, ALU.mult), wait=False)
                dve.wait_ge(*pe_head.at(b, "hT"))
                dve.wait_ge(*a_head.at(b, "sq", -1))
                hp = bank("hT").rearrange("p (k l) -> p k l", l=L)
                for k in range(KF):
                    step(v_h, b, f"hT{k}", dve.tensor_scalar(hT[:, k, :], hp[:, k, :], mod_in[:, 2 + k:3 + k], mod_in[:, k:k + 1],
                                                             ALU.mult, ALU.add), wait=k == KF - 1)
                dve.wait_ge(*a_head.at(b, "hi"))
                dve.wait_ge(*pe_q.at(b, "qb3", -1))
                dve.tensor_tensor(hT_lo[:, :, :], hT[:, :, :], hT_hi[:, :, :].bitcast(F32), ALU.subtract).then_inc(*v_h.does("lo"))
                dve.wait_ge(ld_xT, b * 16 + 16)
                for k in range(KF):
                    step(v_h, b, f"base{k}", dve.scalar_tensor_tensor(out=x2T[:, k, bass.ds(b, 1), :].rearrange("p o l -> p (o l)"), in0=hT[:, k, :], scalar=mod_in[:, 4 + k:5 + k],
                                                                      in1=xTin[:, k, :], op0=ALU.mult, op1=ALU.add), wait=k == KF - 1)
                dve.wait_ge(*pe_head.at(b, "stat"))
                step(v_stat, b, "tok", dve.tensor_scalar(tok[:, :, :], bank("stat")[:, 0:2 * NT].rearrange("p (t s) -> p s t", s=2),
                                                         EPS * EPS, None, ALU.add))
                step(v_stat, b, "epsT", dve.tensor_scalar(epsT[:, :], tok[:, 1, :], EPS, None, ALU.mult))
                dve.wait_ge(*pe_head.at(b, "rows"))
                step(v_stat, b, "qeps", dve.tensor_copy(qeps[:, :], bank("stat")[:, 2 * NT:2 * NT + NI]))
                rsqrt(v_stat, b, "s", stok[:, :], tok[:, 1, :])
                for t in range(NT):
                    dve.wait_ge(*a_kv.at(b, f"ksq{t}"))
                    step(v_kv, b, f"kss{t}", dve.tensor_reduce(kss[:, t, :], ksq[:, :].rearrange("p (g d) -> p g d", d=HD), AX, ALU.add))
                    dve.wait_ge(*a_kv.at(b, f"vhi{t}"))
                    step(v_kv, b, f"vlo{t}", dve.scalar_tensor_tensor(out=v_lo[:, t, :], in0=bank(f"V{t}"), scalar=stok[:, t:t + 1],
                                                                      in1=v_hi[:, t, :].bitcast(F32), op0=ALU.mult, op1=ALU.subtract))
                dve.wait_ge(*pe_kv.at(b, "R"))
                step(v_kv, b, "rraw", dve.tensor_copy(rraw[:, :, :], bank("R")[:, 0:NT * 2 * RD].rearrange("p (t r) -> p t r", t=NT)))
                step(v_kv, b, "rsq", dve.tensor_tensor(rsq[:, :, :], rraw[:, :, 0:RD], rraw[:, :, 0:RD], ALU.mult))
                step(v_kv, b, "rss", dve.tensor_reduce(rss[:, :], rsq[:, :, :], AX, ALU.add))
                nvk = nv[:, 0:NT * HKV].rearrange("p (t g) -> p t g", t=NT)
                step(v_kv, b, "nvk", dve.scalar_tensor_tensor(out=nvk, in0=kss[:, :, :], scalar=1.0 / HD,
                                                              in1=epsT[:, :].unsqueeze(2).broadcast_to([P, NT, HKV]), op0=ALU.mult, op1=ALU.add))
                step(v_kv, b, "nvr", dve.scalar_tensor_tensor(out=nv[:, 8:10], in0=rss[:, :], scalar=1.0 / RD, in1=epsT[:, :],
                                                              op0=ALU.mult, op1=ALU.add))
                rsqrt(v_kv, b, "nr", nr[:, :], nv[:, :])
                step(v_kv, b, "rqn", dve.tensor_tensor(rqn[:, :, :], rraw[:, :, 0:RD], nr[:, 8:10].unsqueeze(2).broadcast_to([P, NT, RD]), ALU.mult))
                step(v_kv, b, "lmn", dve.tensor_tensor(lmn[:, :, :], rraw[:, :, RD:2 * RD], stok[:, :].unsqueeze(2).broadcast_to([P, NT, RD]), ALU.mult))

                def queries(u):
                    for m, name in enumerate("ab"):
                        dve.wait_ge(*a_q.at(b, f"hi{name}{u}"))
                        dve.wait_ge(*pe_o.at(b, f"o{u}", -1))
                        src = bank(f"q{name}{u}")[:, 0:2 * TQ].rearrange("p (h i q) -> p i h q", h=2, q=S)
                        step(v_q, b, f"q{name}{u}", dve.tensor_tensor(qo_lo[:, u, :, 2 * m:2 * m + 2, :], src,
                                                                      qo_hi[:, u, :, 2 * m:2 * m + 2, :].bitcast(F32), ALU.subtract))

                def query_norm(u):
                    dve.wait_ge(*pe_q.at(b, f"ss{u}"))
                    dve.wait_ge(*a_exp.at(b * HKV, "e1", -1))
                    step(v_q, b, f"ss{u}", dve.scalar_tensor_tensor(out=qvar[:, u, :], in0=bank(f"ss{u}")[:, 0:NI], scalar=1.0 / HD,
                                                                    in1=qeps[:, :], op0=ALU.mult, op1=ALU.add))

                queries(0)
                for n, name in enumerate("ab"):
                    dve.wait_ge(*a_kT.at(b, name))
                    src = bank(f"kT{name}").rearrange("p (g l) -> p g l", l=L)[:, :, 0:TQ]
                    step(v_kT, b, name, dve.scalar_tensor_tensor(out=kT_lo[:, 2 * n:2 * n + 2, :], in0=src, scalar=gqk[:, 0:1],
                                                                 in1=kT_hi[:, 2 * n:2 * n + 2, :].bitcast(F32), op0=ALU.mult, op1=ALU.subtract))
                query_norm(0)
                dve.wait_ge(*pe_retr.at(b, "lmean"))
                step(v_retr, b, "lsum", dve.tensor_copy(lsum[:, :], bank("lmean")[0:C, 0:RD]))
                step(v_retr, b, "lsq", dve.tensor_tensor(lsq[:, :], lsum[:, :], lsum[:, :], ALU.mult))
                step(v_retr, b, "lss", dve.tensor_reduce(lss[:, :], lsq[:, :], AX, ALU.add))
                step(v_retr, b, "lvar", dve.tensor_scalar(lvar[:, :], lss[:, :], 1.0 / RD, EPS, ALU.mult, ALU.add))
                rsqrt(v_retr, b, "lrs", lrs[:, :], lvar[:, :])
                step(v_retr, b, "lnorm", dve.tensor_scalar(lnorm[:, :], lsum[:, :], lrs[:, 0:1], None, ALU.mult))
                queries(1)
                dve.wait_ge(*pe_retr.at(b, "qrT"))
                step(v_retr, b, "qrT", dve.tensor_copy(
                    qrT[:, :, :, :], bank("qrT")[0:RD, S:L].rearrange("p (i q) -> p i q", q=S).unsqueeze(2).broadcast_to([RD, NI, G, S])), wait=False)
                step(v_retr, b, "lmkT", dve.tensor_scalar(lmkT[:, :], bank("qrT")[0:RD, L:L + C], grl[:, 0:1], None, ALU.mult))
                query_norm(1)
                queries(2)
                dve.wait_ge(*pe_retr.at(b, "scores"))
                dve.wait_ge(*g_rw.at(b, f"r{NI}", -1))
                step(v_retr, b, "masked", dve.tensor_tensor(rsc[:, :, :], bank("scores")[:, 0:NI * C].rearrange("p (i c) -> p i c", c=C),
                                                            causal[:, :, :], ALU.add))
                step(v_retr, b, "max", dve.tensor_reduce(rmx[:, :], rsc[:, :, :], AX, ALU.max))
                step(v_retr, b, "sub", dve.tensor_tensor(rsc[:, :, :], rsc[:, :, :], rmx[:, :].unsqueeze(2).broadcast_to([P, NI, C]), ALU.subtract))
                query_norm(2)
                dve.wait_ge(*a_retr.at(b, "exp"))
                step(v_retr, b, "sum", dve.tensor_reduce(rsum[:, :], rex[:, :, :], AX, ALU.add))
                step(v_retr, b, "rec", dve.reciprocal(rrec[:, :], rsum[:, :]))
                queries(3)
                query_norm(3)
                rsqrt(v_q, b, "rnq", rnq[:, :, :].rearrange("p u i -> p (u i)"), qvar[:, :, :].rearrange("p u i -> p (u i)"))

                def scores(u):
                    k = b * HKV + u
                    for name, bk, p0, p1 in (("A", SA, 0, PAIRS_A), ("B", SB, PAIRS_A, NPAIR)):
                        dve.wait_ge(*pe_qk.at(k, name))
                        src = ps[:, bk, 0:(p1 - p0) * S].rearrange("p (n k) -> p n k", k=S)
                        step(v_sc, k, f"max{name}", dve.tensor_reduce(smax[:, u % 2, p0:p1], src, AX, ALU.max))
                        dve.wait_ge(*g_pr.at(k, "p1", -2))
                        step(v_sc, k, f"sub{name}", dve.tensor_tensor(
                            d_sc[:, u % 2, p0 * S:p1 * S].rearrange("p (n k) -> p n k", k=S), src,
                            smax[:, u % 2, p0:p1].unsqueeze(2).broadcast_to([P, p1 - p0, S]), ALU.subtract))

                def weights(u):
                    k = b * HKV + u
                    dve.wait_ge(*a_exp.at(k, "e1"))
                    step(v_w, k, "sum", dve.tensor_reduce(ssum[:, u % 2, :], d_sc[:, u % 2, :].rearrange("p (n k) -> p n k", k=S), AX, ALU.add))
                    step(v_w, k, "rec", dve.reciprocal(srec[:, u % 2, :], ssum[:, u % 2, :]))
                    dve.wait_ge(*g_rw.at(b, f"r{NI}"))
                    dve.wait_ge(*g_pr.at(k, "p1", -2))
                    step(v_w, k, "w", dve.tensor_tensor(wpair[:, u % 2, :], srec[:, u % 2, :], rw[:, :], ALU.mult))

                def pt_low(u):
                    k = b * HKV + u
                    for n, (bk, rows, c0, c1) in enumerate(((R0, P, 3, 7), (R1, P, 0, 3), (R2, TQ - P, 7, 10))):
                        dve.wait_ge(*a_pt.at(k, str(n)))
                        dve.wait_ge(*pe_pv.at(k, "1", -1))
                        dve.tensor_tensor(pt_lo[0:rows, c0:c1, :].rearrange("p c r -> p (c r)"), ps[0:rows, bk, 0:(c1 - c0) * P],
                                          pt_hi[0:rows, c0:c1, :].rearrange("p c r -> p (c r)").bitcast(F32), ALU.subtract)\
                           .then_inc(*v_pt.does(str(n)))

                def out_low(u):
                    k = b * HKV + u
                    for n, (bk, i0, i1) in enumerate(((R0, 3, 7), (R1, 0, 3))):
                        dve.wait_ge(*a_ot.at(k, str(n)))
                        dve.tensor_tensor(qo_lo[:, u, i0:i1, :, :].rearrange("p i h q -> p (i h q)"), ps[:, bk, 0:(i1 - i0) * P],
                                          qo_hi[:, u, i0:i1, :, :].rearrange("p i h q -> p (i h q)").bitcast(F32), ALU.subtract)\
                           .then_inc(*v_ot.does(str(n)))

                scores(0)
                weights(0)
                scores(1)
                pt_low(0)
                weights(1)
                out_low(0)
                scores(2)
                pt_low(1)
                weights(2)
                out_low(1)
                scores(3)
                pt_low(2)
                weights(3)
                out_low(2)
                pt_low(3)
                out_low(3)

                step(v_x2, b, "mod", dve.tensor_scalar(mod_out[:, 0:2], modT[:, bass.ds(b, 1), 4:6].rearrange("p o n -> p (o n)"), 1.0, None, ALU.mult))
                dve.wait_ge(*g_keep.at(b, "h2", -1))
                step(v_x2, b, "copy", dve.tensor_scalar(x2cur[:, :, 0:S], x2T[:, :, bass.ds(b, 1), 0:S].rearrange("p k o l -> p k (o l)"), 1.0, None, ALU.mult))
                dve.wait_ge(*pe_o.at(b, f"o{HKV - 1}"))
                for k in range(KF):
                    step(v_x2, b, f"x{k}", dve.scalar_tensor_tensor(out=x2cur[:, k, S:L], in0=ps[:, OB, k * TQ:(k + 1) * TQ],
                                                                    scalar=mod_out[:, k:k + 1], in1=x2T[:, k, bass.ds(b, 1), S:L].rearrange("p o l -> p (o l)"), op0=ALU.mult, op1=ALU.add))
                dve.wait_ge(*pe_tail.at(b, "x"))
                xp = ps[:, OB, :].rearrange("p (t d) -> p t d", d=D)
                for t in range(NT):
                    step(v_x2, b, f"bn{t}", dve.bn_stats(bn6o[:, t, :], xp[:, t, :]), wait=False)
                dve.wait_ge(*v_x2.at(b, "bn1"))
                step(v_x2, b, "mod2", dve.tensor_scalar(mod_out[:, 2:6], modT[:, bass.ds(b, 1), 6:10].rearrange("p o n -> p (o n)"), 1.0, None, ALU.mult), wait=False)
                for t in range(NT):
                    step(v_x2, b, f"ag{t}", dve.bn_aggr(mvo[:, t, :], bn6o[:, t, :]), wait=t == NT - 1)
                step(v_x2, b, "var", dve.tensor_scalar(varo[:, :], mvo[:, :, 1], EPS, None, ALU.add))
                rsqrt(v_x2, b, "rs", rstdo[:, :], varo[:, :])
                for t in range(NT):
                    step(v_x2, b, f"xn{t}", dve.tensor_scalar(xn2[:, t, :], xp[:, t, :], mvo[:, t, 0:1], rstdo[:, t:t + 1],
                                                              ALU.subtract, ALU.mult))
                dve.wait_ge(*pe_tail.at(b, "h"))
                hp2 = ps[:, OB, :].rearrange("p (k l) -> p k l", l=L)
                for k in range(KF):
                    step(v_x2, b, f"h{k}", dve.tensor_scalar(h2cur[:, k, :], hp2[:, k, :], mod_out[:, 4 + k:5 + k], mod_out[:, 2 + k:3 + k],
                                                             ALU.mult, ALU.add))

                def bc(a):
                    return a[:, :].unsqueeze(2).broadcast_to([P, NT, E])

                def g(name, ins):
                    step(v_gate, b, name, ins)

                dve.wait_ge(*a_gate.at(b, "tanh"))
                g("sc", dve.tensor_scalar(gsc[:, :, :], gth[:, :, :], 0.5, 0.5, ALU.mult, ALU.add))
                for n, (score, gm, gx, gs) in enumerate(((gsc, gm1, gx1, gs1), (gsc2, gm2, gx2, gs2)), 1):
                    if n == 2:
                        g("sc2", dve.scalar_tensor_tensor(out=gsc2[:, :, :], in0=gs1[:, :, :], scalar=-4.0, in1=gsc[:, :, :],
                                                          op0=ALU.mult, op1=ALU.add))
                    g(f"m{n}", dve.tensor_reduce(gm[:, :], score[:, :, :], AX, ALU.max))
                    g(f"e{n}", dve.tensor_tensor(gk1[:, :, :], score[:, :, :], bc(gm), ALU.is_equal))
                    g(f"k{n}", dve.tensor_tensor(gk2[:, :, :], gk1[:, :, :], rank[:, :, :], ALU.mult))
                    g(f"x{n}", dve.tensor_reduce(gx[:, :], gk2[:, :, :], AX, ALU.max))
                    g(f"s{n}", dve.tensor_tensor(gs[:, :, :], gk2[:, :, :], bc(gx), ALU.is_equal))
                g("den", dve.scalar_tensor_tensor(out=gden[:, :], in0=gm1[:, :], scalar=1e-20, in1=gm2[:, :], op0=ALU.add, op1=ALU.add))
                g("rec", dve.reciprocal(grec[:, :], gden[:, :]))
                g("sel", dve.tensor_tensor(gs1[:, :, :], gs1[:, :, :], gs2[:, :, :], ALU.add))
                g("num", dve.tensor_tensor(gsc2[:, :, :], gsc[:, :, :], gs1[:, :, :], ALU.mult))
                g("c", dve.scalar_tensor_tensor(out=cfull[:, :, 0:E], in0=gsc2[:, :, :], scalar=0.5 * ROUTED, in1=bc(grec), op0=ALU.mult, op1=ALU.mult))
                g("hi", dve.tensor_copy(c_hi[:, :, :], cfull[:, :, :]))
                g("pad", dve.tensor_copy(cpad[:, :, 0:E + 1], c_hi[:, :, :].bitcast(F32)))
                g("lo", dve.tensor_tensor(cpad[:, :, 32:32 + E + 1], cfull[:, :, :], c_hi[:, :, :].bitcast(F32), ALU.subtract))
                dve.wait_ge(*pe_tail.at(b, "cT"))
                g("cT", dve.tensor_scalar(cw[:, bass.ds(b, 1), :].rearrange("p o l -> p (o l)"), ps[0:64, OB, 0:L], 1.0, None, ALU.mult))

            for k in range(KF):
                dve.wait_ge(f_xhi, k + 1)
                dve.tensor_tensor(f_x_lo[:, k, :], h2T[:, k, :, :].rearrange("p b l -> p (b l)"), f_x_hi[:, k, :].bitcast(F32),
                                  ALU.subtract).then_inc(f_xlo, 1)

            def w_low(j, i):
                dve.wait_ge(*f_whi.at(j, "w"))
                dve.tensor_tensor(w_lo[:, i, :, :], w_raw[:, i, 0:NW - 1, :], w_hi[:, i, 0:NW - 1, :].bitcast(F32), ALU.subtract)\
                   .then_inc(*f_wlo.does("w"))

            def gated(t, i, first=False):
                dve.wait_ge(*f_act.at(t, "th"))
                step(f_dve, t, "a", dve.scalar_tensor_tensor(out=f_a[:, i, :], in0=f_th[:, i, :], scalar=1.0, in1=ps[:, 0, :],
                                                             op0=ALU.add, op1=ALU.mult))
                dve.wait_ge(*f_pe_h.at(t, "u"))
                step(f_dve, t, "b", dve.tensor_tensor(f_a[:, i, :], f_a[:, i, :], ps[:, 1, :], ALU.mult))
                dve.wait_ge(*f_pe_h.at(t, "c"))
                if not first:
                    dve.wait_ge(*f_glo.at(t, "lo", -2))
                    dve.wait_ge(*f_ghi.at(t, "hi", -2))
                step(f_dve, t, "g", dve.tensor_tensor(f_g[:, i, :], f_a[:, i, :], ps[:, R2, :], ALU.mult))

            w_low(0, 0)
            w_low(1, 1)
            gated(0, 0, True)
            gated(1, 1, True)
            with dve.Fori(0, (NJ - 1) // 2) as n:
                gated(n * 4 + 2, 0)
                w_low(n * 2 + 2, 0)
                gated(n * 4 + 3, 1)
                gated(n * 4 + 4, 0)
                w_low(n * 2 + 3, 1)
                gated(n * 4 + 5, 1)
            for n in range(KF * 2):
                k, half = n % 2, n // 2
                dve.wait_ge(*f_pe_y.at(2 * NJ - 2 + half, "y"))
                for b in (2 * half, 2 * half + 1):
                    dve.scalar_tensor_tensor(out=f_out[:, k, b, :], in0=ps[:, 2 + n, (b % 2) * L:(b % 2 + 1) * L],
                                             scalar=modT[:, b, 10 + k:11 + k], in1=x2T[:, k, b, :], op0=ALU.mult, op1=ALU.add)\
                       .then_inc(f_fin, 1)

        @block.tensor
        def _(pe):
            for st in (pe_head, pe_kv, pe_kT, pe_retr, pe_q, pe_tail, pe_qk, pe_pt, pe_pv, pe_o, f_pe_h, f_pe_y):
                st.start(pe)

            def product(out_, pairs, start=True, stop=True):
                for n, (w, m) in enumerate(pairs):
                    ins = pe.matmul(out_, w, m, start=start and n == 0, stop=stop and n == len(pairs) - 1,
                                    skip_group_check=True)
                return ins

            def split(w_hi_, w_lo_, m_hi, m_lo):
                return [(w_hi_, m_hi), (w_hi_, m_lo), (w_lo_, m_hi)]

            pe.wait_ge(ld_mod, 16)
            pe.wait_ge(silu_steps, 2)
            for n in range(12):
                ins = product(ps[:, OB, n * B:(n + 1) * B], [(wmod_sb[:, k, n * P:(n + 1) * P], silu_c[:, k, :]) for k in range(KF)])
            ins.then_inc(mod_product, 1)
            pe.wait_ge(pool_const, POOL_CONSTS)
            pe.wait_ge(w_lo_ready, W_LO)
            pe.wait_ge(ld_gate, 16)
            with pe.Fori(0, B) as b:
                pe.wait_ge(*bank_free(b, "hT"))
                pe.wait_ge(*v_ln.at(b, "xn1"))
                for k in range(KF):
                    for t in range(NT):
                        ins = pe.transpose(bank("hT")[:, k * L + t * P:k * L + (t + 1) * P], xn[:, t, k * P:(k + 1) * P], ident[:, :])
                ins.then_inc(*pe_head.does("hT"))
                pe.wait_ge(*bank_free(b, "stat"))
                pe.wait_ge(*a_head.at(b, "sq"))
                for t in range(NT):
                    ins = product(bank("stat")[:, 2 * t:2 * t + 2], [(hsq[:, k, t * P:(t + 1) * P], statv[:, k, :]) for k in range(KF)])
                ins.then_inc(*pe_head.does("stat"))
                pe.wait_ge(*v_stat.at(b, "tok"))
                for i in range(1, C):
                    ins = product(bank("stat")[:, 2 * NT + i - 1:2 * NT + i], [(pick[:, i % 4, :], tok[:, 0, i // 4:i // 4 + 1])])
                ins.then_inc(*pe_head.does("rows"))
                pe.wait_ge(*v_h.at(b, "lo"))
                for t in range(NT):
                    for name, n0 in (("K", 0), ("V", KVW)):
                        pe.wait_ge(*bank_free(b, f"{name}{t}"))
                        tt = slice(t * P, (t + 1) * P)
                        product(bank(f"{name}{t}"), [x_ for k in range(KF) for x_ in split(
                            hT_hi[:, k, tt], hT_lo[:, k, tt], wkv_hi[:, k, n0:n0 + KVW], wkv_lo[:, k, n0:n0 + KVW])])\
                            .then_inc(*pe_kv.does(f"{name}{t}"))
                pe.wait_ge(*bank_free(b, "R"))
                for t in range(NT):
                    tt = slice(t * P, (t + 1) * P)
                    ins = product(bank("R")[:, t * 2 * RD:(t + 1) * 2 * RD], [x_ for k in range(KF) for x_ in split(
                        hT_hi[:, k, tt], hT_lo[:, k, tt], wkv_hi[:, k, 2 * KVW:], wkv_lo[:, k, 2 * KVW:])])
                ins.then_inc(*pe_kv.does("R"))

                def queries(u):
                    for m, name in enumerate("ab"):
                        pe.wait_ge(*bank_free(b, f"q{name}{u}"))
                        for hh in range(2):
                            h = u * G + 2 * m + hh
                            ins = product(bank(f"q{name}{u}")[:, hh * TQ:(hh + 1) * TQ], [x_ for k in range(KF) for x_ in split(
                                wq_hi[:, k, h * HD:(h + 1) * HD], wq_lo[:, k, h * HD:(h + 1) * HD], hT_hi[:, k, S:L], hT_lo[:, k, S:L])])
                        ins.then_inc(*pe_q.does(f"q{name}{u}"))

                def query_sums(u):
                    pe.wait_ge(*bank_free(b, f"ss{u}"))
                    pe.wait_ge(*a_q.at(b, f"sqb{u}"))
                    for i in range(NI):
                        ins = product(bank(f"ss{u}")[:, i:i + 1], [(q_sq[:, i, :, :].rearrange("p h q -> p (h q)"), ones[:, :])])
                    ins.then_inc(*pe_q.does(f"ss{u}"))

                queries(0)
                for n, name in enumerate("ab"):
                    pe.wait_ge(*bank_free(b, f"kT{name}"))
                    pe.wait_ge(*g_kn.at(b, "1"))
                    for g in range(2):
                        for t, rows in ((0, P), (1, TQ - P)):
                            ins = pe.transpose(bank(f"kT{name}")[:, g * L + t * P:g * L + t * P + rows],
                                               kraw[0:rows, t, (2 * n + g) * HD:(2 * n + g + 1) * HD], ident[0:rows, 0:rows])
                    ins.then_inc(*pe_kT.does(f"kT{name}"))
                query_sums(0)
                pe.wait_ge(*bank_free(b, "lmean"))
                pe.wait_ge(*v_kv.at(b, "lmn"))
                product(bank("lmean")[0:C, 0:RD], [(chunk_mean[:, t, :], lmn[:, t, :]) for t in range(NT)])\
                    .then_inc(*pe_retr.does("lmean"))
                queries(1)
                pe.wait_ge(*bank_free(b, "qrT"))
                pe.wait_ge(*v_retr.at(b, "lnorm"))
                for t in range(NT):
                    product(bank("qrT")[0:RD, t * P:(t + 1) * P], [(rqn[:, t, :], ident[:, :])])
                product(bank("qrT")[0:RD, L:L + C], [(lnorm[:, :], ident[0:C, 0:C])]).then_inc(*pe_retr.does("qrT"))
                query_sums(1)
                queries(2)
                pe.wait_ge(*bank_free(b, "scores"))
                pe.wait_ge(*v_retr.at(b, "lmkT"))
                for i in range(NI):
                    ins = product(bank("scores")[:, i * C:(i + 1) * C], [(qrT[:, i, :, :].rearrange("p h q -> p (h q)"), lmkT[:, :])])
                ins.then_inc(*pe_retr.does("scores"))
                query_sums(2)
                queries(3)
                query_sums(3)

                def scores(u):
                    k = b * HKV + u
                    pe.wait_ge(*v_q.at(b, f"qb{u}"))
                    pe.wait_ge(*v_kT.at(b, "b"))
                    for name, bk, blocks in (("A", SA, BANK_A), ("B", SB, BANK_B)):
                        pe.wait_ge(*v_sc.at(k, f"sub{name}", -1))
                        for i in blocks:
                            c0 = (PAIR0[i] - PAIR0[blocks[0]]) * S
                            q_h, q_l = (a[:, u, i - 1, :, :].rearrange("p h q -> p (h q)") for a in (qo_hi, qo_lo))
                            ins = product(ps[:, bk, c0:c0 + i * S], split(q_h, q_l, kT_hi[:, u, 0:i * S], kT_lo[:, u, 0:i * S]))
                        ins.then_inc(*pe_qk.does(name))

                def transposes(u):
                    k = b * HKV + u
                    for n, (bk, blocks, k0, k1, made, (st, last)) in enumerate((
                            (R0, range(4, 8), 0, P, 4, (v_ot, "0")),
                            (R1, range(1, 4), 0, P, 1, (v_ot, "1")),
                            (R2, range(5, 8), P, TQ, 1, (v_pt, "2")))):
                        pe.wait_ge(*g_pr.at(k, f"p{made}"))
                        pe.wait_ge(*st.at(k, last, -1))
                        for m, i in enumerate(blocks):
                            ins = pe.transpose(ps[0:k1 - k0, bk, m * P:(m + 1) * P], prob[:, i - 1, k0:k1], ident[:, :])
                        ins.then_inc(*pe_pt.does(str(n)))

                def values(u):
                    k = b * HKV + u
                    d = slice(u * HD, (u + 1) * HD)

                    def pt(a, rows, c0, c1):
                        return a[0:rows, c0:c1, :].rearrange("p c r -> p (c r)")
                    r = TQ - P
                    pe.wait_ge(*v_kv.at(b, "vlo1"))
                    pe.wait_ge(*v_pt.at(k, "2"))
                    product(ps[:, R0, :], split(v_hi[:, 0, d], v_lo[:, 0, d], pt(pt_hi, P, 3, 7), pt(pt_lo, P, 3, 7)), stop=False)
                    product(ps[:, R0, P:], split(v_hi[0:r, 1, d], v_lo[0:r, 1, d], pt(pt_hi, r, 7, 10), pt(pt_lo, r, 7, 10)), start=False)\
                        .then_inc(*pe_pv.does("0"))
                    product(ps[:, R1, 0:3 * P], split(v_hi[:, 0, d], v_lo[:, 0, d], pt(pt_hi, P, 0, 3), pt(pt_lo, P, 0, 3)))\
                        .then_inc(*pe_pv.does("1"))

                def project(u):
                    k = b * HKV + u
                    pe.wait_ge(*v_ot.at(k, "1"))
                    if u == 0:
                        pe.wait_ge(*v_gate.at(b, "cT", -1))
                    for hh in range(G):
                        h = u * G + hh
                        for f in range(KF):
                            ins = product(ps[:, OB, f * TQ:(f + 1) * TQ],
                                          split(wo_hi[:, h, f * P:(f + 1) * P], wo_lo[:, h, f * P:(f + 1) * P],
                                                qo_hi[:, u, :, hh, :], qo_lo[:, u, :, hh, :]),
                                          start=(u == 0 and hh == 0 and f == 0), stop=(u == HKV - 1 and hh == G - 1))
                    ins.then_inc(*pe_o.does(f"o{u}"))

                scores(0)
                scores(1)
                transposes(0)
                values(0)
                scores(2)
                project(0)
                transposes(1)
                values(1)
                scores(3)
                project(1)
                transposes(2)
                values(2)
                project(2)
                transposes(3)
                values(3)
                project(3)

                pe.wait_ge(*v_x2.at(b, "x1"))
                for t in range(NT):
                    for k in range(KF):
                        ins = pe.transpose(ps[:, OB, t * D + k * P:t * D + (k + 1) * P], x2cur[:, k, t * P:(t + 1) * P], ident[:, :])
                ins.then_inc(*pe_tail.does("x"))
                pe.wait_ge(*v_x2.at(b, "xn1"))
                for k in range(KF):
                    for t in range(NT):
                        ins = pe.transpose(ps[:, OB, k * L + t * P:k * L + (t + 1) * P], xn2[:, t, k * P:(k + 1) * P], ident[:, :])
                ins.then_inc(*pe_tail.does("h"))
                pe.wait_ge(*v_x2.at(b, "h1"))
                for t in range(NT):
                    ins = product(ps[:, OB, t * E:(t + 1) * E], [(h2cur[:, k, t * P:(t + 1) * P], gate_sb[:, k, :]) for k in range(KF)])
                ins.then_inc(*pe_tail.does("gate"))
                pe.wait_ge(*v_gate.at(b, "lo"))
                for t in range(NT):
                    ins = product(ps[0:64, OB, t * P:(t + 1) * P], [(cpad[:, t, :], ident[:, :])])
                ins.then_inc(*pe_tail.does("cT"))

            def hidden(j, t, half, i):
                pe.wait_ge(*f_whi.at(j, "w"))
                pe.wait_ge(*f_wlo.at(j, "w"))
                for name, bk, w0 in (("h", 0, 0), ("u", 1, 2)):
                    pe.wait_ge(*f_dve.at(t, {"h": "a", "u": "b"}[name], -1))
                    product(ps[:, bk, :], [x_ for k in range(KF) for x_ in split(
                        w_hi[:, i, w0 + k, :], w_lo[:, i, w0 + k, :],
                        f_x_hi[:, k, half * HALF:(half + 1) * HALF], f_x_lo[:, k, half * HALF:(half + 1) * HALF])]).then_inc(*f_pe_h.does(name))
                pe.wait_ge(*f_dve.at(t, "g", -1))
                product(ps[:, R2, :], [(w_hi[0:64, i, 6, :], cw[:, 2 * half:2 * half + 2, :].rearrange("p b l -> p (b l)"))])\
                    .then_inc(*f_pe_h.does("c"))

            def down(t, half, i, first=False):
                pe.wait_ge(*f_ghi.at(t, "hi"))
                pe.wait_ge(*f_glo.at(t, "lo"))
                for f in range(KF):
                    ins = product(ps[:, 2 + 2 * half + f, :], split(w_hi[:, i, 4 + f, :], w_lo[:, i, 4 + f, :],
                                                                    f_g_hi[:, half, :], f_g_lo[:, half, :]), start=first)
                ins.then_inc(*f_pe_y.does("y"))

            pe.wait_ge(f_xhi, KF)
            pe.wait_ge(f_xlo, KF)
            hidden(0, 0, 0, 0)
            hidden(0, 1, 1, 0)
            down(0, 0, 0, True)
            hidden(1, 2, 0, 1)
            down(1, 1, 0, True)
            hidden(1, 3, 1, 1)
            down(2, 0, 1)
            with pe.Fori(1, (NJ - 1) // 2) as n:
                hidden(n * 2, n * 4, 0, 0)
                down(n * 4 - 1, 1, 1)
                hidden(n * 2, n * 4 + 1, 1, 0)
                down(n * 4, 0, 0)
                hidden(n * 2 + 1, n * 4 + 2, 0, 1)
                down(n * 4 + 1, 1, 0)
                hidden(n * 2 + 1, n * 4 + 3, 1, 1)
                down(n * 4 + 2, 0, 1)
            hidden(NJ - 1, 2 * NJ - 2, 0, 0)
            down(2 * NJ - 3, 1, 1)
            hidden(NJ - 1, 2 * NJ - 1, 1, 0)
            down(2 * NJ - 2, 0, 0)
            down(2 * NJ - 1, 1, 0)


def W_PARTS(g_att, g_retr):
    return (0, 2 * KVW, g_att), (2 * KVW, 2 * KVW + RD, g_retr), (2 * KVW + RD, NKV, g_att)


def kernel(**inputs):
    import numpy as np
    import concourse.bacc as bacc
    from concourse.bass_utils import run_bass_kernel_spmd

    g = {k.removeprefix("L0_").removeprefix("attn_").removeprefix("ffn_"): np.asarray(v) for k, v in inputs.items()}
    t = np.ascontiguousarray
    x = g["hidden_states"]
    pad = NJP * P - NHID

    def hidden_tiles(routed, shared):
        w = np.concatenate([routed.transpose(1, 0, 2).reshape(D, E * HE), shared], axis=1)
        w = np.pad(w, ((0, 0), (0, pad)))
        return w.reshape(KF, P, NJP, P).transpose(2, 1, 0, 3)

    w2 = np.pad(np.concatenate([g["w2"].reshape(E * HE, D), g["sw2"]], axis=0), ((0, pad), (0, 0))).reshape(NJP, P, KF, P)
    member = np.zeros((P, NJP * P), np.float32)
    for e in range(E + 1):
        member[e, e * HE:(e + 1) * HE] = 1.0
        member[32 + e, e * HE:(e + 1) * HE] = 1.0
    member = member.reshape(P, NJP, 1, P).transpose(1, 0, 2, 3)
    arrays = {
        "x": t(x),
        "xT": t(x.transpose(2, 0, 1)),
        "wq": t(g["w_q"].T), "wk": t(g["w_k"].T), "wv": t(g["w_v"].T),
        "wr": t(g["w_q_retr"].T), "wl": t(g["w_lmk"].T), "wo": t(g["w_o"].T),
        "gains_d": t(np.stack([g["g_pre"], g["g_chunk_norm"], g["g_pre_retr"]]).reshape(3, KF, P).transpose(2, 0, 1)),
        "gains_hd": t(np.stack([g["g_k_norm"], g["g_q_norm"]], axis=1)),
        "gains_rd": t(np.stack([g["g_q_retr"], g["g_lmk"]], axis=1)),
        "gateT": t(g["gate_w"].T), "cT": t(g["c"].T), "wmod": t(g["wmod"]),
        "wffn": t(np.concatenate([hidden_tiles(g["w1"], g["sw1"]), hidden_tiles(g["w3"], g["sw3"]), w2, member], axis=2)),
    }
    nc = bacc.Bacc("TRN2", target_bir_lowering=False, num_devices=1)
    handles = [nc.dram_tensor(k, a.shape, mybir.dt.from_np(a.dtype), kind="ExternalInput").ap() for k, a in arrays.items()]
    out = nc.dram_tensor("out", (D, B, L), F32, kind="ExternalOutput").ap()
    build(nc, *handles, out)
    r = run_bass_kernel_spmd(nc, [arrays], core_ids=[0])
    return np.ascontiguousarray(r.results[0]["out"].transpose(1, 2, 0))
```

```python
from contextlib import ExitStack

import concourse.bass as bass
from concourse import mybir

F32 = mybir.dt.float32
F32R = mybir.dt.float32r
I32 = mybir.dt.int32
ALU = mybir.AluOpType
ACT = mybir.ActivationFunctionType
AX = mybir.AxisListType.X

P = 128
B = 4
L = 256
D = 256
KF = D // P
NT = L // P
H = 16
HKV = 4
G = H // HKV
HD = 128
S = 32
C = L // S
RD = 32
NI = C - 1
TQ = NI * S
EPS = 1e-5
E = 8
HE = 176
NHID = (E + 1) * HE
NJ = (NHID + P - 1) // P
NJP = NJ + 1
POOL_CONSTS = 29
GAINS = 7
MOD_STEPS = 11
SCALED = 8
NV = NT * HKV + NT + 1
ROUTED = 2.5
KVW = HKV * HD
NKV = 2 * KVW + 2 * RD
HALF = 512
RSQRT_MAGIC = float(0x5F3759DF)

BANK_A = (7, 6, 3)
BANK_B = (5, 4, 2, 1)
PAIR0 = {}
NPAIR = 0
for _i in BANK_A + BANK_B:
    PAIR0[_i] = NPAIR
    NPAIR += _i
PAIRS_A = sum(BANK_A)
COLS = NPAIR * S


class Steps:

    def __init__(self, nc_sem, names, credit):
        self.sem, self.names, self.credit, self.at_name = nc_sem, names, credit, 0

    def does(self, name):
        assert self.names[self.at_name] == name, (self.names[self.at_name], name)
        self.at_name = (self.at_name + 1) % len(self.names)
        return self.sem, 1

    def at(self, unit, name, off=0):
        return self.sem, unit * len(self.names) + ((off + self.credit) * len(self.names) + self.names.index(name) + 1)

    def start(self, eng):
        eng.sem_inc(self.sem, self.credit * len(self.names))


def newton(name):
    return [f"{name}.{n}" for n in range(11)]


def build(nc, x, xT, wq, wk, wv, wr, wl, wo, gains_d, gains_hd, gains_rd, gateT, cT, wmod, wffn, out):
    with ExitStack() as top:
        def sem(name):
            return top.enter_context(nc.semaphore(name))

        def sb(name, shape, dt=F32, ctx=top):
            return ctx.enter_context(nc.sbuf_tensor(name, shape, dt))

        ps = top.enter_context(nc.psum_tensor("banks", [P, 8, 512], F32))
        SA, SB = 2, 3
        R0, R1, R2 = 4, 5, 6
        OB = 7

        ident = sb("ident", [P, P])
        ones = sb("ones", [P, 1])
        pick = sb("pick", [P, 4, P])
        chunk_mean = sb("chunk_mean", [P, NT, C])
        rank = sb("rank", [P, NT, E])
        causal = sb("causal", [P, NI, C])
        w_q, w_kv, w_o = sb("w_q", [P, KF, H * HD]), sb("w_kv", [P, KF, NKV]), sb("w_o", [P, H, D])
        gd = sb("gd", [P, 3, KF])
        ghd = sb("ghd", [P, 2])
        grd = sb("grd", [RD, 2])
        g_att, g_retr, g_sq = (sb(n, [P, KF]) for n in ("g_att", "g_retr", "g_sq"))
        statv = sb("statv", [P, KF, 2])
        gqk, grl = sb("gqk", [P, 1]), sb("grl", [RD, 1])
        gate_sb = sb("gate_sb", [P, KF, E])
        cT_sb, silu_c = sb("cT_sb", [P, KF, B]), sb("silu_c", [P, KF, B])
        gsgn, gabs = sb("gsgn", [P, B, 2]), sb("gabs", [P, B, 2])
        modT = sb("modT", [P, B, 12])
        x2T = sb("x2T", [P, KF, B, L])
        xn = sb("xn", [P, B * NT, D])
        hT = sb("hT", [P, KF, B, L])
        f_x_hi, f_x_lo = sb("f_x_hi", [P, KF, B, L], F32R), sb("f_x_lo", [P, KF, B, L], F32R)
        cw = sb("cw", [64, B, L], F32R)
        bn6, mv = sb("bn6", [P, B * NT, 6]), sb("mv", [P, B * NT, 2])
        var, rstd = sb("var", [P, B * NT]), sb("rstd", [P, B * NT])
        tok = sb("tok", [P, B, 2, NT])
        tscale, epsT, qeps = sb("tscale", [P, B, NT]), sb("epsT", [P, B, NT]), sb("qeps", [P, B, NI])
        hcur, squares = sb("hcur", [P, KF, L]), sb("squares", [P, KF * L])
        stok = sb("stok", [P, NT])
        kraw = sb("kraw", [P, NT, KVW])
        kss, rss = sb("kss", [P, NT, HKV]), sb("rss", [P, NT])
        nv, nr = sb("nv", [P, NV]), sb("nr", [P, NV])
        rraw, rsq = sb("rraw", [P, NT, 2 * RD]), sb("rsq", [P, NT, RD])
        rqn, lmn = sb("rqn", [P, NT, RD]), sb("lmn", [P, NT, RD])
        lsum, lsq, lnorm, lss = sb("lsum", [C, RD]), sb("lsq", [C, RD]), sb("lnorm", [C, RD]), sb("lss", [C, 1])
        lmkT, qrT = sb("lmkT", [RD, C]), sb("qrT", [RD, NI, G, S])
        rsc, rex = sb("rsc", [P, NI, C]), sb("rex", [P, NI, C])
        rmx, rsum, rrec = sb("rmx", [P, NI]), sb("rsum", [P, NI]), sb("rrec", [P, NI])
        rw = sb("rw", [P, NPAIR])
        v_sb, kT = sb("v_sb", [P, NT, KVW]), sb("kT", [P, HKV, TQ])
        qT = sb("qT", [P, HKV, NI, G, S])
        q_sq = sb("q_sq", [P, 2, NI, G, S])
        qvar, rnq = sb("qvar", [P, HKV, NI]), sb("rnq", [P, HKV, NI])
        nw1, nw2 = sb("nw1", [P, HKV * NI]), sb("nw2", [P, HKV * NI])
        x2cur, tail = sb("x2cur", [P, KF, L]), sb("tail", [P, KF * L])
        xn2, h2cur = (tail[:, :].rearrange("p (a b) -> p a b", a=2) for _ in range(2))
        mod_out = sb("mod_out", [P, 6])
        bn6o, mvo, varo, rstdo = sb("bn6o", [P, NT, 6]), sb("mvo", [P, NT, 2]), sb("varo", [P, NT]), sb("rstdo", [P, NT])
        gth, gsc, gk1, gk2, gs1, gs2, gsc2 = (sb(n, [P, NT, E]) for n in ("gth", "gsc", "gk1", "gk2", "gs1", "gs2", "gsc2"))
        gm1, gm2, gx1, gx2, gden, grec = (sb(n, [P, NT]) for n in ("gm1", "gm2", "gx1", "gx2", "gden", "grec"))
        cfull, c_hi = sb("cfull", [P, NT, E + 1]), sb("c_hi", [P, NT, E + 1], F32R)
        cpad = sb("cpad", [P, NT, 64])
        smax, ssum, srec, wpair = (sb(n, [P, 2, NPAIR]) for n in ("smax", "ssum", "srec", "wpair"))
        d_sc = sb("d_sc", [P, 2, COLS])
        pt = sb("pt", [P, 10, P])
        ao = sb("ao", [P, 2, NI, G, S])
        NW = 7
        w_raw = sb("w_raw", [P, 2, NW, P])
        w_hi, w_lo = sb("w_hi", [P, 2, NW, P], F32R), sb("w_lo", [P, 2, NW - 1, P], F32R)
        f_g_hi, f_g_lo = sb("f_g_hi", [P, 2, HALF], F32R), sb("f_g_lo", [P, 2, HALF], F32R)
        with ExitStack() as early:
            wmod_sb = sb("wmod_sb", [P, KF, 6 * D], F32, early)
        f_th, f_a, f_g = (sb(n, [P, 2, HALF]) for n in ("f_th", "f_a", "f_g"))
        f_out = xn[:, :, :].rearrange("p (k b) d -> p k b d", k=KF)

        ld_x0, ld_x, ld_xT, ld_gain, ld_c, ld_mod, ld_kv, ld_q, ld_o, ld_gate = (
            sem(n) for n in ("ld_x0", "ld_x", "ld_xT", "ld_gain", "ld_c", "ld_mod", "ld_kv", "ld_q", "ld_o", "ld_gate"))
        ld_w = [sem("ld_w0"), sem("ld_w1")]
        st_out = sem("st_out")
        pool_const, gains_ready, silu_steps, mod_product, mod_steps, w_scaled, bank_init, xn_steps = (
            sem(n) for n in ("pool_const", "gains_ready", "silu_steps", "mod_product", "mod_steps", "w_scaled", "bank_init", "xn_steps"))
        hT_prod, h_ready, hsq_ready, base_ready, stat_prod, tok_ready, rows_prod, qeps_ready, s_steps = (
            sem(n) for n in ("hT_prod", "h_ready", "hsq_ready", "base_ready", "stat_prod", "tok_ready", "rows_prod", "qeps_ready", "s_steps"))

        def steps(name, names, credit=1):
            return Steps(sem(name), names, credit)

        pe_kv = steps("pe_kv", ["R", "K0", "K1"])
        pe_v = steps("pe_v", ["V0", "V1"])
        pe_kT = steps("pe_kT", ["kTa", "kTb"])
        pe_retr = steps("pe_retr", ["lmean", "qrT", "scores"])
        pe_q = steps("pe_q", ["qa0", "qb0", "qa1", "ss0", "qb1", "ss1", "qa2", "qb2", "qa3", "ss2", "qb3", "ss3"])
        pe_tail = steps("pe_tail", ["x", "h", "gate", "cT"])
        v_kv = steps("v_kv", ["rraw", "rsq", "rss", "stok", "lmn", "kss0", "kss1", "lsum", "lsq", "lss", "nvl", "nvk", "nvr",
                              *newton("nr"), "rqn", "lnorm"])
        v_retr = steps("v_retr", ["qrT", "lmkT", "masked", "max", "sub", "sum", "rec"])
        v_q = steps("v_q", [f"ss{u}" for u in range(HKV)] + newton("rnq"))
        v_x2 = steps("v_x2", ["mod", "copy", "x0", "x1", "bn0", "bn1", "mod2", "ag0", "ag1", "var", *newton("rs"), "xn0", "xn1",
                              "h0", "h1", "hi"])
        v_gate = steps("v_gate", ["sc", "m1", "e1", "k1", "x1", "s1", "sc2", "m2", "e2", "k2", "x2", "s2", "den",
                                  "rec", "sel", "num", "c", "hi", "pad", "lo", "cT"])
        a_kv = steps("a_kv", ["kraw0", "ksq0", "kraw1", "ksq1"])
        a_v = steps("a_v", ["v0", "v1"])
        a_kT = steps("a_kT", ["a", "b"])
        a_retr = steps("a_retr", ["exp"])
        a_q = steps("a_q", [f"{n}{m}{u}" for u in range(HKV) for m in "ab" for n in ("sq", "q")])
        a_gate = steps("a_gate", ["tanh"])
        g_h = steps("g_h", ["h"])
        g_kn = steps("g_kn", ["0", "1"])
        g_rw = steps("g_rw", [f"r{i}" for i in range(1, C)])
        g_keep = steps("g_keep", ["x2", "lo"])
        pe_qk = steps("pe_qk", ["A", "B"], HKV)
        pe_pt = steps("pe_pt", ["0", "1", "2"], 2)
        pe_pv = steps("pe_pv", ["0", "1"])
        pe_o = steps("pe_o", ["o"], 2)
        v_sc = steps("v_sc", ["maxA", "subA", "maxB", "subB"])
        v_w = steps("v_w", ["sum", "rec", "w"])
        a_exp = steps("a_exp", [f"e{i}" for i in BANK_A + BANK_B])
        a_pt = steps("a_pt", ["0", "1", "2"])
        a_ao = steps("a_ao", ["0", "1"])
        g_pr = steps("g_pr", ["A", "B"], 2)

        f_whi, f_wlo = steps("f_whi", ["w"]), steps("f_wlo", ["w"])
        f_pe_h, f_pe_y = steps("f_pe_h", ["h", "u", "c"]), steps("f_pe_y", ["y"])
        f_act = steps("f_act", ["th"])
        f_ghi = steps("f_ghi", ["hi"])
        f_dve = steps("f_dve", ["a", "b", "g"])
        f_glo = steps("f_glo", ["lo"])
        f_fin = sem("f_fin")

        ring = [("tx", v_x2, "xn1"), ("R", v_kv, "rraw"), ("K0", a_kv, "ksq0"), ("K1", a_kv, "ksq1"), ("th", v_x2, "h1"),
                ("lmean", v_kv, "lsum"), ("tg", a_gate, "tanh"), ("qa0", a_q, "qa0"), ("qb0", a_q, "qb0"),
                ("qa1", a_q, "qa1"), ("ss0", v_q, "ss0"), ("qb1", a_q, "qb1"), ("qrT", v_retr, "lmkT"),
                ("kTa", a_kT, "a"), ("kTb", a_kT, "b"), ("ss1", v_q, "ss1"), ("qa2", a_q, "qa2"), ("qb2", a_q, "qb2"),
                ("scores", v_retr, "masked"), ("qa3", a_q, "qa3"), ("ss2", v_q, "ss2"), ("qb3", a_q, "qb3"),
                ("tc", v_gate, "cT"), ("ss3", v_q, "ss3"), ("V0", a_v, "v0"), ("V1", a_v, "v1")]
        ring_names = [r[0] for r in ring]

        def ring_bank(name):
            return ring_names.index(name) % 2

        def bank(name):
            return ps[:, ring_bank(name), :]

        xn_done = {}
        block = top.enter_context(nc.Block())

        @block.sync
        def _(sp):
            sp.dma_start(cT_sb[:, :, :], cT.rearrange("(k p) b -> p k b", p=P)).then_inc(ld_c, 16)
            for b in range(B):
                if b == 1:
                    sp.dma_start(gd[:, :, :], gains_d).then_inc(ld_gain, 16)
                    sp.dma_start(ghd[:, :], gains_hd).then_inc(ld_gain, 16)
                    sp.dma_start(grd[:, :], gains_rd).then_inc(ld_gain, 16)
                    sp.dma_start(wmod_sb[:, :, :], wmod.rearrange("(k p) n -> p k n", p=P)).then_inc(ld_mod, 16)
                sp.dma_start(xn[:, b * NT:(b + 1) * NT, :], x[b, :, :].rearrange("(t p) d -> p t d", p=P))\
                  .then_inc(ld_x if b else ld_x0, 16)
            for w, n0, n in ((wr, 2 * KVW, RD), (wl, 2 * KVW + RD, RD), (wk, 0, KVW), (wv, KVW, KVW)):
                sp.dma_start(w_kv[:, :, n0:n0 + n], w.rearrange("(k p) n -> p k n", p=P)).then_inc(ld_kv, 16)
            for k in range(KF):
                sp.dma_start(w_q[:, k, :], wq[k * P:(k + 1) * P, :]).then_inc(ld_q, 16)
            sp.dma_start(x2T[:, :, :, :], xT.rearrange("(k p) b l -> p k b l", p=P)).then_inc(ld_xT, 16)
            sp.dma_start(w_o[:, :, :], wo.rearrange("(h p) n -> p h n", p=P)).then_inc(ld_o, 16)
            sp.dma_start(gate_sb[:, :, :], gateT.rearrange("(k p) e -> p k e", p=P)).then_inc(ld_gate, 16)
            for j in range(2):
                sp.dma_start(w_raw[:, j, :, :], wffn[j, :, :, :]).then_inc(ld_w[j], 16)
            with sp.Fori(0, (NJP - 2) // 2) as n:
                for j in range(2):
                    sp.wait_ge(*f_whi.at(n * 2, "w", j))
                    sp.wait_ge(*f_wlo.at(n * 2, "w", j))
                    sp.dma_start(w_raw[:, j, :, :], wffn[bass.ds(n * 2 + 2 + j, 1), :, :, :].rearrange("o p s n -> p (o s) n"))\
                      .then_inc(ld_w[j], 16)
            for n in range(KF * 2):
                k, half = n % 2, n // 2
                sp.wait_ge(f_fin, 2 * (n + 1))
                sp.dma_start(out[k * P:(k + 1) * P, 2 * half:2 * half + 2, :], f_out[:, k, 2 * half:2 * half + 2, :]).then_inc(st_out, 16)
            sp.wait_ge(st_out, 16 * KF * 2)

        @block.gpsimd
        def _(pool):
            for st in (g_h, g_kn, g_rw, g_pr, g_keep, f_glo):
                st.start(pool)
            n = 0

            def const(ins):
                nonlocal n
                ins.then_inc(pool_const, 1)
                n += 1
                pool.wait_ge(pool_const, n)

            const(pool.memset(ident[:, :], 0.0))
            const(pool.affine_select(out=ident[:, :], in_=ident[:, :], compare_op=ALU.not_equal, fill=1.0,
                                     base=0, pattern=[[-1, P]], channel_multiplier=1))
            const(pool.memset(ones[:, :], 1.0))
            for m in range(4):
                const(pool.tensor_copy(pick[:, m, :].rearrange("p (r q) -> p r q", q=S),
                                       ident[:, m * S:(m + 1) * S].unsqueeze(1).broadcast_to([P, G, S])))
            const(pool.memset(chunk_mean[:, :, :], 1.0 / S))
            const(pool.affine_select(out=chunk_mean[:, :, :], in_=chunk_mean[:, :, :], compare_op=ALU.is_ge, fill=0.0,
                                     base=0, pattern=[[P, NT], [-S, C]], channel_multiplier=1))
            const(pool.affine_select(out=chunk_mean[:, :, :], in_=chunk_mean[:, :, :], compare_op=ALU.is_ge, fill=0.0,
                                     base=S - 1, pattern=[[-P, NT], [S, C]], channel_multiplier=-1))
            for e in range(E):
                const(pool.memset(rank[:, :, e:e + 1], float(E - e)))
            const(pool.memset(causal[:, :, :], 0.0))
            for i in range(1, C):
                const(pool.memset(causal[:, i - 1, i:C], -1e30))
            const(pool.memset(cpad[:, :, :], 0.0))
            const(pool.memset(cfull[:, :, E:E + 1], 0.5))
            const(pool.memset(nv[:, NV - 1:NV], 1.0))
            assert n == POOL_CONSTS, n

            def take_h(b, o):
                pool.wait_ge(*pe_v.at(b, "V1", o - 1))
                pool.tensor_copy(hcur[:, :, :], hT[:, :, bass.ds(b + o, 1), :].rearrange("p k o l -> p k (o l)")).then_inc(*g_h.does("h"))

            def keys(b, o):
                pool.wait_ge(*v_kv.at(b, "nr.10", o))
                pool.wait_ge(*a_kv.at(b, "kraw1", o))
                for t in range(NT):
                    kk = kraw[:, t, :].rearrange("p (g d) -> p g d", d=HD)
                    r = nr[:, t * HKV:(t + 1) * HKV].unsqueeze(2).broadcast_to([P, HKV, HD])
                    pool.tensor_tensor(kk, kk, r, ALU.mult).then_inc(*g_kn.does(str(t)))

            def chunk_weights(b, o):
                pool.wait_ge(*v_retr.at(b, "rec", o))
                pool.wait_ge(*v_w.at(b * HKV, "w", (o - 1) * HKV + 3))
                for i in range(1, C):
                    pool.tensor_tensor(rw[:, PAIR0[i]:PAIR0[i] + i], rex[:, i - 1, 0:i], rrec[:, i - 1:i].broadcast_to([P, i]), ALU.mult)\
                        .then_inc(*g_rw.does(f"r{i}"))

            def weigh(b, u):
                pool.wait_ge(*v_w.at(b * HKV, "w", u))
                for name, p0, p1 in (("A", 0, PAIRS_A), ("B", PAIRS_A, NPAIR)):
                    seg = d_sc[:, u % 2, S * p0:S * p1].rearrange("p (n k) -> p n k", k=S)
                    w = wpair[:, u % 2, p0:p1].unsqueeze(2).broadcast_to([P, p1 - p0, S])
                    pool.tensor_tensor(seg, seg, w, ALU.mult).then_inc(*g_pr.does(name))

            def keep_x2(b, o):
                pool.wait_ge(*v_x2.at(b, "x1", o))
                pool.tensor_copy(x2T[:, :, bass.ds(b + o, 1), :].rearrange("p k o l -> p k (o l)"), x2cur[:, :, :])\
                    .then_inc(*g_keep.does("x2"))

            def keep_lo(b, o):
                pool.wait_ge(*v_x2.at(b, "hi", o))
                pool.tensor_tensor(f_x_lo[:, :, bass.ds(b + o, 1), :].rearrange("p k o l -> p k (o l)"), h2cur,
                                   f_x_hi[:, :, bass.ds(b + o, 1), :].rearrange("p k o l -> p k (o l)").bitcast(F32), ALU.subtract)\
                    .then_inc(*g_keep.does("lo"))

            def iteration(b, head, tail_):
                if head:
                    take_h(b, 1)
                weigh(b, 1)
                if tail_:
                    keep_x2(b, -1)
                    keep_lo(b, -1)
                weigh(b, 2)
                if head:
                    keys(b, 1)
                weigh(b, 3)
                if head:
                    chunk_weights(b, 1)
                    weigh(b, 4)

            pool.wait_ge(h_ready, KF)
            take_h(0, 0)
            keys(0, 0)
            chunk_weights(0, 0)
            weigh(0, 0)
            iteration(0, True, False)
            with pool.Fori(1, B - 1) as b:
                iteration(b, True, True)
            iteration(B - 1, False, True)
            keep_x2(B - 1, 0)
            keep_lo(B - 1, 0)

            def g_lo(t, o, i, first=False):
                pool.wait_ge(*f_ghi.at(t, "hi", o))
                if not first:
                    pool.wait_ge(*f_pe_y.at(t, "y", o - 2))
                pool.tensor_tensor(f_g_lo[:, i, :], f_g[:, i, :], f_g_hi[:, i, :].bitcast(F32), ALU.subtract)\
                    .then_inc(*f_glo.does("lo"))

            for i in range(2):
                g_lo(i, 0, i, True)
            with pool.Fori(1, NJ) as j:
                for i in range(2):
                    g_lo(j * 2, i, i)

        @block.scalar
        def _(act):
            for st in (a_kv, a_v, a_kT, a_retr, a_q, a_exp, a_pt, a_ao, a_gate, f_whi, f_act, f_ghi):
                st.start(act)
            act.wait_ge(ld_c, 16)
            act.activation(silu_c[:, :, :], cT_sb[:, :, :], ACT.Tanh, scale=0.5).then_inc(silu_steps, 1)
            for b in range(B):
                act.wait_ge(h_ready, KF * (b + 1))
                if b:
                    act.wait_ge(stat_prod, b)
                act.activation(squares[:, :].rearrange("p (k l) -> p k l", k=KF), hT[:, :, b, :], ACT.Square).then_inc(hsq_ready, 1)
                if b == 0:
                    act.wait_ge(gains_ready, GAINS)
                    act.wait_ge(ld_kv, 64)
                    for k in range(KF):
                        for n0, n1, g in W_PARTS(g_att, g_retr):
                            act.activation(w_kv[:, k, n0:n1], w_kv[:, k, n0:n1], ACT.Copy, scale=g[:, k:k + 1]).then_inc(w_scaled, 1)
            act.wait_ge(ld_q, 16 * KF)
            for k in range(KF):
                act.activation(w_q[:, k, :], w_q[:, k, :], ACT.Copy, scale=gd[:, 0, k:k + 1]).then_inc(w_scaled, 1)

            def key_tiles(b, o):
                act.wait_ge(*pe_kT.at(b, "kTb", o - 1))
                for t in range(NT):
                    act.wait_ge(*pe_kv.at(b, f"K{t}", o))
                    act.activation(kraw[:, t, :], bank(f"K{t}"), ACT.Copy).then_inc(*a_kv.does(f"kraw{t}"))
                    act.wait_ge(*(v_kv.at(b, "kss0", o) if t else v_kv.at(b, "kss1", o - 1)))
                    act.activation(squares[:, :], bank(f"K{t}"), ACT.Square).then_inc(*a_kv.does(f"ksq{t}"))

            def value_tiles(b, o):
                for t in range(NT):
                    act.wait_ge(*pe_v.at(b, f"V{t}", o))
                    act.wait_ge(*v_kv.at(b, "stok", o))
                    act.wait_ge(*pe_pv.at(b * HKV, "1", (o - 1) * HKV + 3))
                    act.activation(v_sb[:, t, :], bank(f"V{t}"), ACT.Copy, scale=stok[:, t:t + 1]).then_inc(*a_v.does(f"v{t}"))

            def queries(b, o, u, m):
                name = f"{'ab'[m]}{u}"
                act.wait_ge(*pe_q.at(b, f"q{name}", o))
                act.wait_ge(*(pe_q.at(b, f"ss{u - 2}", o) if u > 1 else pe_q.at(b, f"ss{u + 2}", o - 1)))
                act.wait_ge(*pe_qk.at(b * HKV, "B", (o - 1) * HKV + u))
                src = bank(f"q{name}")[:, 0:2 * TQ].rearrange("p (h i q) -> p i h q", h=2, q=S)
                act.activation(q_sq[:, u % 2, :, 2 * m:2 * m + 2, :], src, ACT.Square).then_inc(*a_q.does(f"sq{name}"))
                act.activation(qT[:, u, :, 2 * m:2 * m + 2, :], src, ACT.Copy).then_inc(*a_q.does(f"q{name}"))

            def keys_T(b, o):
                act.wait_ge(*pe_qk.at(b * HKV, "B", (o - 1) * HKV + 3))
                for n, name in enumerate("ab"):
                    act.wait_ge(*pe_kT.at(b, f"kT{name}", o))
                    act.activation(kT[:, 2 * n:2 * n + 2, :], bank(f"kT{name}").rearrange("p (g l) -> p g l", l=L)[:, :, 0:TQ],
                                   ACT.Copy, scale=gqk[:, 0:1]).then_inc(*a_kT.does(name))

            def retrieval(b, o):
                act.wait_ge(*v_retr.at(b, "sub", o))
                act.wait_ge(*g_rw.at(b, f"r{NI}", o - 1))
                act.activation(rex[:, :, :], rsc[:, :, :], ACT.Exp).then_inc(*a_retr.does("exp"))

            def exps(b, u):
                act.wait_ge(*v_q.at(b, "rnq.10", u // HKV))
                for i in BANK_A + BANK_B:
                    act.wait_ge(*v_sc.at(b * HKV, "subA" if i in BANK_A else "subB", u))
                    seg = d_sc[:, u % 2, S * PAIR0[i]:S * (PAIR0[i] + i)]
                    act.activation(seg, seg, ACT.Exp, scale=rnq[:, u % HKV, i - 1:i]).then_inc(*a_exp.does(f"e{i}"))

            def probs_T(b, u):
                act.wait_ge(*pe_pv.at(b * HKV, "1", u - 1))
                for n, (bk, rows, c0, c1) in enumerate(((R0, P, 3, 7), (R2, TQ - P, 7, 10), (R1, TQ - P, 0, 3))):
                    act.wait_ge(*pe_pt.at(b * HKV, str(n), u))
                    act.activation(pt[0:rows, c0:c1, :].rearrange("p c r -> p (c r)"), ps[0:rows, bk, 0:(c1 - c0) * P],
                                   ACT.Copy).then_inc(*a_pt.does(str(n)))

            def outputs(b, u):
                act.wait_ge(*pe_o.at(b * HKV, "o", u - 2))
                for n, (bk, i0, i1) in enumerate(((R0, 3, 7), (R1, 0, 3))):
                    act.wait_ge(*pe_pv.at(b * HKV, str(n), u))
                    act.activation(ao[:, u % 2, i0:i1, :, :].rearrange("p i h q -> p (i h q)"), ps[:, bk, 0:(i1 - i0) * P],
                                   ACT.Copy).then_inc(*a_ao.does(str(n)))

            def gate_scores(b, o):
                act.wait_ge(*pe_tail.at(b, "gate", o))
                act.activation(gth[:, :, :], bank("tg")[:, 0:NT * E].rearrange("p (t e) -> p t e", e=E), ACT.Tanh, scale=0.5)\
                    .then_inc(*a_gate.does("tanh"))

            def iteration(b, head, tail_):
                probs_T(b, 0)
                exps(b, 1)
                outputs(b, 0)
                if head:
                    key_tiles(b, 1)
                probs_T(b, 1)
                exps(b, 2)
                outputs(b, 1)
                if tail_:
                    gate_scores(b, -1)
                if head:
                    for u, m in ((0, 0), (0, 1), (1, 0), (1, 1)):
                        queries(b, 1, u, m)
                probs_T(b, 2)
                exps(b, 3)
                outputs(b, 2)
                if head:
                    keys_T(b, 1)
                    for u, m in ((2, 0), (2, 1)):
                        queries(b, 1, u, m)
                    retrieval(b, 1)
                    for u, m in ((3, 0), (3, 1)):
                        queries(b, 1, u, m)
                probs_T(b, 3)
                if head:
                    exps(b, 4)
                outputs(b, 3)
                if head:
                    value_tiles(b, 1)

            key_tiles(0, 0)
            for u, m in ((0, 0), (0, 1), (1, 0), (1, 1)):
                queries(0, 0, u, m)
            keys_T(0, 0)
            for u, m in ((2, 0), (2, 1)):
                queries(0, 0, u, m)
            retrieval(0, 0)
            for u, m in ((3, 0), (3, 1)):
                queries(0, 0, u, m)
            exps(0, 0)
            value_tiles(0, 0)
            iteration(0, True, False)
            with act.Fori(1, B - 1) as b:
                iteration(b, True, True)

            def w_high(i, count):
                act.wait_ge(ld_w[i], count)
                act.activation(w_hi[:, i, :, :], w_raw[:, i, :, :], ACT.Copy).then_inc(*f_whi.does("w"))

            def gate(t, o, i, first=False):
                act.wait_ge(*f_pe_h.at(t, "h", o))
                if not first:
                    act.wait_ge(*f_dve.at(t, "a", o - 2))
                act.activation(f_th[:, i, :], ps[:, 2, :], ACT.Tanh, scale=0.5).then_inc(*f_act.does("th"))
                act.wait_ge(*f_dve.at(t, "g", o))
                if not first:
                    act.wait_ge(*f_pe_y.at(t, "y", o - 2))
                    act.wait_ge(*f_glo.at(t, "lo", o - 2))
                act.activation(f_g_hi[:, i, :], f_g[:, i, :], ACT.Copy).then_inc(*f_ghi.does("hi"))

            w_high(0, 16)
            w_high(1, 16)
            iteration(B - 1, False, True)
            gate_scores(B - 1, 0)

            gate(0, 0, 0, True)
            gate(0, 1, 1, True)
            with act.Fori(0, (NJ - 1) // 2) as n:
                gate(n * 4, 2, 0)
                act.wait_ge(*f_pe_y.at(n * 4, "y", 1))
                w_high(0, n * 16 + 32)
                gate(n * 4, 3, 1)
                gate(n * 4, 4, 0)
                act.wait_ge(*f_pe_y.at(n * 4, "y", 3))
                w_high(1, n * 16 + 32)
                gate(n * 4, 5, 1)

        @block.vector
        def _(dve):
            for st in (v_kv, v_retr, v_q, v_sc, v_w, v_x2, v_gate, f_wlo, f_dve):
                st.start(dve)

            def step(st, b, o, name, ins, wait=True):
                ins.then_inc(*st.does(name))
                if wait:
                    dve.wait_ge(*st.at(b, name, o))

            def rsqrt(signal, y, v):
                rows, cols = v.shape[0], v.shape[-1]
                t1, t2 = nw1[0:rows, 0:cols], nw2[0:rows, 0:cols]
                signal(0, dve.tensor_scalar(t1.bitcast(I32), v.bitcast(I32), 1, None, ALU.logical_shift_right))
                signal(1, dve.tensor_scalar(y.bitcast(I32), t1.bitcast(I32), -1.0, RSQRT_MAGIC, ALU.mult, ALU.add))
                for n in range(3):
                    signal(3 * n + 2, dve.scalar_tensor_tensor(out=t1, in0=y, scalar=-0.5, in1=y, op0=ALU.mult, op1=ALU.mult))
                    signal(3 * n + 3, dve.tensor_tensor(t2, t1, v, ALU.mult))
                    signal(3 * n + 4, dve.scalar_tensor_tensor(out=y, in0=t2, scalar=1.5, in1=y, op0=ALU.add, op1=ALU.mult))

            for bk in (R1, R2):
                dve.memset(ps[:, bk, :], 0.0).then_inc(bank_init, 1)

            dve.wait_ge(silu_steps, 1)
            dve.scalar_tensor_tensor(out=silu_c[:, :, :], in0=silu_c[:, :, :], scalar=1.0, in1=cT_sb[:, :, :],
                                     op0=ALU.add, op1=ALU.mult).then_inc(silu_steps, 1)

            n = 0

            def xstep(ins, wait=True):
                nonlocal n
                ins.then_inc(xn_steps, 1)
                n += 1
                if wait:
                    dve.wait_ge(xn_steps, n)

            for t0, t1 in ((0, NT), (NT, B * NT)):
                if t0:
                    dve.wait_ge(ld_x, 16 * (B - 1))
                else:
                    dve.wait_ge(ld_x0, 16)
                for t in range(t0, t1):
                    xstep(dve.bn_stats(bn6[:, t, :], xn[:, t, :]), wait=t == t1 - 1)
                for t in range(t0, t1):
                    xstep(dve.bn_aggr(mv[:, t, :], bn6[:, t, :]), wait=t == t1 - 1)
                xstep(dve.tensor_scalar(var[:, t0:t1], mv[:, t0:t1, 1], EPS, None, ALU.add))
                rsqrt(lambda _, ins: xstep(ins), rstd[:, t0:t1], var[:, t0:t1])
                for t in range(t0, t1):
                    xstep(dve.tensor_scalar(xn[:, t, :], xn[:, t, :], mv[:, t, 0:1], rstd[:, t:t + 1], ALU.subtract, ALU.mult), wait=False)
                    xn_done[t] = n

                if t0 == 0:
                    dve.wait_ge(ld_gain, 48)
                    dve.tensor_tensor(g_att[:, :], gd[:, 0, :], gd[:, 1, :], ALU.mult).then_inc(gains_ready, 1)
                    dve.tensor_tensor(g_retr[:, :], gd[:, 0, :], gd[:, 2, :], ALU.mult).then_inc(gains_ready, 1)
                    dve.tensor_tensor(g_sq[:, :], gd[:, 0, :], gd[:, 0, :], ALU.mult).then_inc(gains_ready, 1)
                    dve.scalar_tensor_tensor(out=gqk[:, :], in0=ghd[:, 0:1], scalar=float(HD) ** -0.5, in1=ghd[:, 1:2],
                                             op0=ALU.mult, op1=ALU.mult).then_inc(gains_ready, 1)
                    dve.scalar_tensor_tensor(out=grl[:, :], in0=grd[:, 0:1], scalar=float(RD) ** -0.5, in1=grd[:, 1:2],
                                             op0=ALU.mult, op1=ALU.mult).then_inc(gains_ready, 1)
                    dve.memset(statv[:, :, 0:1], EPS / D).then_inc(gains_ready, 1)
                    dve.wait_ge(gains_ready, 6)
                    dve.tensor_scalar(statv[:, :, 1], g_sq[:, :], 1.0 / D, EPS / D, ALU.mult, ALU.add).then_inc(gains_ready, 1)
                    dve.wait_ge(mod_product, 1)
                    m = 0

                    def mod(ins):
                        nonlocal m
                        ins.then_inc(mod_steps, 1)
                        m += 1
                        dve.wait_ge(mod_steps, m)

                    mod(dve.tensor_scalar(modT[:, :, :].rearrange("p b n -> p n b"),
                                          ps[:, OB, 0:12 * B].rearrange("p (n b) -> p n b", b=B), 0.5, None, ALU.mult))
                    for n0 in (2, 8):
                        mod(dve.tensor_scalar(modT[:, :, n0:n0 + 2], modT[:, :, n0:n0 + 2], 1.0, None, ALU.add))
                    for n0 in (4, 10):
                        seg = modT[:, :, n0:n0 + 2]
                        mod(dve.tensor_scalar(gsgn[:, :, :], seg, 0.0, 2.0, ALU.is_ge, ALU.mult))
                        mod(dve.scalar_tensor_tensor(out=gabs[:, :, :], in0=gsgn[:, :, :], scalar=-1.0, in1=seg, op0=ALU.add, op1=ALU.mult))
                        mod(dve.tensor_scalar(gabs[:, :, :], gabs[:, :, :], 0.25, None, ALU.max))
                        mod(dve.scalar_tensor_tensor(out=seg, in0=gsgn[:, :, :], scalar=-1.0, in1=gabs[:, :, :], op0=ALU.add, op1=ALU.mult))
                    assert m == MOD_STEPS, m

                for b in range(t0 // NT, t1 // NT):
                    dve.wait_ge(hT_prod, b + 1)
                    for k in range(KF):
                        dve.tensor_scalar(hT[:, k, b, :], ps[:, b % 2, k * L:(k + 1) * L], modT[:, b, 2 + k:3 + k], modT[:, b, k:k + 1],
                                          ALU.mult, ALU.add).then_inc(h_ready, 1)

            dve.wait_ge(stat_prod, B)
            dve.tensor_scalar(tok[:, :, :, :], ps[:, SA, 0:B * 2 * NT].rearrange("p (b t s) -> p b s t", b=B, s=2),
                              EPS * EPS, None, ALU.add).then_inc(tok_ready, 1)
            dve.wait_ge(tok_ready, 1)
            n = 0

            def sstep(ins):
                nonlocal n
                ins.then_inc(s_steps, 1)
                n += 1
                dve.wait_ge(s_steps, n)

            sstep(dve.tensor_copy(var[:, :].rearrange("p (b t) -> p b t", t=NT), tok[:, :, 1, :]))
            sstep(dve.tensor_scalar(epsT[:, :, :], tok[:, :, 1, :], EPS, None, ALU.mult))
            rsqrt(lambda _, ins: sstep(ins), tscale[:, :, :].rearrange("p b t -> p (b t)"), var[:, :])
            dve.wait_ge(rows_prod, 1)
            dve.tensor_copy(qeps[:, :, :], ps[:, SB, 0:B * NI].rearrange("p (b i) -> p b i", i=NI)).then_inc(qeps_ready, 1)
            dve.wait_ge(pool_const, POOL_CONSTS)

            def residual():
                dve.wait_ge(ld_xT, 16)
                for b in range(B):
                    for k in range(KF):
                        dve.scalar_tensor_tensor(out=x2T[:, k, b, :], in0=hT[:, k, b, :], scalar=modT[:, b, 4 + k:5 + k],
                                                 in1=x2T[:, k, b, :], op0=ALU.mult, op1=ALU.add).then_inc(base_ready, 1)

            def retrieval_raw(b, o):
                dve.wait_ge(*pe_kv.at(b, "R", o))
                step(v_kv, b, o, "rraw", dve.tensor_copy(rraw[:, :, :], bank("R")[:, 0:NT * 2 * RD].rearrange("p (t r) -> p t r", t=NT)))
                step(v_kv, b, o, "rsq", dve.tensor_tensor(rsq[:, :, :], rraw[:, :, 0:RD], rraw[:, :, 0:RD], ALU.mult))
                step(v_kv, b, o, "rss", dve.tensor_reduce(rss[:, :], rsq[:, :, :], AX, ALU.add), wait=False)
                dve.wait_ge(*a_v.at(b, "v1", o - 1))
                step(v_kv, b, o, "stok", dve.tensor_scalar(stok[:, :], tscale[:, bass.ds(b + o, 1), :].rearrange("p o t -> p (o t)"),
                                                           1.0, None, ALU.mult))
                dve.wait_ge(*pe_retr.at(b, "lmean", o - 1))
                step(v_kv, b, o, "lmn", dve.tensor_tensor(lmn[:, :, :], rraw[:, :, RD:2 * RD], stok[:, :].unsqueeze(2).broadcast_to([P, NT, RD]), ALU.mult),
                     wait=False)

            def key_sums(b, o, t):
                dve.wait_ge(*a_kv.at(b, f"ksq{t}", o))
                step(v_kv, b, o, f"kss{t}", dve.tensor_reduce(kss[:, t, :], squares[:, :].rearrange("p (g d) -> p g d", d=HD), AX, ALU.add),
                     wait=t == 1)

            def norms(b, o):
                dve.wait_ge(*pe_retr.at(b, "lmean", o))
                step(v_kv, b, o, "lsum", dve.tensor_copy(lsum[:, :], bank("lmean")[0:C, 0:RD]))
                step(v_kv, b, o, "lsq", dve.tensor_tensor(lsq[:, :], lsum[:, :], lsum[:, :], ALU.mult))
                step(v_kv, b, o, "lss", dve.tensor_reduce(lss[:, :], lsq[:, :], AX, ALU.add))
                step(v_kv, b, o, "nvl", dve.tensor_scalar(nv[0:C, NV - 1:NV], lss[:, :], 1.0 / RD, EPS, ALU.mult, ALU.add), wait=False)
                eT = epsT[:, bass.ds(b + o, 1), :].rearrange("p o t -> p (o t)")
                nvk = nv[:, 0:NT * HKV].rearrange("p (t g) -> p t g", t=NT)
                step(v_kv, b, o, "nvk", dve.scalar_tensor_tensor(out=nvk, in0=kss[:, :, :], scalar=1.0 / HD,
                                                                 in1=eT.unsqueeze(2).broadcast_to([P, NT, HKV]), op0=ALU.mult, op1=ALU.add), wait=False)
                step(v_kv, b, o, "nvr", dve.scalar_tensor_tensor(out=nv[:, NT * HKV:NT * HKV + NT], in0=rss[:, :], scalar=1.0 / RD, in1=eT,
                                                                 op0=ALU.mult, op1=ALU.add))
                dve.wait_ge(*g_kn.at(b, "1", o - 1))
                rsqrt(lambda i, ins: step(v_kv, b, o, f"nr.{i}", ins), nr[:, :], nv[:, :])
                dve.wait_ge(*pe_retr.at(b, "qrT", o - 1))
                step(v_kv, b, o, "rqn", dve.tensor_tensor(rqn[:, :, :], rraw[:, :, 0:RD],
                                                          nr[:, NT * HKV:NT * HKV + NT].unsqueeze(2).broadcast_to([P, NT, RD]), ALU.mult), wait=False)
                step(v_kv, b, o, "lnorm", dve.tensor_scalar(lnorm[:, :], lsum[:, :], nr[0:C, NV - 1:NV], None, ALU.mult), wait=False)

            def retrieval_T(b, o):
                dve.wait_ge(*pe_retr.at(b, "qrT", o))
                dve.wait_ge(*pe_retr.at(b, "scores", o - 1))
                step(v_retr, b, o, "qrT", dve.tensor_copy(
                    qrT[:, :, :, :], bank("qrT")[0:RD, S:L].rearrange("p (i q) -> p i q", q=S).unsqueeze(2).broadcast_to([RD, NI, G, S])), wait=False)
                step(v_retr, b, o, "lmkT", dve.tensor_scalar(lmkT[:, :], bank("qrT")[0:RD, L:L + C], grl[:, 0:1], None, ALU.mult), wait=False)

            def retrieval_max(b, o):
                dve.wait_ge(*pe_retr.at(b, "scores", o))
                step(v_retr, b, o, "masked", dve.tensor_tensor(rsc[:, :, :], bank("scores")[:, 0:NI * C].rearrange("p (i c) -> p i c", c=C),
                                                               causal[:, :, :], ALU.add))
                step(v_retr, b, o, "max", dve.tensor_reduce(rmx[:, :], rsc[:, :, :], AX, ALU.max))
                step(v_retr, b, o, "sub", dve.tensor_tensor(rsc[:, :, :], rsc[:, :, :], rmx[:, :].unsqueeze(2).broadcast_to([P, NI, C]), ALU.subtract),
                     wait=False)

            def retrieval_sum(b, o):
                dve.wait_ge(*a_retr.at(b, "exp", o))
                step(v_retr, b, o, "sum", dve.tensor_reduce(rsum[:, :], rex[:, :, :], AX, ALU.add))
                step(v_retr, b, o, "rec", dve.reciprocal(rrec[:, :], rsum[:, :]), wait=False)

            def query_sums(b, o, u):
                dve.wait_ge(*pe_q.at(b, f"ss{u}", o))
                step(v_q, b, o, f"ss{u}", dve.scalar_tensor_tensor(
                    out=qvar[:, u, :], in0=bank(f"ss{u}")[:, 0:NI], scalar=1.0 / HD,
                    in1=qeps[:, bass.ds(b + o, 1), :].rearrange("p o i -> p (o i)"), op0=ALU.mult, op1=ALU.add), wait=u == HKV - 1)

            def query_norms(b, o):
                dve.wait_ge(*a_exp.at(b * HKV, "e1", (o - 1) * HKV + 3))
                rsqrt(lambda i, ins: step(v_q, b, o, f"rnq.{i}", ins), rnq[:, :, :].rearrange("p u i -> p (u i)"),
                      qvar[:, :, :].rearrange("p u i -> p (u i)"))

            def scores(b, u):
                for name, bk, p0, p1 in (("A", SA, 0, PAIRS_A), ("B", SB, PAIRS_A, NPAIR)):
                    dve.wait_ge(*pe_qk.at(b * HKV, name, u))
                    src = ps[:, bk, 0:(p1 - p0) * S].rearrange("p (n k) -> p n k", k=S)
                    step(v_sc, b * HKV, u, f"max{name}", dve.tensor_reduce(smax[:, u % 2, p0:p1], src, AX, ALU.max))
                    dve.wait_ge(*pe_pt.at(b * HKV, "2", u - 2))
                    step(v_sc, b * HKV, u, f"sub{name}", dve.tensor_tensor(
                        d_sc[:, u % 2, p0 * S:p1 * S].rearrange("p (n k) -> p n k", k=S), src,
                        smax[:, u % 2, p0:p1].unsqueeze(2).broadcast_to([P, p1 - p0, S]), ALU.subtract), wait=False)

            def weights(b, u):
                dve.wait_ge(*a_exp.at(b * HKV, "e1", u))
                step(v_w, b * HKV, u, "sum", dve.tensor_reduce(ssum[:, u % 2, :], d_sc[:, u % 2, :].rearrange("p (n k) -> p n k", k=S), AX, ALU.add))
                step(v_w, b * HKV, u, "rec", dve.reciprocal(srec[:, u % 2, :], ssum[:, u % 2, :]))
                dve.wait_ge(*g_rw.at(b, f"r{NI}", u // HKV))
                dve.wait_ge(*g_pr.at(b * HKV, "B", u - 2))
                step(v_w, b * HKV, u, "w", dve.tensor_tensor(wpair[:, u % 2, :], srec[:, u % 2, :], rw[:, :], ALU.mult), wait=False)

            def x2(b, o):
                step(v_x2, b, o, "mod", dve.tensor_scalar(mod_out[:, 0:2], modT[:, bass.ds(b + o, 1), 4:6].rearrange("p o n -> p (o n)"),
                                                          1.0, None, ALU.mult))
                dve.wait_ge(*g_keep.at(b, "x2", o - 1))
                dve.wait_ge(*pe_tail.at(b, "x", o - 1))
                step(v_x2, b, o, "copy", dve.tensor_scalar(x2cur[:, :, 0:S], x2T[:, :, bass.ds(b + o, 1), 0:S].rearrange("p k o l -> p k (o l)"),
                                                           1.0, None, ALU.mult), wait=False)
                dve.wait_ge(*pe_o.at(b * HKV, "o", o * HKV + HKV - 1))
                for k in range(KF):
                    step(v_x2, b, o, f"x{k}", dve.scalar_tensor_tensor(
                        out=x2cur[:, k, S:L], in0=ps[:, OB, k * TQ:(k + 1) * TQ], scalar=mod_out[:, k:k + 1],
                        in1=x2T[:, k, bass.ds(b + o, 1), S:L].rearrange("p o l -> p (o l)"), op0=ALU.mult, op1=ALU.add), wait=False)

            def x2_norm(b, o):
                dve.wait_ge(*pe_tail.at(b, "x", o))
                xp = bank("tx").rearrange("p (t d) -> p t d", d=D)
                for t in range(NT):
                    step(v_x2, b, o, f"bn{t}", dve.bn_stats(bn6o[:, t, :], xp[:, t, :]), wait=t == NT - 1)
                step(v_x2, b, o, "mod2", dve.tensor_scalar(mod_out[:, 2:6], modT[:, bass.ds(b + o, 1), 6:10].rearrange("p o n -> p (o n)"),
                                                           1.0, None, ALU.mult), wait=False)
                for t in range(NT):
                    step(v_x2, b, o, f"ag{t}", dve.bn_aggr(mvo[:, t, :], bn6o[:, t, :]), wait=t == NT - 1)
                step(v_x2, b, o, "var", dve.tensor_scalar(varo[:, :], mvo[:, :, 1], EPS, None, ALU.add))
                rsqrt(lambda i, ins: step(v_x2, b, o, f"rs.{i}", ins), rstdo[:, :], varo[:, :])
                dve.wait_ge(*g_keep.at(b, "lo", o - 1))
                dve.wait_ge(*pe_tail.at(b, "gate", o - 1))
                for t in range(NT):
                    step(v_x2, b, o, f"xn{t}", dve.tensor_scalar(xn2[:, t, :], xp[:, t, :], mvo[:, t, 0:1], rstdo[:, t:t + 1],
                                                                 ALU.subtract, ALU.mult), wait=False)

            def h2(b, o):
                dve.wait_ge(*pe_tail.at(b, "h", o))
                hp2 = bank("th").rearrange("p (k l) -> p k l", l=L)
                for k in range(KF):
                    step(v_x2, b, o, f"h{k}", dve.tensor_scalar(h2cur[:, k, :], hp2[:, k, :], mod_out[:, 4 + k:5 + k], mod_out[:, 2 + k:3 + k],
                                                                ALU.mult, ALU.add), wait=k == KF - 1)
                step(v_x2, b, o, "hi", dve.tensor_scalar(f_x_hi[:, :, bass.ds(b + o, 1), :].rearrange("p k o l -> p k (o l)"), h2cur,
                                                         1.0, None, ALU.mult), wait=False)

            def gate(b, o):
                def bc(a):
                    return a[:, :].unsqueeze(2).broadcast_to([P, NT, E])

                def g(name, ins, wait=True):
                    step(v_gate, b, o, name, ins, wait)

                dve.wait_ge(*a_gate.at(b, "tanh", o))
                g("sc", dve.tensor_scalar(gsc[:, :, :], gth[:, :, :], 0.5, 0.5, ALU.mult, ALU.add))
                for n, (score, gm, gx, gs) in enumerate(((gsc, gm1, gx1, gs1), (gsc2, gm2, gx2, gs2)), 1):
                    if n == 2:
                        g("sc2", dve.scalar_tensor_tensor(out=gsc2[:, :, :], in0=gs1[:, :, :], scalar=-4.0, in1=gsc[:, :, :],
                                                          op0=ALU.mult, op1=ALU.add))
                    g(f"m{n}", dve.tensor_reduce(gm[:, :], score[:, :, :], AX, ALU.max))
                    g(f"e{n}", dve.tensor_tensor(gk1[:, :, :], score[:, :, :], bc(gm), ALU.is_equal))
                    g(f"k{n}", dve.tensor_tensor(gk2[:, :, :], gk1[:, :, :], rank[:, :, :], ALU.mult))
                    g(f"x{n}", dve.tensor_reduce(gx[:, :], gk2[:, :, :], AX, ALU.max))
                    g(f"s{n}", dve.tensor_tensor(gs[:, :, :], gk2[:, :, :], bc(gx), ALU.is_equal))
                g("den", dve.scalar_tensor_tensor(out=gden[:, :], in0=gm1[:, :], scalar=1e-20, in1=gm2[:, :], op0=ALU.add, op1=ALU.add))
                g("rec", dve.reciprocal(grec[:, :], gden[:, :]), wait=False)
                g("sel", dve.tensor_tensor(gs1[:, :, :], gs1[:, :, :], gs2[:, :, :], ALU.add))
                g("num", dve.tensor_tensor(gsc2[:, :, :], gsc[:, :, :], gs1[:, :, :], ALU.mult))
                g("c", dve.scalar_tensor_tensor(out=cfull[:, :, 0:E], in0=gsc2[:, :, :], scalar=0.5 * ROUTED, in1=bc(grec), op0=ALU.mult, op1=ALU.mult))
                g("hi", dve.tensor_copy(c_hi[:, :, :], cfull[:, :, :]))
                dve.wait_ge(*pe_tail.at(b, "cT", o - 1))
                g("pad", dve.tensor_copy(cpad[:, :, 0:E + 1], c_hi[:, :, :].bitcast(F32)), wait=False)
                g("lo", dve.tensor_tensor(cpad[:, :, 32:32 + E + 1], cfull[:, :, :], c_hi[:, :, :].bitcast(F32), ALU.subtract), wait=False)

            def gate_T(b, o):
                dve.wait_ge(*pe_tail.at(b, "cT", o))
                step(v_gate, b, o, "cT", dve.tensor_scalar(cw[:, bass.ds(b + o, 1), :].rearrange("p o l -> p (o l)"), bank("tc")[0:64, 0:L],
                                                           1.0, None, ALU.mult), wait=False)

            def iteration(b, head, tail_):
                if tail_:
                    x2(b, -1)
                scores(b, 1)
                if tail_:
                    x2_norm(b, -1)
                weights(b, 1)
                if head:
                    retrieval_raw(b, 1)
                    for t in range(NT):
                        key_sums(b, 1, t)
                if tail_:
                    h2(b, -1)
                scores(b, 2)
                if head:
                    norms(b, 1)
                weights(b, 2)
                if tail_:
                    gate(b, -1)
                if head:
                    query_sums(b, 1, 0)
                scores(b, 3)
                if head:
                    retrieval_T(b, 1)
                weights(b, 3)
                if head:
                    query_sums(b, 1, 1)
                    retrieval_max(b, 1)
                    query_sums(b, 1, 2)
                    retrieval_sum(b, 1)
                if tail_:
                    gate_T(b, -1)
                if head:
                    query_sums(b, 1, 3)
                    query_norms(b, 1)
                    scores(b, 4)
                    weights(b, 4)

            def w_low(j, o, i):
                dve.wait_ge(*f_whi.at(j, "w", o))
                dve.tensor_tensor(w_lo[:, i, :, :], w_raw[:, i, 0:NW - 1, :], w_hi[:, i, 0:NW - 1, :].bitcast(F32), ALU.subtract)\
                   .then_inc(*f_wlo.does("w"))

            retrieval_raw(0, 0)
            for t in range(NT):
                key_sums(0, 0, t)
            norms(0, 0)
            query_sums(0, 0, 0)
            retrieval_T(0, 0)
            query_sums(0, 0, 1)
            retrieval_max(0, 0)
            query_sums(0, 0, 2)
            retrieval_sum(0, 0)
            query_sums(0, 0, 3)
            query_norms(0, 0)
            scores(0, 0)
            weights(0, 0)
            iteration(0, True, False)
            residual()
            with dve.Fori(1, B - 1) as b:
                iteration(b, True, True)
            for j in range(2):
                w_low(j, 0, j)
            iteration(B - 1, False, True)
            x2(B - 1, 0)
            x2_norm(B - 1, 0)
            h2(B - 1, 0)
            gate(B - 1, 0)
            gate_T(B - 1, 0)

            def gated(t, o, i, first=False):
                dve.wait_ge(*f_act.at(t, "th", o))
                step(f_dve, t, o, "a", dve.scalar_tensor_tensor(out=f_a[:, i, :], in0=f_th[:, i, :], scalar=1.0, in1=ps[:, 2, :],
                                                                op0=ALU.add, op1=ALU.mult))
                dve.wait_ge(*f_pe_h.at(t, "u", o))
                step(f_dve, t, o, "b", dve.tensor_tensor(f_a[:, i, :], f_a[:, i, :], ps[:, 3, :], ALU.mult))
                dve.wait_ge(*f_pe_h.at(t, "c", o))
                if not first:
                    dve.wait_ge(*f_glo.at(t, "lo", o - 2))
                    dve.wait_ge(*f_ghi.at(t, "hi", o - 2))
                step(f_dve, t, o, "g", dve.tensor_tensor(f_g[:, i, :], f_a[:, i, :], ps[:, 0, :], ALU.mult), wait=False)

            gated(0, 0, 0, True)
            gated(0, 1, 1, True)
            with dve.Fori(0, (NJ - 1) // 2) as n:
                gated(n * 4, 2, 0)
                w_low(n * 2, 2, 0)
                gated(n * 4, 3, 1)
                gated(n * 4, 4, 0)
                w_low(n * 2, 3, 1)
                gated(n * 4, 5, 1)
            for n in range(KF * 2):
                k, half = n % 2, n // 2
                dve.wait_ge(*f_pe_y.at(2 * NJ - 2 + half, "y"))
                for b in (2 * half, 2 * half + 1):
                    dve.scalar_tensor_tensor(out=f_out[:, k, b, :], in0=ps[:, 4 + n, (b % 2) * L:(b % 2 + 1) * L],
                                             scalar=modT[:, b, 10 + k:11 + k], in1=x2T[:, k, b, :], op0=ALU.mult, op1=ALU.add)\
                       .then_inc(f_fin, 1)

        @block.tensor
        def _(pe):
            for st in (pe_kv, pe_v, pe_kT, pe_retr, pe_q, pe_tail, pe_qk, pe_pt, pe_pv, pe_o, f_pe_h, f_pe_y):
                st.start(pe)

            def product(out_, pairs, start=True, stop=True):
                for n, (w, m) in enumerate(pairs):
                    ins = pe.matmul(out_, w, m, start=start and n == 0, stop=stop and n == len(pairs) - 1,
                                    skip_group_check=True)
                return ins

            def split(w_hi_, w_lo_, m_hi, m_lo):
                return [(w_hi_, m_hi), (w_hi_, m_lo), (w_lo_, m_hi)]

            last = {}

            def take(name, b, o):
                bk = ring_bank(name)
                if bk in last:
                    st, b0, step_, o0 = last[bk]
                    pe.wait_ge(*st.at(b0, step_, o0))
                _, st, step_ = ring[ring_names.index(name)]
                last[bk] = (st, b, step_, o)
                return ps[:, bk, :]

            pe.wait_ge(ld_mod, 16)
            pe.wait_ge(silu_steps, 2)
            for n in range(12):
                ins = product(ps[:, OB, n * B:(n + 1) * B], [(wmod_sb[:, k, n * P:(n + 1) * P], silu_c[:, k, :]) for k in range(KF)])
            ins.then_inc(mod_product, 1)
            pe.wait_ge(pool_const, POOL_CONSTS)
            for b in range(B + 1):
                if b < B:
                    pe.wait_ge(xn_steps, xn_done[b * NT + NT - 1])
                    if b > 1:
                        pe.wait_ge(h_ready, KF * (b - 1))
                    for k in range(KF):
                        for t in range(NT):
                            ins = pe.transpose(ps[:, b % 2, k * L + t * P:k * L + (t + 1) * P], xn[:, b * NT + t, k * P:(k + 1) * P], ident[:, :])
                    ins.then_inc(hT_prod, 1)
                if b > 0:
                    pe.wait_ge(hsq_ready, b)
                    pe.wait_ge(gains_ready, GAINS)
                    for t in range(NT):
                        ins = product(ps[:, SA, ((b - 1) * NT + t) * 2:((b - 1) * NT + t + 1) * 2],
                                      [(squares[:, k * L + t * P:k * L + (t + 1) * P], statv[:, k, :]) for k in range(KF)])
                    ins.then_inc(stat_prod, 1)
            pe.wait_ge(tok_ready, 1)
            for b in range(B):
                for i in range(1, C):
                    ins = product(ps[:, SB, b * NI + i - 1:b * NI + i], [(pick[:, i % 4, :], tok[:, b, 0, i // 4:i // 4 + 1])])
            ins.then_inc(rows_prod, 1)

            def project_kv(name, b, o, t, n0):
                bk = take(name, b, o)
                product(bk, [(hcur[:, k, t * P:(t + 1) * P], w_kv[:, k, n0:n0 + KVW]) for k in range(KF)])\
                    .then_inc(*(pe_kv if name[0] == "K" else pe_v).does(name))

            def retrieval(b, o):
                bk = take("R", b, o)
                pe.wait_ge(*g_h.at(b, "h", o))
                for t in range(NT):
                    ins = product(bk[:, t * 2 * RD:(t + 1) * 2 * RD], [(hcur[:, k, t * P:(t + 1) * P], w_kv[:, k, 2 * KVW:]) for k in range(KF)])
                ins.then_inc(*pe_kv.does("R"))

            def chunk_means(b, o):
                bk = take("lmean", b, o)
                pe.wait_ge(*v_kv.at(b, "lmn", o))
                product(bk[0:C, 0:RD], [(chunk_mean[:, t, :], lmn[:, t, :]) for t in range(NT)]).then_inc(*pe_retr.does("lmean"))

            def queries(b, o, u, m):
                bk = take(f"q{'ab'[m]}{u}", b, o)
                for hh in range(2):
                    h = u * G + 2 * m + hh
                    ins = product(bk[:, hh * TQ:(hh + 1) * TQ], [(w_q[:, k, h * HD:(h + 1) * HD], hcur[:, k, S:L]) for k in range(KF)])
                ins.then_inc(*pe_q.does(f"q{'ab'[m]}{u}"))

            def query_sums(b, o, u):
                bk = take(f"ss{u}", b, o)
                pe.wait_ge(*a_q.at(b, f"sqb{u}", o))
                for i in range(NI):
                    ins = product(bk[:, i:i + 1], [(q_sq[:, u % 2, i, :, :].rearrange("p h q -> p (h q)"), ones[:, :])])
                ins.then_inc(*pe_q.does(f"ss{u}"))

            def retrieval_T(b, o):
                bk = take("qrT", b, o)
                pe.wait_ge(*v_kv.at(b, "lnorm", o))
                for t in range(NT):
                    product(bk[0:RD, t * P:(t + 1) * P], [(rqn[:, t, :], ident[:, :])])
                product(bk[0:RD, L:L + C], [(lnorm[:, :], ident[0:C, 0:C])]).then_inc(*pe_retr.does("qrT"))

            def retrieval_scores(b, o):
                bk = take("scores", b, o)
                pe.wait_ge(*v_retr.at(b, "lmkT", o))
                for i in range(NI):
                    ins = product(bk[:, i * C:(i + 1) * C], [(qrT[:, i, :, :].rearrange("p h q -> p (h q)"), lmkT[:, :])])
                ins.then_inc(*pe_retr.does("scores"))

            def keys_T(b, o):
                for n, name in enumerate("ab"):
                    bk = take(f"kT{name}", b, o)
                    pe.wait_ge(*g_kn.at(b, "1", o))
                    for g in range(2):
                        for t, rows in ((0, P), (1, TQ - P)):
                            ins = pe.transpose(bk[:, g * L + t * P:g * L + t * P + rows],
                                               kraw[0:rows, t, (2 * n + g) * HD:(2 * n + g + 1) * HD], ident[0:rows, 0:rows])
                    ins.then_inc(*pe_kT.does(f"kT{name}"))

            def scores(b, u):
                o = u // HKV
                pe.wait_ge(*a_q.at(b, f"qb{u % HKV}", o))
                pe.wait_ge(*a_kT.at(b, "b", o))
                for name, bk, blocks in (("A", SA, BANK_A), ("B", SB, BANK_B)):
                    pe.wait_ge(*v_sc.at(b * HKV, f"sub{name}", u - 1))
                    for i in blocks:
                        c0 = (PAIR0[i] - PAIR0[blocks[0]]) * S
                        ins = product(ps[:, bk, c0:c0 + i * S], [(qT[:, u % HKV, i - 1, :, :].rearrange("p h q -> p (h q)"), kT[:, u % HKV, 0:i * S])])
                    ins.then_inc(*pe_qk.does(name))

            def transposes(b, u):
                pe.wait_ge(*g_pr.at(b * HKV, "B", u))
                for n, (bk, blocks, k0, (st, last_)) in enumerate((
                        (R0, range(4, 8), 0, (a_ao, "0")), (R2, range(5, 8), P, (a_pt, "1")), (R1, range(1, 4), 0, (a_ao, "1")))):
                    pe.wait_ge(*st.at(b * HKV, last_, u - 1))
                    for m, i in enumerate(blocks):
                        rows = min(P, i * S - k0)
                        c0 = PAIR0[i] * S + k0
                        ins = pe.transpose(ps[0:rows, bk, m * P:(m + 1) * P], d_sc[:, u % 2, c0:c0 + rows], ident[:, :])
                    ins.then_inc(*pe_pt.does(str(n)))

            def values(b, u):
                d = slice(u * HD, (u + 1) * HD)
                pe.wait_ge(*a_v.at(b, "v1"))
                pe.wait_ge(*a_pt.at(b * HKV, "2", u))
                product(ps[:, R0, :], [(v_sb[:, 0, d], pt[:, 3:7, :].rearrange("p c r -> p (c r)"))], stop=False)
                for m in range(3):
                    r = (m + 1) * S
                    ins = product(ps[:, R0, (m + 1) * P:(m + 2) * P], [(v_sb[0:r, 1, d], pt[0:r, 7 + m, :])], start=False)
                ins.then_inc(*pe_pv.does("0"))
                for m in range(3):
                    r = (m + 1) * S
                    ins = product(ps[:, R1, m * P:(m + 1) * P], [(v_sb[0:r, 0, d], pt[0:r, m, :])])
                ins.then_inc(*pe_pv.does("1"))

            def project(b, u):
                pe.wait_ge(*a_ao.at(b * HKV, "1", u))
                if u == 0:
                    pe.wait_ge(*v_x2.at(b, "x1", -1))
                for hh in range(G):
                    h = u * G + hh
                    for f in range(KF):
                        ins = product(ps[:, OB, f * TQ:(f + 1) * TQ], [(w_o[:, h, f * P:(f + 1) * P], ao[:, u % 2, :, hh, :])],
                                      start=(u == 0 and hh == 0 and f == 0), stop=(u == HKV - 1 and hh == G - 1))
                ins.then_inc(*pe_o.does("o"))

            def tail_x(b, o):
                bk = take("tx", b, o)
                pe.wait_ge(*v_x2.at(b, "x1", o))
                for t in range(NT):
                    for k in range(KF):
                        ins = pe.transpose(bk[:, t * D + k * P:t * D + (k + 1) * P], x2cur[:, k, t * P:(t + 1) * P], ident[:, :])
                ins.then_inc(*pe_tail.does("x"))

            def tail_h(b, o):
                bk = take("th", b, o)
                pe.wait_ge(*v_x2.at(b, "xn1", o))
                for k in range(KF):
                    for t in range(NT):
                        ins = pe.transpose(bk[:, k * L + t * P:k * L + (t + 1) * P], xn2[:, t, k * P:(k + 1) * P], ident[:, :])
                ins.then_inc(*pe_tail.does("h"))

            def tail_gate(b, o):
                bk = take("tg", b, o)
                pe.wait_ge(*v_x2.at(b, "h1", o))
                for t in range(NT):
                    ins = product(bk[:, t * E:(t + 1) * E], [(h2cur[:, k, t * P:(t + 1) * P], gate_sb[:, k, :]) for k in range(KF)])
                ins.then_inc(*pe_tail.does("gate"))

            def tail_c(b, o):
                bk = take("tc", b, o)
                pe.wait_ge(*v_gate.at(b, "lo", o))
                for t in range(NT):
                    ins = product(bk[0:64, t * P:(t + 1) * P], [(cpad[:, t, :], ident[:, :])])
                ins.then_inc(*pe_tail.does("cT"))

            def iteration(b, head, tail_):
                scores(b, 1)
                transposes(b, 0)
                if tail_:
                    tail_x(b, -1)
                if head:
                    retrieval(b, 1)
                    project_kv("K0", b, 1, 0, 0)
                values(b, 0)
                if head:
                    project_kv("K1", b, 1, 1, 0)
                if tail_:
                    tail_h(b, -1)
                scores(b, 2)
                transposes(b, 1)
                project(b, 0)
                values(b, 1)
                if head:
                    chunk_means(b, 1)
                if tail_:
                    tail_gate(b, -1)
                if head:
                    queries(b, 1, 0, 0)
                    queries(b, 1, 0, 1)
                    queries(b, 1, 1, 0)
                    query_sums(b, 1, 0)
                    queries(b, 1, 1, 1)
                    retrieval_T(b, 1)
                scores(b, 3)
                transposes(b, 2)
                project(b, 1)
                values(b, 2)
                if head:
                    keys_T(b, 1)
                    query_sums(b, 1, 1)
                    queries(b, 1, 2, 0)
                    queries(b, 1, 2, 1)
                    retrieval_scores(b, 1)
                    queries(b, 1, 3, 0)
                    query_sums(b, 1, 2)
                    queries(b, 1, 3, 1)
                if tail_:
                    tail_c(b, -1)
                if head:
                    query_sums(b, 1, 3)
                    scores(b, 4)
                transposes(b, 3)
                project(b, 2)
                values(b, 3)
                if head:
                    project_kv("V0", b, 1, 0, KVW)
                    project_kv("V1", b, 1, 1, KVW)
                project(b, 3)

            pe.wait_ge(w_scaled, SCALED - KF)
            pe.wait_ge(h_ready, KF * B)
            pe.wait_ge(stat_prod, B)
            retrieval(0, 0)
            project_kv("K0", 0, 0, 0, 0)
            project_kv("K1", 0, 0, 1, 0)
            chunk_means(0, 0)
            pe.wait_ge(w_scaled, SCALED)
            queries(0, 0, 0, 0)
            queries(0, 0, 0, 1)
            queries(0, 0, 1, 0)
            query_sums(0, 0, 0)
            queries(0, 0, 1, 1)
            retrieval_T(0, 0)
            keys_T(0, 0)
            query_sums(0, 0, 1)
            queries(0, 0, 2, 0)
            queries(0, 0, 2, 1)
            retrieval_scores(0, 0)
            queries(0, 0, 3, 0)
            query_sums(0, 0, 2)
            queries(0, 0, 3, 1)
            query_sums(0, 0, 3)
            pe.wait_ge(qeps_ready, 1)
            scores(0, 0)
            project_kv("V0", 0, 0, 0, KVW)
            project_kv("V1", 0, 0, 1, KVW)
            pe.wait_ge(bank_init, 2)
            pe.wait_ge(mod_steps, 1)
            pe.wait_ge(ld_o, 16)
            pe.wait_ge(ld_gate, 16)
            iteration(0, True, False)
            for name in ("V0", "V1"):
                assert ring[ring_names.index(name)][1:] == (last[ring_bank(name)][0], last[ring_bank(name)][2])
            with pe.Fori(1, B - 1) as b:
                for bk in last:
                    last[bk] = (last[bk][0], b, last[bk][2], 0)
                iteration(b, True, True)
            for bk in last:
                last[bk] = (last[bk][0], B - 1, last[bk][2], 0)
            iteration(B - 1, False, True)
            tail_x(B - 1, 0)
            tail_h(B - 1, 0)
            tail_gate(B - 1, 0)
            tail_c(B - 1, 0)

            def hidden(j, t, o, half, i):
                pe.wait_ge(*f_whi.at(j, "w"))
                pe.wait_ge(*f_wlo.at(j, "w"))
                xh, xl = (a[:, :, 2 * half:2 * half + 2, :].rearrange("p k b l -> p k (b l)") for a in (f_x_hi, f_x_lo))
                for name, bk, w0, step_ in (("h", 2, 0, "a"), ("u", 3, 2, "b")):
                    pe.wait_ge(*f_dve.at(t, step_, o - 1))
                    product(ps[:, bk, :], [x_ for k in range(KF) for x_ in split(
                        w_hi[:, i, w0 + k, :], w_lo[:, i, w0 + k, :], xh[:, k, :], xl[:, k, :])]).then_inc(*f_pe_h.does(name))
                pe.wait_ge(*f_dve.at(t, "g", o - 1))
                product(ps[:, 0, :], [(w_hi[0:64, i, 6, :], cw[:, 2 * half:2 * half + 2, :].rearrange("p b l -> p (b l)"))])\
                    .then_inc(*f_pe_h.does("c"))

            def down(t, o, half, i, first=False):
                pe.wait_ge(*f_ghi.at(t, "hi", o))
                pe.wait_ge(*f_glo.at(t, "lo", o))
                for f in range(KF):
                    ins = product(ps[:, 4 + 2 * half + f, :], split(w_hi[:, i, 4 + f, :], w_lo[:, i, 4 + f, :],
                                                                    f_g_hi[:, half, :], f_g_lo[:, half, :]), start=first)
                ins.then_inc(*f_pe_y.does("y"))

            pe.wait_ge(*g_keep.at(B - 1, "lo"))
            pe.wait_ge(*v_gate.at(B - 1, "cT"))
            hidden(0, 0, 0, 0, 0)
            hidden(0, 0, 1, 1, 0)
            down(0, 0, 0, 0, True)
            hidden(1, 0, 2, 0, 1)
            down(0, 1, 1, 0, True)
            hidden(1, 0, 3, 1, 1)
            down(0, 2, 0, 1)
            with pe.Fori(1, (NJ - 1) // 2) as n:
                hidden(n * 2, n * 4, 0, 0, 0)
                down(n * 4, -1, 1, 1)
                hidden(n * 2, n * 4, 1, 1, 0)
                down(n * 4, 0, 0, 0)
                hidden(n * 2 + 1, n * 4, 2, 0, 1)
                down(n * 4, 1, 1, 0)
                hidden(n * 2 + 1, n * 4, 3, 1, 1)
                down(n * 4, 2, 0, 1)
            hidden(NJ - 1, 2 * NJ - 2, 0, 0, 0)
            down(2 * NJ - 3, 0, 1, 1)
            hidden(NJ - 1, 2 * NJ - 1, 0, 1, 0)
            down(2 * NJ - 2, 0, 0, 0)
            down(2 * NJ - 1, 0, 1, 0)


def W_PARTS(g_att, g_retr):
    return (0, 2 * KVW, g_att), (2 * KVW, 2 * KVW + RD, g_retr), (2 * KVW + RD, NKV, g_att)


def kernel(**inputs):
    import numpy as np
    import concourse.bacc as bacc
    from concourse.bass_utils import run_bass_kernel_spmd

    g = {k.removeprefix("L0_").removeprefix("attn_").removeprefix("ffn_"): np.asarray(v) for k, v in inputs.items()}
    t = np.ascontiguousarray
    x = g["hidden_states"]
    pad = NJP * P - NHID

    def hidden_tiles(routed, shared):
        w = np.concatenate([routed.transpose(1, 0, 2).reshape(D, E * HE), shared], axis=1)
        w = np.pad(w, ((0, 0), (0, pad)))
        return w.reshape(KF, P, NJP, P).transpose(2, 1, 0, 3)

    w2 = np.pad(np.concatenate([g["w2"].reshape(E * HE, D), g["sw2"]], axis=0), ((0, pad), (0, 0))).reshape(NJP, P, KF, P)
    member = np.zeros((P, NJP * P), np.float32)
    for e in range(E + 1):
        member[e, e * HE:(e + 1) * HE] = 1.0
        member[32 + e, e * HE:(e + 1) * HE] = 1.0
    member = member.reshape(P, NJP, 1, P).transpose(1, 0, 2, 3)
    arrays = {
        "x": t(x),
        "xT": t(x.transpose(2, 0, 1)),
        "wq": t(g["w_q"].T), "wk": t(g["w_k"].T), "wv": t(g["w_v"].T),
        "wr": t(g["w_q_retr"].T), "wl": t(g["w_lmk"].T), "wo": t(g["w_o"].T),
        "gains_d": t(np.stack([g["g_pre"], g["g_chunk_norm"], g["g_pre_retr"]]).reshape(3, KF, P).transpose(2, 0, 1)),
        "gains_hd": t(np.stack([g["g_k_norm"], g["g_q_norm"]], axis=1)),
        "gains_rd": t(np.stack([g["g_q_retr"], g["g_lmk"]], axis=1)),
        "gateT": t(g["gate_w"].T), "cT": t(g["c"].T), "wmod": t(g["wmod"]),
        "wffn": t(np.concatenate([hidden_tiles(g["w1"], g["sw1"]), hidden_tiles(g["w3"], g["sw3"]), w2, member], axis=2)),
    }
    nc = bacc.Bacc("TRN2", target_bir_lowering=False, num_devices=1)
    handles = [nc.dram_tensor(k, a.shape, mybir.dt.from_np(a.dtype), kind="ExternalInput").ap() for k, a in arrays.items()]
    out = nc.dram_tensor("out", (D, B, L), F32, kind="ExternalOutput").ap()
    build(nc, *handles, out)
    r = run_bass_kernel_spmd(nc, [arrays], core_ids=[0])
    return np.ascontiguousarray(r.results[0]["out"].transpose(1, 2, 0))
```

```python
from contextlib import ExitStack

import concourse.bass as bass
from concourse import mybir

F32 = mybir.dt.float32
F32R = mybir.dt.float32r
I32 = mybir.dt.int32
ALU = mybir.AluOpType
ACT = mybir.ActivationFunctionType
AX = mybir.AxisListType.X

P = 128
B = 4
L = 256
D = 256
KF = D // P
NT = L // P
H = 16
HKV = 4
G = H // HKV
HD = 128
S = 32
C = L // S
RD = 32
NI = C - 1
TQ = NI * S
EPS = 1e-5
E = 8
HE = 176
NHID = (E + 1) * HE
NJ = (NHID + P - 1) // P
NJP = NJ + 1
POOL_CONSTS = 29
GAINS = 7
MOD_A_STEPS, MOD_STEPS = 2, 12
WARM = 30
BUSY = 64
KEEP_WARM = 8, 14, 8
S_STEPS = 15
NV = NT * HKV + NT + 1
ROUTED = 2.5
KVW = HKV * HD
NKV = 2 * KVW + 2 * RD
HALF = 512
RSQRT_MAGIC = float(0x5F3759DF)

BANK_A = (7, 6, 3)
BANK_B = (5, 4, 2, 1)
PAIR0 = {}
NPAIR = 0
for _i in BANK_A + BANK_B:
    PAIR0[_i] = NPAIR
    NPAIR += _i
PAIRS_A = sum(BANK_A)
COLS = NPAIR * S


class Steps:

    def __init__(self, nc_sem, names, credit):
        self.sem, self.names, self.credit, self.at_name = nc_sem, names, credit, 0

    def does(self, name):
        assert self.names[self.at_name] == name, (self.names[self.at_name], name)
        self.at_name = (self.at_name + 1) % len(self.names)
        return self.sem, 1

    def at(self, unit, name, off=0):
        return self.sem, unit * len(self.names) + ((off + self.credit) * len(self.names) + self.names.index(name) + 1)

    def start(self, eng):
        eng.sem_inc(self.sem, self.credit * len(self.names))


def newton(name):
    return [f"{name}.{n}" for n in range(11)]


def build(nc, x, xT, wq, wk, wv, wr, wl, wo, gains_d, gains_hd, gains_rd, gateT, cT, wmod, wffn, out):
    with ExitStack() as top:
        def sem(name):
            return top.enter_context(nc.semaphore(name))

        def sb(name, shape, dt=F32, ctx=top):
            return ctx.enter_context(nc.sbuf_tensor(name, shape, dt))

        ps = top.enter_context(nc.psum_tensor("banks", [P, 8, 512], F32))
        SA, SB = 2, 3
        R0, R1, R2 = 4, 5, 6
        OB = 7

        ident = sb("ident", [P, P])
        ones = sb("ones", [P, 1])
        pick = sb("pick", [P, 4, P])
        chunk_mean = sb("chunk_mean", [P, NT, C])
        rank = sb("rank", [P, NT, E])
        causal = sb("causal", [P, NI, C])
        w_q, w_kv, w_o = sb("w_q", [P, KF, H * HD]), sb("w_kv", [P, KF, NKV]), sb("w_o", [P, H, D])
        gd = sb("gd", [P, 3, KF])
        ghd = sb("ghd", [P, 2])
        grd = sb("grd", [RD, 2])
        g_att, g_retr, g_sq = (sb(n, [P, KF]) for n in ("g_att", "g_retr", "g_sq"))
        statv = sb("statv", [P, KF, 2])
        gqk, grl = sb("gqk", [P, 1]), sb("grl", [RD, 1])
        gate_sb = sb("gate_sb", [P, KF, E])
        cT_sb, silu_c = sb("cT_sb", [P, KF, B]), sb("silu_c", [P, KF, B])
        gsgn, gabs = sb("gsgn", [P, B, 2]), sb("gabs", [P, B, 2])
        modT = sb("modT", [P, B, 12])
        x2T = sb("x2T", [P, KF, B, L])
        xn = sb("xn", [P, B * NT, D])
        hT = sb("hT", [P, KF, B, L])
        with ExitStack() as early:
            h_sq = sb("h_sq", [P, KF, B, L], F32, early)
        f_x_hi, f_x_lo = sb("f_x_hi", [P, KF, B, L], F32R), sb("f_x_lo", [P, KF, B, L], F32R)
        cw = sb("cw", [64, B, L], F32R)
        bn6, mv = sb("bn6", [P, B * NT, 6]), sb("mv", [P, B * NT, 2])
        var, rstd = sb("var", [P, B * NT]), sb("rstd", [P, B * NT])
        tok = sb("tok", [P, B, 2, NT])
        tscale, epsT, qeps = sb("tscale", [P, B, NT]), sb("epsT", [P, B, NT]), sb("qeps", [P, B, C])
        hcur, squares = sb("hcur", [P, KF, L]), sb("squares", [P, KF * L])
        stok = sb("stok", [P, NT])
        kraw = sb("kraw", [P, NT, KVW])
        kss, rss = sb("kss", [P, NT, HKV]), sb("rss", [P, NT])
        nv, nr = sb("nv", [P, NV]), sb("nr", [P, NV])
        rraw, rsq = sb("rraw", [P, NT, 2 * RD]), sb("rsq", [P, NT, RD])
        rqn, lmn = sb("rqn", [P, NT, RD]), sb("lmn", [P, NT, RD])
        lsum, lsq, lnorm, lss = sb("lsum", [C, RD]), sb("lsq", [C, RD]), sb("lnorm", [C, RD]), sb("lss", [C, 1])
        lmkT, qrT = sb("lmkT", [RD, C]), sb("qrT", [RD, NI, G, S])
        rsc, rex = sb("rsc", [P, NI, C]), sb("rex", [P, NI, C])
        rmx, rsum, rrec = sb("rmx", [P, NI]), sb("rsum", [P, NI]), sb("rrec", [P, NI])
        rw = sb("rw", [P, NPAIR])
        v_sb, kT = sb("v_sb", [P, NT, KVW]), sb("kT", [P, HKV, TQ])
        qT = sb("qT", [P, HKV, NI, G, S])
        q_sq = sb("q_sq", [P, 2, NI, G, S])
        qvar, rnq = sb("qvar", [P, HKV, NI]), sb("rnq", [P, HKV, NI])
        nw1, nw2 = sb("nw1", [P, HKV * NI]), sb("nw2", [P, HKV * NI])
        x2cur, tail = sb("x2cur", [P, KF, L]), sb("tail", [P, KF * L])
        xn2, h2cur = (tail[:, :].rearrange("p (a b) -> p a b", a=2) for _ in range(2))
        mod_out = sb("mod_out", [P, 6])
        bn6o, mvo, varo, rstdo = sb("bn6o", [P, NT, 6]), sb("mvo", [P, NT, 2]), sb("varo", [P, NT]), sb("rstdo", [P, NT])
        gth, gsc, gk1, gk2, gs1, gs2, gsc2 = (sb(n, [P, NT, E]) for n in ("gth", "gsc", "gk1", "gk2", "gs1", "gs2", "gsc2"))
        gm1, gm2, gx1, gx2, gden, grec = (sb(n, [P, NT]) for n in ("gm1", "gm2", "gx1", "gx2", "gden", "grec"))
        cfull, c_hi = sb("cfull", [P, NT, E + 1]), sb("c_hi", [P, NT, E + 1], F32R)
        cpad = sb("cpad", [P, NT, 64])
        smax, ssum, srec, wpair = (sb(n, [P, 2, NPAIR]) for n in ("smax", "ssum", "srec", "wpair"))
        d_sc = sb("d_sc", [P, 2, COLS])
        pt = sb("pt", [P, 10, P])
        ao = sb("ao", [P, 2, NI, G, S])
        NW = 7
        w_raw = sb("w_raw", [P, 2, NW, P])
        w_hi, w_lo = sb("w_hi", [P, 3, NW, P], F32R), sb("w_lo", [P, 3, NW - 1, P], F32R)
        f_g_hi, f_g_lo = sb("f_g_hi", [P, 2, HALF], F32R), sb("f_g_lo", [P, 2, HALF], F32R)
        with ExitStack() as early:
            wmod_sb = sb("wmod_sb", [P, KF, 6 * D], F32, early)
        f_th, f_a, f_g = (sb(n, [P, 2, HALF]) for n in ("f_th", "f_a", "f_g"))
        f_out = xn[:, :, :].rearrange("p (k b) d -> p k b d", k=KF)

        ld_x0, ld_x, ld_xT, ld_gain, ld_c, ld_mod_a, ld_mod_b, ld_k, ld_v, ld_q0, ld_q1, ld_o, ld_gate = (
            sem(n) for n in ("ld_x0", "ld_x", "ld_xT", "ld_gain", "ld_c", "ld_mod_a", "ld_mod_b", "ld_k", "ld_v", "ld_q0", "ld_q1", "ld_o",
                             "ld_gate"))
        ld_w = [sem("ld_w0"), sem("ld_w1")]
        st_out = sem("st_out")
        pool_const, gains_ready, silu_steps, mod_product, mod_steps, bank_init, xn_steps = (
            sem(n) for n in ("pool_const", "gains_ready", "silu_steps", "mod_product", "mod_steps", "bank_init", "xn_steps"))
        wk_scaled, wv_scaled, wq_scaled_a, wq_scaled_v = (sem(n) for n in ("wk_scaled", "wv_scaled", "wq_scaled_a", "wq_scaled_v"))
        hT_prod, h_ready, h0_taken, hsq_ready, base_ready, stat_prod, rows_prod, s_steps = (
            sem(n) for n in ("hT_prod", "h_ready", "h0_taken", "hsq_ready", "base_ready", "stat_prod", "rows_prod", "s_steps"))

        def steps(name, names, credit=1):
            return Steps(sem(name), names, credit)

        pe_kv = steps("pe_kv", ["R", "K0", "K1"])
        pe_v = steps("pe_v", ["V0", "V1"])
        pe_kT = steps("pe_kT", ["kTa", "kTb"])
        pe_retr = steps("pe_retr", ["lmean", "qrT", "scores"])
        pe_q = steps("pe_q", ["qa0", "qb0", "qa1", "ss0", "qb1", "ss1", "qa2", "qb2", "qa3", "ss2", "qb3", "ss3"])
        pe_tail = steps("pe_tail", ["x", "h", "gate", "cT"])
        v_kv = steps("v_kv", ["rraw", "rsq", "rss", "stok", "lmn", "kss0", "kss1", "lsum", "lsq", "lss", "nvl", "nvk", "nvr",
                              *newton("nr"), "rqn", "lnorm"])
        v_retr = steps("v_retr", ["qrT", "lmkT", "masked", "max", "sub", "sum", "rec"])
        v_q = steps("v_q", [f"ss{u}" for u in range(HKV)] + newton("rnq"))
        v_x2 = steps("v_x2", ["mod", "copy", "x0", "x1", "bn0", "bn1", "mod2", "ag0", "ag1", "var", *newton("rs"), "xn0", "xn1",
                              "h0", "h1", "hi"])
        v_gate = steps("v_gate", ["sc", "m1", "e1", "k1", "x1", "s1", "sc2", "m2", "e2", "k2", "x2", "s2", "den",
                                  "rec", "sel", "num", "c", "hi", "pad", "lo", "cT"])
        a_kv = steps("a_kv", ["kraw0", "ksq0", "kraw1", "ksq1"])
        a_v = steps("a_v", ["v0", "v1"])
        a_kT = steps("a_kT", ["a", "b"])
        a_retr = steps("a_retr", ["exp"])
        a_q = steps("a_q", [f"{n}{m}{u}" for u in range(HKV) for m in "ab" for n in ("sq", "q")])
        a_gate = steps("a_gate", ["tanh"])
        g_h = steps("g_h", ["h"])
        g_kn = steps("g_kn", ["0", "1"])
        g_rw = steps("g_rw", [f"r{i}" for i in range(1, C)])
        g_keep = steps("g_keep", ["x2", "lo"])
        pe_qk = steps("pe_qk", ["A", "B"], HKV)
        pe_pt = steps("pe_pt", ["0", "1", "2"], 2)
        pe_pv = steps("pe_pv", ["0", "1"])
        pe_o = steps("pe_o", ["o"], 2)
        v_sc = steps("v_sc", ["maxA", "subA", "maxB", "subB"])
        v_w = steps("v_w", ["sum", "rec", "w", "prob"], 2)
        a_exp = steps("a_exp", [f"e{i}" for i in BANK_A + BANK_B])
        a_pt = steps("a_pt", ["0", "1", "2"])
        a_ao = steps("a_ao", ["0", "1"])
        g_pr = steps("g_pr", ["p"], 2)

        f_whi, f_wlo = steps("f_whi", ["w"]), steps("f_wlo", ["w"])
        f_pe_h, f_pe_y = steps("f_pe_h", ["h", "u", "c"]), steps("f_pe_y", ["y"])
        f_act = steps("f_act", ["th"])
        f_ghi = steps("f_ghi", ["hi"])
        f_dve = steps("f_dve", ["a", "b", "g", "lo"])
        f_fin = sem("f_fin")

        ring = [("R", v_kv, "rraw"), ("K0", a_kv, "ksq0"), ("K1", a_kv, "ksq1"), ("tx", v_x2, "xn1"), ("th", v_x2, "h1"),
                ("lmean", v_kv, "lsum"), ("qa0", a_q, "qa0"), ("qb0", a_q, "qb0"), ("qa1", a_q, "qa1"), ("ss0", v_q, "ss0"),
                ("qb1", a_q, "qb1"), ("qrT", v_retr, "lmkT"), ("tg", a_gate, "tanh"), ("kTa", a_kT, "a"), ("kTb", a_kT, "b"),
                ("ss1", v_q, "ss1"), ("qa2", a_q, "qa2"), ("qb2", a_q, "qb2"), ("scores", v_retr, "masked"), ("qa3", a_q, "qa3"),
                ("ss2", v_q, "ss2"), ("qb3", a_q, "qb3"), ("tc", v_gate, "cT"), ("ss3", v_q, "ss3"), ("V0", a_v, "v0"), ("V1", a_v, "v1")]
        ring_names = [r[0] for r in ring]

        def ring_bank(name):
            return ring_names.index(name) % 2

        def bank(name):
            return ps[:, ring_bank(name), :]

        xn_done = {}
        block = top.enter_context(nc.Block())

        @block.sync
        def _(sp):
            sp.dma_start(cT_sb[:, :, :], cT.rearrange("(k p) b -> p k b", p=P)).then_inc(ld_c, 16)
            sp.dma_start(xn[:, 0:NT, :], x[0, :, :].rearrange("(t p) d -> p t d", p=P)).then_inc(ld_x0, 16)
            wm = wmod.rearrange("(k p) n -> p k n", p=P)
            sp.dma_start(wmod_sb[:, :, 0:2 * D], wm[:, :, 0:2 * D]).then_inc(ld_mod_a, 16)
            sp.dma_start(gd[:, :, :], gains_d).then_inc(ld_gain, 16)
            sp.dma_start(ghd[:, :], gains_hd).then_inc(ld_gain, 16)
            sp.dma_start(grd[:, :], gains_rd).then_inc(ld_gain, 16)
            for w, n0, n in ((wk, 0, KVW), (wr, 2 * KVW, RD), (wl, 2 * KVW + RD, RD)):
                sp.dma_start(w_kv[:, :, n0:n0 + n], w.rearrange("(k p) n -> p k n", p=P)).then_inc(ld_k, 16)
            sp.dma_start(xn[:, NT:B * NT, :], x[1:B, :, :].rearrange("b (t p) d -> p (b t) d", p=P)).then_inc(ld_x, 16)
            for k in range(KF):
                sp.dma_start(w_q[:, k, :], wq[k * P:(k + 1) * P, :]).then_inc((ld_q0, ld_q1)[k], 16)
            sp.dma_start(w_kv[:, :, KVW:2 * KVW], wv.rearrange("(k p) n -> p k n", p=P)).then_inc(ld_v, 16)
            sp.dma_start(wmod_sb[:, :, 2 * D:6 * D], wm[:, :, 2 * D:6 * D]).then_inc(ld_mod_b, 16)
            sp.dma_start(x2T[:, :, :, :], xT.rearrange("(k p) b l -> p k b l", p=P)).then_inc(ld_xT, 16)
            sp.dma_start(w_o[:, :, :], wo.rearrange("(h p) n -> p h n", p=P)).then_inc(ld_o, 16)
            sp.dma_start(gate_sb[:, :, :], gateT.rearrange("(k p) e -> p k e", p=P)).then_inc(ld_gate, 16)
            for j in range(2):
                sp.dma_start(w_raw[:, j, :, :], wffn[j, :, :, :]).then_inc(ld_w[j], 16)
            with sp.Fori(0, (NJP - 2) // 2) as n:
                for j in range(2):
                    sp.wait_ge(*f_whi.at(n * 2, "w", j))
                    sp.wait_ge(*f_wlo.at(n * 2, "w", j))
                    sp.dma_start(w_raw[:, j, :, :], wffn[bass.ds(n * 2 + 2 + j, 1), :, :, :].rearrange("o p s n -> p (o s) n"))\
                      .then_inc(ld_w[j], 16)
            for n in range(KF * 2):
                k, half = n % 2, n // 2
                sp.wait_ge(f_fin, 2 * (n + 1))
                sp.dma_start(out[k * P:(k + 1) * P, 2 * half:2 * half + 2, :], f_out[:, k, 2 * half:2 * half + 2, :]).then_inc(st_out, 16)
            sp.wait_ge(st_out, 16 * KF * 2)

        def weigh_pairs(eng, u, p0, p1):
            seg = d_sc[:, u % 2, S * p0:S * p1].rearrange("p (n k) -> p n k", k=S)
            w = wpair[:, u % 2, p0:p1].unsqueeze(2).broadcast_to([P, p1 - p0, S])
            return eng.tensor_tensor(seg, seg, w, ALU.mult)

        @block.gpsimd
        def _(pool):
            for st in (g_h, g_kn, g_rw, g_pr, g_keep, f_wlo):
                st.start(pool)
            n = 0

            def const(ins):
                nonlocal n
                ins.then_inc(pool_const, 1)
                n += 1
                pool.wait_ge(pool_const, n)

            const(pool.memset(ident[:, :], 0.0))
            const(pool.affine_select(out=ident[:, :], in_=ident[:, :], compare_op=ALU.not_equal, fill=1.0,
                                     base=0, pattern=[[-1, P]], channel_multiplier=1))
            const(pool.memset(ones[:, :], 1.0))
            for m in range(4):
                const(pool.tensor_copy(pick[:, m, :].rearrange("p (r q) -> p r q", q=S),
                                       ident[:, m * S:(m + 1) * S].unsqueeze(1).broadcast_to([P, G, S])))
            const(pool.memset(chunk_mean[:, :, :], 1.0 / S))
            const(pool.affine_select(out=chunk_mean[:, :, :], in_=chunk_mean[:, :, :], compare_op=ALU.is_ge, fill=0.0,
                                     base=0, pattern=[[P, NT], [-S, C]], channel_multiplier=1))
            const(pool.affine_select(out=chunk_mean[:, :, :], in_=chunk_mean[:, :, :], compare_op=ALU.is_ge, fill=0.0,
                                     base=S - 1, pattern=[[-P, NT], [S, C]], channel_multiplier=-1))
            for e in range(E):
                const(pool.memset(rank[:, :, e:e + 1], float(E - e)))
            const(pool.memset(causal[:, :, :], 0.0))
            for i in range(1, C):
                const(pool.memset(causal[:, i - 1, i:C], -1e30))
            const(pool.memset(cpad[:, :, :], 0.0))
            const(pool.memset(cfull[:, :, E:E + 1], 0.5))
            const(pool.memset(nv[:, NV - 1:NV], 1.0))
            assert n == POOL_CONSTS, n

            def take_h(b, o):
                pool.wait_ge(*pe_v.at(b, "V1", o - 1))
                pool.tensor_copy(hcur[:, :, :], hT[:, :, bass.ds(b + o, 1), :].rearrange("p k o l -> p k (o l)")).then_inc(*g_h.does("h"))

            def keys(b, o):
                pool.wait_ge(*v_kv.at(b, "nr.10", o))
                pool.wait_ge(*a_kv.at(b, "kraw1", o))
                for t in range(NT):
                    kk = kraw[:, t, :].rearrange("p (g d) -> p g d", d=HD)
                    r = nr[:, t * HKV:(t + 1) * HKV].unsqueeze(2).broadcast_to([P, HKV, HD])
                    pool.tensor_tensor(kk, kk, r, ALU.mult).then_inc(*g_kn.does(str(t)))

            def chunk_weights(b, o):
                pool.wait_ge(*v_retr.at(b, "rec", o))
                pool.wait_ge(*v_w.at(b * HKV, "w", (o - 1) * HKV + 3))
                for i in range(1, C):
                    pool.tensor_tensor(rw[:, PAIR0[i]:PAIR0[i] + i], rex[:, i - 1, 0:i], rrec[:, i - 1:i].broadcast_to([P, i]), ALU.mult)\
                        .then_inc(*g_rw.does(f"r{i}"))

            def weigh(b, u):
                pool.wait_ge(*v_w.at(b * HKV, "w", u))
                weigh_pairs(pool, u, 0, PAIRS_A).then_inc(*g_pr.does("p"))

            def keep_x2(b, o):
                pool.wait_ge(*v_x2.at(b, "x1", o))
                pool.tensor_copy(x2T[:, :, bass.ds(b + o, 1), :].rearrange("p k o l -> p k (o l)"), x2cur[:, :, :])\
                    .then_inc(*g_keep.does("x2"))

            def keep_lo(b, o):
                pool.wait_ge(*v_x2.at(b, "hi", o))
                pool.tensor_tensor(f_x_lo[:, :, bass.ds(b + o, 1), :].rearrange("p k o l -> p k (o l)"), h2cur,
                                   f_x_hi[:, :, bass.ds(b + o, 1), :].rearrange("p k o l -> p k (o l)").bitcast(F32), ALU.subtract)\
                    .then_inc(*g_keep.does("lo"))

            def iteration(b, head, tail_):
                if head:
                    take_h(b, 1)
                weigh(b, 1)
                if tail_:
                    keep_x2(b, -1)
                    keep_lo(b, -1)
                weigh(b, 2)
                if head:
                    keys(b, 1)
                weigh(b, 3)
                if head:
                    chunk_weights(b, 1)
                    weigh(b, 4)

            keys(0, 0)
            chunk_weights(0, 0)
            weigh(0, 0)
            pool.wait_ge(h_ready, KF * B)
            iteration(0, True, False)
            with pool.Fori(1, B - 1) as b:
                iteration(b, True, True)

            def w_low(j, o, i, buf):
                pool.wait_ge(*f_whi.at(j, "w", o))
                pool.tensor_tensor(w_lo[:, buf, :, :], w_raw[:, i, 0:NW - 1, :], w_hi[:, buf, 0:NW - 1, :].bitcast(F32), ALU.subtract)\
                    .then_inc(*f_wlo.does("w"))

            for j in range(2):
                w_low(j, 0, j, j)
            iteration(B - 1, False, True)
            w_low(2, 0, 0, 2)
            keep_x2(B - 1, 0)
            keep_lo(B - 1, 0)
            w_low(3, 0, 1, 0)
            with pool.Fori(1, (NJ - 1) // 2) as n:
                w_low(n * 2, 2, 0, 1)
                w_low(n * 2, 3, 1, 0)

        @block.scalar
        def _(act):
            for st in (a_kv, a_v, a_kT, a_retr, a_q, a_exp, a_pt, a_ao, a_gate, f_whi, f_act, f_ghi):
                st.start(act)
            act.wait_ge(ld_c, 16)
            act.activation(silu_c[:, :, :], cT_sb[:, :, :], ACT.Tanh, scale=0.5).then_inc(silu_steps, 1)
            act.wait_ge(gains_ready, GAINS)
            act.wait_ge(ld_k, 48)
            for k in range(KF):
                for n0, n1, g in ((0, KVW, g_att), (2 * KVW, 2 * KVW + RD, g_retr), (2 * KVW + RD, NKV, g_att)):
                    act.activation(w_kv[:, k, n0:n1], w_kv[:, k, n0:n1], ACT.Copy, scale=g[:, k:k + 1]).then_inc(wk_scaled, 1)
            act.wait_ge(h_ready, KF)
            act.activation(hcur[:, :, :], hT[:, :, 0, :], ACT.Copy).then_inc(h0_taken, 1)

            def h_squares(b):
                act.activation(h_sq[:, :, b, :], hT[:, :, b, :], ACT.Square).then_inc(hsq_ready, 1)

            h_squares(0)
            act.wait_ge(ld_q1, 16)
            act.activation(w_q[:, 1, :], w_q[:, 1, :], ACT.Copy, scale=gd[:, 0, 1:2]).then_inc(wq_scaled_a, 1)

            def key_tiles(b, o):
                act.wait_ge(*pe_kT.at(b, "kTb", o - 1))
                for t in range(NT):
                    act.wait_ge(*pe_kv.at(b, f"K{t}", o))
                    act.activation(kraw[:, t, :], bank(f"K{t}"), ACT.Copy).then_inc(*a_kv.does(f"kraw{t}"))
                    act.wait_ge(*(v_kv.at(b, "kss0", o) if t else v_kv.at(b, "kss1", o - 1)))
                    act.activation(squares[:, :], bank(f"K{t}"), ACT.Square).then_inc(*a_kv.does(f"ksq{t}"))

            def value_tiles(b, o):
                for t in range(NT):
                    act.wait_ge(*pe_v.at(b, f"V{t}", o))
                    act.wait_ge(*v_kv.at(b, "stok", o))
                    act.wait_ge(*pe_pv.at(b * HKV, "1", (o - 1) * HKV + 3))
                    act.activation(v_sb[:, t, :], bank(f"V{t}"), ACT.Copy, scale=stok[:, t:t + 1]).then_inc(*a_v.does(f"v{t}"))

            def queries(b, o, u, m):
                name = f"{'ab'[m]}{u}"
                act.wait_ge(*pe_q.at(b, f"q{name}", o))
                act.wait_ge(*(pe_q.at(b, f"ss{u - 2}", o) if u > 1 else pe_q.at(b, f"ss{u + 2}", o - 1)))
                act.wait_ge(*pe_qk.at(b * HKV, "B", (o - 1) * HKV + u))
                src = bank(f"q{name}")[:, 0:2 * TQ].rearrange("p (h i q) -> p i h q", h=2, q=S)
                act.activation(q_sq[:, u % 2, :, 2 * m:2 * m + 2, :], src, ACT.Square).then_inc(*a_q.does(f"sq{name}"))
                act.activation(qT[:, u, :, 2 * m:2 * m + 2, :], src, ACT.Copy).then_inc(*a_q.does(f"q{name}"))

            def keys_T(b, o):
                act.wait_ge(*pe_qk.at(b * HKV, "B", (o - 1) * HKV + 3))
                for n, name in enumerate("ab"):
                    act.wait_ge(*pe_kT.at(b, f"kT{name}", o))
                    act.activation(kT[:, 2 * n:2 * n + 2, :], bank(f"kT{name}").rearrange("p (g l) -> p g l", l=L)[:, :, 0:TQ],
                                   ACT.Copy, scale=gqk[:, 0:1]).then_inc(*a_kT.does(name))

            def retrieval(b, o):
                act.wait_ge(*v_retr.at(b, "sub", o))
                act.wait_ge(*g_rw.at(b, f"r{NI}", o - 1))
                act.activation(rex[:, :, :], rsc[:, :, :], ACT.Exp).then_inc(*a_retr.does("exp"))

            def exps(b, u):
                act.wait_ge(*v_q.at(b, "rnq.10", u // HKV))
                for i in BANK_A + BANK_B:
                    act.wait_ge(*v_sc.at(b * HKV, "subA" if i in BANK_A else "subB", u))
                    seg = d_sc[:, u % 2, S * PAIR0[i]:S * (PAIR0[i] + i)]
                    act.activation(seg, seg, ACT.Exp, scale=rnq[:, u % HKV, i - 1:i]).then_inc(*a_exp.does(f"e{i}"))

            def probs_T(b, u):
                act.wait_ge(*pe_pv.at(b * HKV, "1", u - 1))
                for n, (bk, rows, c0, c1) in enumerate(((R0, P, 3, 7), (R2, TQ - P, 7, 10), (R1, TQ - P, 0, 3))):
                    act.wait_ge(*pe_pt.at(b * HKV, str(n), u))
                    act.activation(pt[0:rows, c0:c1, :].rearrange("p c r -> p (c r)"), ps[0:rows, bk, 0:(c1 - c0) * P],
                                   ACT.Copy).then_inc(*a_pt.does(str(n)))

            def outputs(b, u):
                act.wait_ge(*pe_o.at(b * HKV, "o", u - 2))
                for n, (bk, i0, i1) in enumerate(((R0, 3, 7), (R1, 0, 3))):
                    act.wait_ge(*pe_pv.at(b * HKV, str(n), u))
                    act.activation(ao[:, u % 2, i0:i1, :, :].rearrange("p i h q -> p (i h q)"), ps[:, bk, 0:(i1 - i0) * P],
                                   ACT.Copy).then_inc(*a_ao.does(str(n)))

            def gate_scores(b, o):
                act.wait_ge(*pe_tail.at(b, "gate", o))
                act.activation(gth[:, :, :], bank("tg")[:, 0:NT * E].rearrange("p (t e) -> p t e", e=E), ACT.Tanh, scale=0.5)\
                    .then_inc(*a_gate.does("tanh"))

            def iteration(b, head, tail_):
                probs_T(b, 0)
                exps(b, 1)
                outputs(b, 0)
                if head:
                    key_tiles(b, 1)
                probs_T(b, 1)
                exps(b, 2)
                outputs(b, 1)
                if head:
                    for u, m in ((0, 0), (0, 1), (1, 0), (1, 1)):
                        queries(b, 1, u, m)
                if tail_:
                    gate_scores(b, -1)
                probs_T(b, 2)
                exps(b, 3)
                outputs(b, 2)
                if head:
                    keys_T(b, 1)
                    for u, m in ((2, 0), (2, 1)):
                        queries(b, 1, u, m)
                    retrieval(b, 1)
                    for u, m in ((3, 0), (3, 1)):
                        queries(b, 1, u, m)
                probs_T(b, 3)
                if head:
                    exps(b, 4)
                outputs(b, 3)
                if head:
                    value_tiles(b, 1)

            key_tiles(0, 0)
            for u, m in ((0, 0), (0, 1), (1, 0), (1, 1)):
                queries(0, 0, u, m)
            queries(0, 0, 2, 0)
            for b in range(1, B):
                act.wait_ge(h_ready, KF * (b + 1))
                h_squares(b)
            retrieval(0, 0)
            queries(0, 0, 2, 1)
            keys_T(0, 0)
            act.wait_ge(ld_v, 16)
            for k in range(KF):
                act.activation(w_kv[:, k, KVW:2 * KVW], w_kv[:, k, KVW:2 * KVW], ACT.Copy, scale=g_att[:, k:k + 1]).then_inc(wv_scaled, 1)
            for u, m in ((3, 0), (3, 1)):
                queries(0, 0, u, m)
            exps(0, 0)
            value_tiles(0, 0)
            iteration(0, True, False)
            with act.Fori(1, B - 1) as b:
                iteration(b, True, True)

            def w_high(i, count, buf):
                act.wait_ge(ld_w[i], count)
                act.activation(w_hi[:, buf, :, :], w_raw[:, i, :, :], ACT.Copy).then_inc(*f_whi.does("w"))

            def gate(t, o, i, first=False, between=None):
                act.wait_ge(*f_pe_h.at(t, "h", o))
                if not first:
                    act.wait_ge(*f_dve.at(t, "a", o - 2))
                act.activation(f_th[:, i, :], ps[:, 2, :], ACT.Tanh, scale=0.5).then_inc(*f_act.does("th"))
                if between:
                    between()
                act.wait_ge(*f_dve.at(t, "g", o))
                if not first:
                    act.wait_ge(*f_pe_y.at(t, "y", o - 2))
                act.activation(f_g_hi[:, i, :], f_g[:, i, :], ACT.Copy).then_inc(*f_ghi.does("hi"))

            w_high(0, 16, 0)
            w_high(1, 16, 1)
            iteration(B - 1, False, True)
            act.wait_ge(*f_wlo.at(0, "w"))
            w_high(0, 32, 2)

            gate(0, 0, 0, True)
            gate(1, 0, 1, True, between=lambda: gate_scores(B - 1, 0))
            gate(2, 0, 0)

            def fourth_tile():
                act.wait_ge(*f_pe_y.at(2, "y"))
                w_high(1, 32, 0)

            gate(3, 0, 1, between=fourth_tile)
            gate(4, 0, 0)
            gate(5, 0, 1)
            with act.Fori(1, (NJ - 1) // 2) as n:
                gate(n * 4, 2, 0)
                act.wait_ge(*f_pe_y.at(n * 4, "y", 1))
                w_high(0, n * 16 + 32, 1)
                gate(n * 4, 3, 1)
                gate(n * 4, 4, 0)
                act.wait_ge(*f_pe_y.at(n * 4, "y", 3))
                w_high(1, n * 16 + 32, 0)
                gate(n * 4, 5, 1)

        @block.vector
        def _(dve):
            for st in (v_kv, v_retr, v_q, v_sc, v_w, v_x2, v_gate, f_dve):
                st.start(dve)

            def step(st, b, o, name, ins, wait=True):
                ins.then_inc(*st.does(name))
                if wait:
                    dve.wait_ge(*st.at(b, name, o))

            def rsqrt(signal, y, v):
                rows, cols = v.shape[0], v.shape[-1]
                t1, t2 = nw1[0:rows, 0:cols], nw2[0:rows, 0:cols]
                signal(0, dve.tensor_scalar(t1.bitcast(I32), v.bitcast(I32), 1, None, ALU.logical_shift_right))
                signal(1, dve.tensor_scalar(y.bitcast(I32), t1.bitcast(I32), -1.0, RSQRT_MAGIC, ALU.mult, ALU.add))
                for n in range(3):
                    signal(3 * n + 2, dve.scalar_tensor_tensor(out=t1, in0=y, scalar=-0.5, in1=y, op0=ALU.mult, op1=ALU.mult))
                    signal(3 * n + 3, dve.tensor_tensor(t2, t1, v, ALU.mult))
                    signal(3 * n + 4, dve.scalar_tensor_tensor(out=y, in0=t2, scalar=1.5, in1=y, op0=ALU.add, op1=ALU.mult))

            for bk in (R1, R2):
                dve.memset(ps[:, bk, :], 0.0).then_inc(bank_init, 1)

            dve.wait_ge(silu_steps, 1)
            dve.scalar_tensor_tensor(out=silu_c[:, :, :], in0=silu_c[:, :, :], scalar=1.0, in1=cT_sb[:, :, :],
                                     op0=ALU.add, op1=ALU.mult).then_inc(silu_steps, 1)

            n = 0

            def xstep(ins, wait=True):
                nonlocal n
                ins.then_inc(xn_steps, 1)
                n += 1
                if wait:
                    dve.wait_ge(xn_steps, n)

            def x_stats(t0, t1):
                for t in range(t0, t1):
                    xstep(dve.bn_stats(bn6[:, t, :], xn[:, t, :]), wait=t == t1 - 1)
                for t in range(t0, t1):
                    xstep(dve.bn_aggr(mv[:, t, :], bn6[:, t, :]), wait=t == t1 - 1)

            def x_scale(t0, t1):
                xstep(dve.tensor_scalar(var[:, t0:t1], mv[:, t0:t1, 1], EPS, None, ALU.add))
                rsqrt(lambda _, ins: xstep(ins), rstd[:, t0:t1], var[:, t0:t1])

            def x_normalise(t0, t1):
                for t in range(t0, t1):
                    xstep(dve.tensor_scalar(xn[:, t, :], xn[:, t, :], mv[:, t, 0:1], rstd[:, t:t + 1], ALU.subtract, ALU.mult), wait=False)
                    xn_done[t] = n

            def h(b, bk):
                dve.wait_ge(hT_prod, b + 1)
                for k in range(KF):
                    dve.tensor_scalar(hT[:, k, b, :], ps[:, bk, k * L:(k + 1) * L], modT[:, b, 2 + k:3 + k], modT[:, b, k:k + 1],
                                      ALU.mult, ALU.add).then_inc(h_ready, 1)

            m = 0

            def mod(ins):
                nonlocal m
                ins.then_inc(mod_steps, 1)
                m += 1
                dve.wait_ge(mod_steps, m)

            def mod_take(n0, n1):
                mod(dve.tensor_scalar(modT[:, :, n0:n1].rearrange("p b n -> p n b"),
                                      ps[:, OB, n0 * B:n1 * B].rearrange("p (n b) -> p n b", b=B), 0.5, None, ALU.mult))

            dve.wait_ge(ld_x0, 16)
            x_stats(0, NT)
            dve.wait_ge(ld_gain, 48)
            dve.tensor_tensor(g_att[:, :], gd[:, 0, :], gd[:, 1, :], ALU.mult).then_inc(gains_ready, 1)
            dve.tensor_tensor(g_retr[:, :], gd[:, 0, :], gd[:, 2, :], ALU.mult).then_inc(gains_ready, 1)
            dve.tensor_tensor(g_sq[:, :], gd[:, 0, :], gd[:, 0, :], ALU.mult).then_inc(gains_ready, 1)
            dve.scalar_tensor_tensor(out=gqk[:, :], in0=ghd[:, 0:1], scalar=float(HD) ** -0.5, in1=ghd[:, 1:2],
                                     op0=ALU.mult, op1=ALU.mult).then_inc(gains_ready, 1)
            dve.scalar_tensor_tensor(out=grl[:, :], in0=grd[:, 0:1], scalar=float(RD) ** -0.5, in1=grd[:, 1:2],
                                     op0=ALU.mult, op1=ALU.mult).then_inc(gains_ready, 1)
            dve.memset(statv[:, :, 0:1], EPS / D).then_inc(gains_ready, 1)
            dve.wait_ge(gains_ready, 6)
            dve.tensor_scalar(statv[:, :, 1], g_sq[:, :], 1.0 / D, EPS / D, ALU.mult, ALU.add).then_inc(gains_ready, 1)
            x_scale(0, NT)
            x_normalise(0, NT)
            dve.wait_ge(mod_product, 4)
            mod_take(0, 4)
            mod(dve.tensor_scalar(modT[:, :, 2:4], modT[:, :, 2:4], 1.0, None, ALU.add))
            assert m == MOD_A_STEPS, m
            h(0, 0)

            ns = 0

            def sstep(ins):
                nonlocal ns
                ins.then_inc(s_steps, 1)
                ns += 1
                dve.wait_ge(s_steps, ns)

            def token_stats(b0, b1, bk, group):
                dve.wait_ge(stat_prod, b1)
                sstep(dve.tensor_scalar(tok[:, b0:b1, :, :], ps[:, bk, 0:(b1 - b0) * 2 * NT].rearrange("p (b t s) -> p b s t", t=NT, s=2),
                                        EPS * EPS, None, ALU.add))
                v = var[:, b0 * NT:b1 * NT]
                sstep(dve.tensor_copy(v.rearrange("p (b t) -> p b t", t=NT), tok[:, b0:b1, 1, :]))
                sstep(dve.tensor_scalar(epsT[:, b0:b1, :], tok[:, b0:b1, 1, :], EPS, None, ALU.mult))
                rsqrt(lambda _, ins: sstep(ins), tscale[:, b0:b1, :].rearrange("p b t -> p (b t)"), v)
                dve.wait_ge(rows_prod, group + 1)
                sstep(dve.tensor_copy(qeps[:, b0:b1, :].rearrange("p b (t m) -> p m b t", t=NT),
                                      ps[:, bk, 64:64 + (b1 - b0) * C].rearrange("p (m b t) -> p m b t", b=b1 - b0, t=NT)))
                assert ns == S_STEPS * (group + 1), ns

            def modulations():
                dve.wait_ge(mod_product, 12)
                mod_take(4, 12)
                mod(dve.tensor_scalar(modT[:, :, 8:10], modT[:, :, 8:10], 1.0, None, ALU.add))
                for n0 in (4, 10):
                    seg = modT[:, :, n0:n0 + 2]
                    mod(dve.tensor_scalar(gsgn[:, :, :], seg, 0.0, 2.0, ALU.is_ge, ALU.mult))
                    mod(dve.scalar_tensor_tensor(out=gabs[:, :, :], in0=gsgn[:, :, :], scalar=-1.0, in1=seg, op0=ALU.add, op1=ALU.mult))
                    mod(dve.tensor_scalar(gabs[:, :, :], gabs[:, :, :], 0.25, None, ALU.max))
                    mod(dve.scalar_tensor_tensor(out=seg, in0=gsgn[:, :, :], scalar=-1.0, in1=gabs[:, :, :], op0=ALU.add, op1=ALU.mult))
                assert m == MOD_STEPS, m

            dve.wait_ge(ld_q0, 16)
            dve.tensor_scalar(w_q[:, 0, :], w_q[:, 0, :], gd[:, 0, 0:1], None, ALU.mult).then_inc(wq_scaled_v, 1)

            def residual():
                dve.wait_ge(ld_xT, 16)
                for b in range(B):
                    for k in range(KF):
                        dve.scalar_tensor_tensor(out=x2T[:, k, b, :], in0=hT[:, k, b, :], scalar=modT[:, b, 4 + k:5 + k],
                                                 in1=x2T[:, k, b, :], op0=ALU.mult, op1=ALU.add).then_inc(base_ready, 1)

            def retrieval_raw(b, o):
                dve.wait_ge(*pe_kv.at(b, "R", o))
                step(v_kv, b, o, "rraw", dve.tensor_copy(rraw[:, :, :], bank("R")[:, 0:NT * 2 * RD].rearrange("p (t r) -> p t r", t=NT)))
                step(v_kv, b, o, "rsq", dve.tensor_tensor(rsq[:, :, :], rraw[:, :, 0:RD], rraw[:, :, 0:RD], ALU.mult))
                step(v_kv, b, o, "rss", dve.tensor_reduce(rss[:, :], rsq[:, :, :], AX, ALU.add), wait=False)

            def landmark_scale(b, o):
                dve.wait_ge(*a_v.at(b, "v1", o - 1))
                step(v_kv, b, o, "stok", dve.tensor_scalar(stok[:, :], tscale[:, bass.ds(b + o, 1), :].rearrange("p o t -> p (o t)"),
                                                           1.0, None, ALU.mult))
                dve.wait_ge(*pe_retr.at(b, "lmean", o - 1))
                step(v_kv, b, o, "lmn", dve.tensor_tensor(lmn[:, :, :], rraw[:, :, RD:2 * RD], stok[:, :].unsqueeze(2).broadcast_to([P, NT, RD]), ALU.mult),
                     wait=False)

            def key_sums(b, o, t):
                dve.wait_ge(*a_kv.at(b, f"ksq{t}", o))
                step(v_kv, b, o, f"kss{t}", dve.tensor_reduce(kss[:, t, :], squares[:, :].rearrange("p (g d) -> p g d", d=HD), AX, ALU.add),
                     wait=t == 1)

            def norms(b, o):
                dve.wait_ge(*pe_retr.at(b, "lmean", o))
                step(v_kv, b, o, "lsum", dve.tensor_copy(lsum[:, :], bank("lmean")[0:C, 0:RD]))
                step(v_kv, b, o, "lsq", dve.tensor_tensor(lsq[:, :], lsum[:, :], lsum[:, :], ALU.mult))
                step(v_kv, b, o, "lss", dve.tensor_reduce(lss[:, :], lsq[:, :], AX, ALU.add))
                step(v_kv, b, o, "nvl", dve.tensor_scalar(nv[0:C, NV - 1:NV], lss[:, :], 1.0 / RD, EPS, ALU.mult, ALU.add), wait=False)
                eT = epsT[:, bass.ds(b + o, 1), :].rearrange("p o t -> p (o t)")
                nvk = nv[:, 0:NT * HKV].rearrange("p (t g) -> p t g", t=NT)
                step(v_kv, b, o, "nvk", dve.scalar_tensor_tensor(out=nvk, in0=kss[:, :, :], scalar=1.0 / HD,
                                                                 in1=eT.unsqueeze(2).broadcast_to([P, NT, HKV]), op0=ALU.mult, op1=ALU.add), wait=False)
                step(v_kv, b, o, "nvr", dve.scalar_tensor_tensor(out=nv[:, NT * HKV:NT * HKV + NT], in0=rss[:, :], scalar=1.0 / RD, in1=eT,
                                                                 op0=ALU.mult, op1=ALU.add))
                dve.wait_ge(*g_kn.at(b, "1", o - 1))
                rsqrt(lambda i, ins: step(v_kv, b, o, f"nr.{i}", ins), nr[:, :], nv[:, :])
                dve.wait_ge(*pe_retr.at(b, "qrT", o - 1))
                step(v_kv, b, o, "rqn", dve.tensor_tensor(rqn[:, :, :], rraw[:, :, 0:RD],
                                                          nr[:, NT * HKV:NT * HKV + NT].unsqueeze(2).broadcast_to([P, NT, RD]), ALU.mult), wait=False)
                step(v_kv, b, o, "lnorm", dve.tensor_scalar(lnorm[:, :], lsum[:, :], nr[0:C, NV - 1:NV], None, ALU.mult), wait=False)

            def retrieval_T(b, o):
                dve.wait_ge(*pe_retr.at(b, "qrT", o))
                dve.wait_ge(*pe_retr.at(b, "scores", o - 1))
                step(v_retr, b, o, "qrT", dve.tensor_copy(
                    qrT[:, :, :, :], bank("qrT")[0:RD, S:L].rearrange("p (i q) -> p i q", q=S).unsqueeze(2).broadcast_to([RD, NI, G, S])), wait=False)
                step(v_retr, b, o, "lmkT", dve.tensor_scalar(lmkT[:, :], bank("qrT")[0:RD, L:L + C], grl[:, 0:1], None, ALU.mult), wait=False)

            def retrieval_max(b, o):
                dve.wait_ge(*pe_retr.at(b, "scores", o))
                step(v_retr, b, o, "masked", dve.tensor_tensor(rsc[:, :, :], bank("scores")[:, 0:NI * C].rearrange("p (i c) -> p i c", c=C),
                                                               causal[:, :, :], ALU.add))
                step(v_retr, b, o, "max", dve.tensor_reduce(rmx[:, :], rsc[:, :, :], AX, ALU.max))
                step(v_retr, b, o, "sub", dve.tensor_tensor(rsc[:, :, :], rsc[:, :, :], rmx[:, :].unsqueeze(2).broadcast_to([P, NI, C]), ALU.subtract),
                     wait=False)

            def retrieval_sum(b, o):
                dve.wait_ge(*a_retr.at(b, "exp", o))
                step(v_retr, b, o, "sum", dve.tensor_reduce(rsum[:, :], rex[:, :, :], AX, ALU.add))
                step(v_retr, b, o, "rec", dve.reciprocal(rrec[:, :], rsum[:, :]), wait=False)

            def query_sums(b, o, u):
                dve.wait_ge(*pe_q.at(b, f"ss{u}", o))
                step(v_q, b, o, f"ss{u}", dve.scalar_tensor_tensor(
                    out=qvar[:, u, :], in0=bank(f"ss{u}")[:, 0:NI * BUSY].rearrange("p (i r) -> p i r", r=BUSY)[:, :, 0], scalar=1.0 / HD,
                    in1=qeps[:, bass.ds(b + o, 1), 1:C].rearrange("p o i -> p (o i)"), op0=ALU.mult, op1=ALU.add), wait=u == HKV - 1)

            def query_norms(b, o):
                dve.wait_ge(*a_exp.at(b * HKV, "e1", (o - 1) * HKV + 3))
                rsqrt(lambda i, ins: step(v_q, b, o, f"rnq.{i}", ins), rnq[:, :, :].rearrange("p u i -> p (u i)"),
                      qvar[:, :, :].rearrange("p u i -> p (u i)"))

            def scores(b, u):
                for name, bk, p0, p1 in (("A", SA, 0, PAIRS_A), ("B", SB, PAIRS_A, NPAIR)):
                    dve.wait_ge(*pe_qk.at(b * HKV, name, u))
                    src = ps[:, bk, 0:(p1 - p0) * S].rearrange("p (n k) -> p n k", k=S)
                    step(v_sc, b * HKV, u, f"max{name}", dve.tensor_reduce(smax[:, u % 2, p0:p1], src, AX, ALU.max))
                    dve.wait_ge(*pe_pt.at(b * HKV, "2", u - 2))
                    step(v_sc, b * HKV, u, f"sub{name}", dve.tensor_tensor(
                        d_sc[:, u % 2, p0 * S:p1 * S].rearrange("p (n k) -> p n k", k=S), src,
                        smax[:, u % 2, p0:p1].unsqueeze(2).broadcast_to([P, p1 - p0, S]), ALU.subtract), wait=False)

            def weights(b, u):
                dve.wait_ge(*a_exp.at(b * HKV, "e1", u))
                step(v_w, b * HKV, u, "sum", dve.tensor_reduce(ssum[:, u % 2, :], d_sc[:, u % 2, :].rearrange("p (n k) -> p n k", k=S), AX, ALU.add))
                step(v_w, b * HKV, u, "rec", dve.reciprocal(srec[:, u % 2, :], ssum[:, u % 2, :]))
                dve.wait_ge(*g_rw.at(b, f"r{NI}", u // HKV))
                dve.wait_ge(*g_pr.at(b * HKV, "p", u - 2))
                step(v_w, b * HKV, u, "w", dve.tensor_tensor(wpair[:, u % 2, :], srec[:, u % 2, :], rw[:, :], ALU.mult))
                step(v_w, b * HKV, u, "prob", weigh_pairs(dve, u, PAIRS_A, NPAIR), wait=False)

            def x2(b, o):
                step(v_x2, b, o, "mod", dve.tensor_scalar(mod_out[:, 0:2], modT[:, bass.ds(b + o, 1), 4:6].rearrange("p o n -> p (o n)"),
                                                          1.0, None, ALU.mult))
                dve.wait_ge(*g_keep.at(b, "x2", o - 1))
                dve.wait_ge(*pe_tail.at(b, "x", o - 1))
                step(v_x2, b, o, "copy", dve.tensor_scalar(x2cur[:, :, 0:S], x2T[:, :, bass.ds(b + o, 1), 0:S].rearrange("p k o l -> p k (o l)"),
                                                           1.0, None, ALU.mult), wait=False)
                dve.wait_ge(*pe_o.at(b * HKV, "o", o * HKV + HKV - 1))
                for k in range(KF):
                    step(v_x2, b, o, f"x{k}", dve.scalar_tensor_tensor(
                        out=x2cur[:, k, S:L], in0=ps[:, OB, k * TQ:(k + 1) * TQ], scalar=mod_out[:, k:k + 1],
                        in1=x2T[:, k, bass.ds(b + o, 1), S:L].rearrange("p o l -> p (o l)"), op0=ALU.mult, op1=ALU.add), wait=False)

            def x2_norm(b, o):
                dve.wait_ge(*pe_tail.at(b, "x", o))
                xp = bank("tx").rearrange("p (t d) -> p t d", d=D)
                for t in range(NT):
                    step(v_x2, b, o, f"bn{t}", dve.bn_stats(bn6o[:, t, :], xp[:, t, :]), wait=t == NT - 1)
                step(v_x2, b, o, "mod2", dve.tensor_scalar(mod_out[:, 2:6], modT[:, bass.ds(b + o, 1), 6:10].rearrange("p o n -> p (o n)"),
                                                           1.0, None, ALU.mult), wait=False)
                for t in range(NT):
                    step(v_x2, b, o, f"ag{t}", dve.bn_aggr(mvo[:, t, :], bn6o[:, t, :]), wait=t == NT - 1)
                step(v_x2, b, o, "var", dve.tensor_scalar(varo[:, :], mvo[:, :, 1], EPS, None, ALU.add))
                rsqrt(lambda i, ins: step(v_x2, b, o, f"rs.{i}", ins), rstdo[:, :], varo[:, :])
                dve.wait_ge(*g_keep.at(b, "lo", o - 1))
                dve.wait_ge(*pe_tail.at(b, "gate", o - 1))
                for t in range(NT):
                    step(v_x2, b, o, f"xn{t}", dve.tensor_scalar(xn2[:, t, :], xp[:, t, :], mvo[:, t, 0:1], rstdo[:, t:t + 1],
                                                                 ALU.subtract, ALU.mult), wait=False)

            def h2(b, o):
                dve.wait_ge(*pe_tail.at(b, "h", o))
                hp2 = bank("th").rearrange("p (k l) -> p k l", l=L)
                for k in range(KF):
                    step(v_x2, b, o, f"h{k}", dve.tensor_scalar(h2cur[:, k, :], hp2[:, k, :], mod_out[:, 4 + k:5 + k], mod_out[:, 2 + k:3 + k],
                                                                ALU.mult, ALU.add), wait=k == KF - 1)
                step(v_x2, b, o, "hi", dve.tensor_scalar(f_x_hi[:, :, bass.ds(b + o, 1), :].rearrange("p k o l -> p k (o l)"), h2cur,
                                                         1.0, None, ALU.mult), wait=False)

            def gate(b, o):
                def bc(a):
                    return a[:, :].unsqueeze(2).broadcast_to([P, NT, E])

                def g(name, ins, wait=True):
                    step(v_gate, b, o, name, ins, wait)

                dve.wait_ge(*a_gate.at(b, "tanh", o))
                g("sc", dve.tensor_scalar(gsc[:, :, :], gth[:, :, :], 0.5, 0.5, ALU.mult, ALU.add))
                for n, (score, gm, gx, gs) in enumerate(((gsc, gm1, gx1, gs1), (gsc2, gm2, gx2, gs2)), 1):
                    if n == 2:
                        g("sc2", dve.scalar_tensor_tensor(out=gsc2[:, :, :], in0=gs1[:, :, :], scalar=-4.0, in1=gsc[:, :, :],
                                                          op0=ALU.mult, op1=ALU.add))
                    g(f"m{n}", dve.tensor_reduce(gm[:, :], score[:, :, :], AX, ALU.max))
                    g(f"e{n}", dve.tensor_tensor(gk1[:, :, :], score[:, :, :], bc(gm), ALU.is_equal))
                    g(f"k{n}", dve.tensor_tensor(gk2[:, :, :], gk1[:, :, :], rank[:, :, :], ALU.mult))
                    g(f"x{n}", dve.tensor_reduce(gx[:, :], gk2[:, :, :], AX, ALU.max))
                    g(f"s{n}", dve.tensor_tensor(gs[:, :, :], gk2[:, :, :], bc(gx), ALU.is_equal))
                g("den", dve.scalar_tensor_tensor(out=gden[:, :], in0=gm1[:, :], scalar=1e-20, in1=gm2[:, :], op0=ALU.add, op1=ALU.add))
                g("rec", dve.reciprocal(grec[:, :], gden[:, :]), wait=False)
                g("sel", dve.tensor_tensor(gs1[:, :, :], gs1[:, :, :], gs2[:, :, :], ALU.add))
                g("num", dve.tensor_tensor(gsc2[:, :, :], gsc[:, :, :], gs1[:, :, :], ALU.mult))
                g("c", dve.scalar_tensor_tensor(out=cfull[:, :, 0:E], in0=gsc2[:, :, :], scalar=0.5 * ROUTED, in1=bc(grec), op0=ALU.mult, op1=ALU.mult))
                g("hi", dve.tensor_copy(c_hi[:, :, :], cfull[:, :, :]))
                dve.wait_ge(*pe_tail.at(b, "cT", o - 1))
                g("pad", dve.tensor_copy(cpad[:, :, 0:E + 1], c_hi[:, :, :].bitcast(F32)), wait=False)
                g("lo", dve.tensor_tensor(cpad[:, :, 32:32 + E + 1], cfull[:, :, :], c_hi[:, :, :].bitcast(F32), ALU.subtract), wait=False)

            def gate_T(b, o):
                dve.wait_ge(*pe_tail.at(b, "cT", o))
                step(v_gate, b, o, "cT", dve.tensor_scalar(cw[:, bass.ds(b + o, 1), :].rearrange("p o l -> p (o l)"), bank("tc")[0:64, 0:L],
                                                           1.0, None, ALU.mult), wait=False)

            def iteration(b, head, tail_):
                if tail_:
                    x2(b, -1)
                scores(b, 1)
                if head:
                    retrieval_raw(b, 1)
                    landmark_scale(b, 1)
                weights(b, 1)
                if head:
                    for t in range(NT):
                        key_sums(b, 1, t)
                if tail_:
                    x2_norm(b, -1)
                scores(b, 2)
                if tail_:
                    h2(b, -1)
                if head:
                    norms(b, 1)
                weights(b, 2)
                if head:
                    query_sums(b, 1, 0)
                    retrieval_T(b, 1)
                scores(b, 3)
                if tail_:
                    gate(b, -1)
                weights(b, 3)
                if head:
                    query_sums(b, 1, 1)
                    retrieval_max(b, 1)
                    query_sums(b, 1, 2)
                    retrieval_sum(b, 1)
                if tail_:
                    gate_T(b, -1)
                if head:
                    scores(b, 4)
                    query_sums(b, 1, 3)
                    query_norms(b, 1)
                    weights(b, 4)

            dve.wait_ge(pool_const, POOL_CONSTS)
            retrieval_raw(0, 0)
            token_stats(0, 1, SB, 0)
            landmark_scale(0, 0)
            for t in range(NT):
                key_sums(0, 0, t)
            dve.wait_ge(ld_x, 16)
            x_stats(NT, B * NT)
            norms(0, 0)
            query_sums(0, 0, 0)
            retrieval_T(0, 0)
            x_scale(NT, B * NT)
            x_normalise(NT, B * NT)
            query_sums(0, 0, 1)
            for b in range(1, B):
                h(b, R0 + b - 1)
            retrieval_max(0, 0)
            retrieval_sum(0, 0)
            query_sums(0, 0, 2)
            token_stats(1, B, SA, 1)
            scores(0, 0)
            query_sums(0, 0, 3)
            query_norms(0, 0)
            weights(0, 0)
            modulations()
            iteration(0, True, False)
            residual()
            with dve.Fori(1, B - 1) as b:
                iteration(b, True, True)
            iteration(B - 1, False, True)

            def gated(t, o, i, first=False, cb=0):
                dve.wait_ge(*f_act.at(t, "th", o))
                step(f_dve, t, o, "a", dve.scalar_tensor_tensor(out=f_a[:, i, :], in0=f_th[:, i, :], scalar=1.0, in1=ps[:, 2, :],
                                                                op0=ALU.add, op1=ALU.mult))
                dve.wait_ge(*f_pe_h.at(t, "u", o))
                step(f_dve, t, o, "b", dve.tensor_tensor(f_a[:, i, :], f_a[:, i, :], ps[:, 3, :], ALU.mult))
                dve.wait_ge(*f_pe_h.at(t, "c", o))
                step(f_dve, t, o, "g", dve.tensor_tensor(f_g[:, i, :], f_a[:, i, :], ps[:, cb, :], ALU.mult))
                dve.wait_ge(*f_ghi.at(t, "hi", o))
                if not first:
                    dve.wait_ge(*f_pe_y.at(t, "y", o - 2))
                step(f_dve, t, o, "lo", dve.tensor_tensor(f_g_lo[:, i, :], f_g[:, i, :], f_g_hi[:, i, :].bitcast(F32), ALU.subtract),
                     wait=False)

            x2(B - 1, 0)
            x2_norm(B - 1, 0)
            gated(0, 0, 0, True, R2)
            h2(B - 1, 0)
            gated(0, 1, 1, True, R2)
            gate(B - 1, 0)
            gate_T(B - 1, 0)
            gated(2, 0, 0)
            gated(3, 0, 1)
            gated(4, 0, 0)
            gated(5, 0, 1)
            with dve.Fori(1, (NJ - 1) // 2) as n:
                gated(n * 4, 2, 0)
                gated(n * 4, 3, 1)
                gated(n * 4, 4, 0)
                gated(n * 4, 5, 1)
            for n in range(KF * 2):
                k, half = n % 2, n // 2
                dve.wait_ge(*f_pe_y.at(2 * NJ - 2 + half, "y"))
                for b in (2 * half, 2 * half + 1):
                    dve.scalar_tensor_tensor(out=f_out[:, k, b, :], in0=ps[:, 4 + n, (b % 2) * L:(b % 2 + 1) * L],
                                             scalar=modT[:, b, 10 + k:11 + k], in1=x2T[:, k, b, :], op0=ALU.mult, op1=ALU.add)\
                       .then_inc(f_fin, 1)

        @block.tensor
        def _(pe):
            for st in (pe_kv, pe_v, pe_kT, pe_retr, pe_q, pe_tail, pe_qk, pe_pt, pe_pv, pe_o, f_pe_h, f_pe_y):
                st.start(pe)

            def product(out_, pairs, start=True, stop=True):
                for n, (w, m) in enumerate(pairs):
                    ins = pe.matmul(out_, w, m, start=start and n == 0, stop=stop and n == len(pairs) - 1,
                                    skip_group_check=True)
                return ins

            def split(w_hi_, w_lo_, m_hi, m_lo):
                return [(w_hi_, m_hi), (w_hi_, m_lo), (w_lo_, m_hi)]

            last = {}

            def take(name, b, o):
                bk = ring_bank(name)
                if bk in last:
                    st, b0, step_, o0 = last[bk]
                    pe.wait_ge(*st.at(b0, step_, o0))
                _, st, step_ = ring[ring_names.index(name)]
                last[bk] = (st, b, step_, o)
                return ps[:, bk, :]

            def mod_products(n0, n1):
                for n in range(n0, n1):
                    product(ps[:, OB, n * B:(n + 1) * B], [(wmod_sb[:, k, n * P:(n + 1) * P], silu_c[:, k, :]) for k in range(KF)])\
                        .then_inc(mod_product, 1)

            def h_transposes(b, bk):
                pe.wait_ge(xn_steps, xn_done[b * NT + NT - 1])
                for k in range(KF):
                    for t in range(NT):
                        ins = pe.transpose(ps[:, bk, k * L + t * P:k * L + (t + 1) * P], xn[:, b * NT + t, k * P:(k + 1) * P], ident[:, :])
                ins.then_inc(hT_prod, 1)

            def token_sums(b, bk, c0):
                pe.wait_ge(hsq_ready, b + 1)
                pe.wait_ge(gains_ready, GAINS)
                for t in range(NT):
                    ins = product(ps[:, bk, c0 + 2 * t:c0 + 2 * t + 2], [(h_sq[:, k, b, t * P:(t + 1) * P], statv[:, k, :]) for k in range(KF)])
                ins.then_inc(stat_prod, 1)

            def token_rows(b0, b1, bk, group):
                pe.wait_ge(s_steps, S_STEPS * group + 1)
                for m in range(4):
                    c0 = 64 + m * (b1 - b0) * NT
                    ins = product(ps[:, bk, c0:c0 + (b1 - b0) * NT], [(pick[:, m, :], tok[:, b0:b1, 0, :])])
                ins.then_inc(rows_prod, 1)

            def idle(count):
                for _ in range(count):
                    pe.transpose(ps[:, R0, 0:P], ident[:, :], ident[:, :])

            pe.wait_ge(pool_const, 2)
            idle(WARM)
            pe.wait_ge(ld_mod_a, 16)
            pe.wait_ge(silu_steps, 2)
            mod_products(0, 4)
            idle(KEEP_WARM[0])
            h_transposes(0, 0)
            idle(KEEP_WARM[1])

            def project_kv(name, b, o, t, n0):
                bk = take(name, b, o)
                product(bk, [(hcur[:, k, t * P:(t + 1) * P], w_kv[:, k, n0:n0 + KVW]) for k in range(KF)])\
                    .then_inc(*(pe_kv if name[0] == "K" else pe_v).does(name))

            def retrieval(b, o):
                bk = take("R", b, o)
                if type(b) is int and b + o == 0:
                    pe.wait_ge(h0_taken, 1)
                else:
                    pe.wait_ge(*g_h.at(b, "h", o - 1))
                for t in range(NT):
                    ins = product(bk[:, t * 2 * RD:(t + 1) * 2 * RD], [(hcur[:, k, t * P:(t + 1) * P], w_kv[:, k, 2 * KVW:]) for k in range(KF)])
                ins.then_inc(*pe_kv.does("R"))

            def chunk_means(b, o):
                bk = take("lmean", b, o)
                pe.wait_ge(*v_kv.at(b, "lmn", o))
                product(bk[0:C, 0:RD], [(chunk_mean[:, t, :], lmn[:, t, :]) for t in range(NT)]).then_inc(*pe_retr.does("lmean"))

            def queries(b, o, u, m):
                bk = take(f"q{'ab'[m]}{u}", b, o)
                for hh in range(2):
                    h = u * G + 2 * m + hh
                    ins = product(bk[:, hh * TQ:(hh + 1) * TQ], [(w_q[:, k, h * HD:(h + 1) * HD], hcur[:, k, S:L]) for k in range(KF)])
                ins.then_inc(*pe_q.does(f"q{'ab'[m]}{u}"))

            def query_sums(b, o, u):
                bk = take(f"ss{u}", b, o)
                pe.wait_ge(*a_q.at(b, f"sqb{u}", o))
                for i in range(NI):
                    ins = product(bk[:, i * BUSY:(i + 1) * BUSY], [(q_sq[:, u % 2, i, :, :].rearrange("p h q -> p (h q)"),
                                                                    ones[:, :].broadcast_to([P, BUSY]))])
                ins.then_inc(*pe_q.does(f"ss{u}"))

            def retrieval_T(b, o):
                bk = take("qrT", b, o)
                pe.wait_ge(*v_kv.at(b, "lnorm", o))
                for t in range(NT):
                    product(bk[0:RD, t * P:(t + 1) * P], [(rqn[:, t, :], ident[:, :])])
                product(bk[0:RD, L:L + C], [(lnorm[:, :], ident[0:C, 0:C])]).then_inc(*pe_retr.does("qrT"))

            def retrieval_scores(b, o):
                bk = take("scores", b, o)
                pe.wait_ge(*v_retr.at(b, "lmkT", o))
                for i in range(NI):
                    ins = product(bk[:, i * C:(i + 1) * C], [(qrT[:, i, :, :].rearrange("p h q -> p (h q)"), lmkT[:, :])])
                ins.then_inc(*pe_retr.does("scores"))

            def keys_T(b, o):
                for n, name in enumerate("ab"):
                    bk = take(f"kT{name}", b, o)
                    pe.wait_ge(*g_kn.at(b, "1", o))
                    for g in range(2):
                        for t, rows in ((0, P), (1, TQ - P)):
                            ins = pe.transpose(bk[:, g * L + t * P:g * L + t * P + rows],
                                               kraw[0:rows, t, (2 * n + g) * HD:(2 * n + g + 1) * HD], ident[0:rows, 0:rows])
                    ins.then_inc(*pe_kT.does(f"kT{name}"))

            def scores(b, u):
                o = u // HKV
                pe.wait_ge(*a_q.at(b, f"qb{u % HKV}", o))
                pe.wait_ge(*a_kT.at(b, "b", o))
                for name, bk, blocks in (("A", SA, BANK_A), ("B", SB, BANK_B)):
                    pe.wait_ge(*v_sc.at(b * HKV, f"sub{name}", u - 1))
                    for i in blocks:
                        c0 = (PAIR0[i] - PAIR0[blocks[0]]) * S
                        ins = product(ps[:, bk, c0:c0 + i * S], [(qT[:, u % HKV, i - 1, :, :].rearrange("p h q -> p (h q)"), kT[:, u % HKV, 0:i * S])])
                    ins.then_inc(*pe_qk.does(name))

            def transposes(b, u):
                pe.wait_ge(*g_pr.at(b * HKV, "p", u))
                pe.wait_ge(*v_w.at(b * HKV, "prob", u))
                for n, (bk, blocks, k0, (st, last_)) in enumerate((
                        (R0, range(4, 8), 0, (a_ao, "0")), (R2, range(5, 8), P, (a_pt, "1")), (R1, range(1, 4), 0, (a_ao, "1")))):
                    pe.wait_ge(*st.at(b * HKV, last_, u - 1))
                    for m, i in enumerate(blocks):
                        rows = min(P, i * S - k0)
                        c0 = PAIR0[i] * S + k0
                        ins = pe.transpose(ps[0:rows, bk, m * P:(m + 1) * P], d_sc[:, u % 2, c0:c0 + rows], ident[:, :])
                    ins.then_inc(*pe_pt.does(str(n)))

            def values(b, u):
                d = slice(u * HD, (u + 1) * HD)
                pe.wait_ge(*a_v.at(b, "v1"))
                pe.wait_ge(*a_pt.at(b * HKV, "2", u))
                product(ps[:, R0, :], [(v_sb[:, 0, d], pt[:, 3:7, :].rearrange("p c r -> p (c r)"))], stop=False)
                for m in range(3):
                    r = (m + 1) * S
                    ins = product(ps[:, R0, (m + 1) * P:(m + 2) * P], [(v_sb[0:r, 1, d], pt[0:r, 7 + m, :])], start=False)
                ins.then_inc(*pe_pv.does("0"))
                for m in range(3):
                    r = (m + 1) * S
                    ins = product(ps[:, R1, m * P:(m + 1) * P], [(v_sb[0:r, 0, d], pt[0:r, m, :])])
                ins.then_inc(*pe_pv.does("1"))

            def project(b, u):
                pe.wait_ge(*a_ao.at(b * HKV, "1", u))
                if u == 0:
                    pe.wait_ge(*v_x2.at(b, "x1", -1))
                for hh in range(G):
                    h = u * G + hh
                    for f in range(KF):
                        ins = product(ps[:, OB, f * TQ:(f + 1) * TQ], [(w_o[:, h, f * P:(f + 1) * P], ao[:, u % 2, :, hh, :])],
                                      start=(u == 0 and hh == 0 and f == 0), stop=(u == HKV - 1 and hh == G - 1))
                ins.then_inc(*pe_o.does("o"))

            def tail_x(b, o):
                bk = take("tx", b, o)
                pe.wait_ge(*v_x2.at(b, "x1", o))
                for t in range(NT):
                    for k in range(KF):
                        ins = pe.transpose(bk[:, t * D + k * P:t * D + (k + 1) * P], x2cur[:, k, t * P:(t + 1) * P], ident[:, :])
                ins.then_inc(*pe_tail.does("x"))

            def tail_h(b, o):
                bk = take("th", b, o)
                pe.wait_ge(*v_x2.at(b, "xn1", o))
                for k in range(KF):
                    for t in range(NT):
                        ins = pe.transpose(bk[:, k * L + t * P:k * L + (t + 1) * P], xn2[:, t, k * P:(k + 1) * P], ident[:, :])
                ins.then_inc(*pe_tail.does("h"))

            def tail_gate(b, o):
                bk = take("tg", b, o)
                pe.wait_ge(*v_x2.at(b, "h1", o))
                for t in range(NT):
                    ins = product(bk[:, t * E:(t + 1) * E], [(h2cur[:, k, t * P:(t + 1) * P], gate_sb[:, k, :]) for k in range(KF)])
                ins.then_inc(*pe_tail.does("gate"))

            def tail_c(b, o):
                bk = take("tc", b, o)
                pe.wait_ge(*v_gate.at(b, "lo", o))
                for t in range(NT):
                    ins = product(bk[0:64, t * P:(t + 1) * P], [(cpad[:, t, :], ident[:, :])])
                ins.then_inc(*pe_tail.does("cT"))

            def iteration(b, head, tail_):
                scores(b, 1)
                transposes(b, 0)
                if head:
                    retrieval(b, 1)
                    project_kv("K0", b, 1, 0, 0)
                values(b, 0)
                if head:
                    project_kv("K1", b, 1, 1, 0)
                if tail_:
                    tail_x(b, -1)
                scores(b, 2)
                transposes(b, 1)
                project(b, 0)
                if tail_:
                    tail_h(b, -1)
                values(b, 1)
                if head:
                    chunk_means(b, 1)
                    queries(b, 1, 0, 0)
                    queries(b, 1, 0, 1)
                    queries(b, 1, 1, 0)
                    query_sums(b, 1, 0)
                    queries(b, 1, 1, 1)
                    retrieval_T(b, 1)
                scores(b, 3)
                if tail_:
                    tail_gate(b, -1)
                transposes(b, 2)
                project(b, 1)
                values(b, 2)
                if head:
                    keys_T(b, 1)
                    query_sums(b, 1, 1)
                    queries(b, 1, 2, 0)
                    queries(b, 1, 2, 1)
                    retrieval_scores(b, 1)
                    queries(b, 1, 3, 0)
                    query_sums(b, 1, 2)
                    queries(b, 1, 3, 1)
                if tail_:
                    tail_c(b, -1)
                if head:
                    scores(b, 4)
                    query_sums(b, 1, 3)
                transposes(b, 3)
                project(b, 2)
                values(b, 3)
                if head:
                    project_kv("V0", b, 1, 0, KVW)
                    project_kv("V1", b, 1, 1, KVW)
                project(b, 3)

            pe.wait_ge(wk_scaled, 3 * KF)
            pe.wait_ge(h_ready, KF)
            retrieval(0, 0)
            token_sums(0, SB, 0)
            pe.wait_ge(pool_const, POOL_CONSTS)
            project_kv("K0", 0, 0, 0, 0)
            token_rows(0, 1, SB, 0)
            project_kv("K1", 0, 0, 1, 0)
            pe.wait_ge(wq_scaled_a, 1)
            pe.wait_ge(wq_scaled_v, 1)
            idle(KEEP_WARM[2])
            queries(0, 0, 0, 0)
            queries(0, 0, 0, 1)
            queries(0, 0, 1, 0)
            chunk_means(0, 0)
            query_sums(0, 0, 0)
            queries(0, 0, 1, 1)
            pe.wait_ge(bank_init, 2)
            retrieval_T(0, 0)
            query_sums(0, 0, 1)
            queries(0, 0, 2, 0)
            for b in range(1, B):
                h_transposes(b, R0 + b - 1)
            token_sums(1, SA, 0)
            retrieval_scores(0, 0)
            queries(0, 0, 2, 1)
            token_sums(2, SA, 2 * NT)
            keys_T(0, 0)
            queries(0, 0, 3, 0)
            token_sums(3, SA, 4 * NT)
            query_sums(0, 0, 2)
            queries(0, 0, 3, 1)
            token_rows(1, B, SA, 1)
            pe.wait_ge(s_steps, 2 * S_STEPS)
            scores(0, 0)
            pe.wait_ge(mod_steps, 1)
            pe.wait_ge(ld_mod_b, 16)
            mod_products(4, 6)
            query_sums(0, 0, 3)
            pe.wait_ge(wv_scaled, KF)
            project_kv("V0", 0, 0, 0, KVW)
            mod_products(6, 9)
            project_kv("V1", 0, 0, 1, KVW)
            mod_products(9, 12)
            pe.wait_ge(h_ready, KF * B)
            pe.wait_ge(mod_steps, MOD_A_STEPS + 1)
            pe.wait_ge(ld_o, 16)
            pe.wait_ge(ld_gate, 16)
            iteration(0, True, False)
            for name in ("V0", "V1"):
                assert ring[ring_names.index(name)][1:] == (last[ring_bank(name)][0], last[ring_bank(name)][2])
            with pe.Fori(1, B - 1) as b:
                for bk in last:
                    last[bk] = (last[bk][0], b, last[bk][2], 0)
                iteration(b, True, True)
            for bk in last:
                last[bk] = (last[bk][0], B - 1, last[bk][2], 0)
            iteration(B - 1, False, True)

            def hidden(j, t, o, half, i, cb=0, before_c=None):
                pe.wait_ge(*f_whi.at(j, "w"))
                pe.wait_ge(*f_wlo.at(j, "w"))
                xh, xl = (a[:, :, 2 * half:2 * half + 2, :].rearrange("p k b l -> p k (b l)") for a in (f_x_hi, f_x_lo))
                for name, bk, w0, step_ in (("h", 2, 0, "a"), ("u", 3, 2, "b")):
                    pe.wait_ge(*f_dve.at(t, step_, o - 1))
                    product(ps[:, bk, :], [x_ for k in range(KF) for x_ in split(
                        w_hi[:, i, w0 + k, :], w_lo[:, i, w0 + k, :], xh[:, k, :], xl[:, k, :])]).then_inc(*f_pe_h.does(name))
                if before_c:
                    before_c()
                pe.wait_ge(*f_dve.at(t, "g", o - 1))
                product(ps[:, cb, :], [(w_hi[0:64, i, 6, :], cw[:, 2 * half:2 * half + 2, :].rearrange("p b l -> p (b l)"))])\
                    .then_inc(*f_pe_h.does("c"))

            def down(t, o, half, i, first=False, buf=None):
                buf = half if buf is None else buf
                pe.wait_ge(*f_ghi.at(t, "hi", o))
                pe.wait_ge(*f_dve.at(t, "lo", o))
                for f in range(KF):
                    ins = product(ps[:, 4 + 2 * half + f, :], split(w_hi[:, i, 4 + f, :], w_lo[:, i, 4 + f, :],
                                                                    f_g_hi[:, buf, :], f_g_lo[:, buf, :]), start=first)
                ins.then_inc(*f_pe_y.does("y"))

            pe.wait_ge(*g_keep.at(1, "lo"))
            pe.wait_ge(*v_gate.at(1, "cT"))
            tail_x(B - 1, 0)
            hidden(0, 0, 0, 0, 0, R2)
            tail_h(B - 1, 0)
            hidden(1, 1, 0, 0, 1, R2)
            tail_gate(B - 1, 0)
            down(0, 0, 0, 0, True)
            down(1, 0, 0, 1, buf=1)
            pe.wait_ge(*g_keep.at(B - 1, "lo"))

            def last_weights():
                tail_c(B - 1, 0)
                pe.wait_ge(*v_gate.at(B - 1, "cT"))

            hidden(0, 2, 0, 1, 0, before_c=last_weights)
            hidden(1, 3, 0, 1, 1)
            down(2, 0, 1, 0, True, buf=0)

            def turn(n, last_odd, even, odd):
                hidden(n * 2, n * 4, 0, 0, even)
                down(n * 4, -1, 1, last_odd)
                hidden(n * 2, n * 4, 1, 1, even)
                down(n * 4, 0, 0, even)
                hidden(n * 2 + 1, n * 4, 2, 0, odd)
                down(n * 4, 1, 1, even)
                hidden(n * 2 + 1, n * 4, 3, 1, odd)
                down(n * 4, 2, 0, odd)

            turn(1, 1, 2, 0)
            with pe.Fori(2, (NJ - 1) // 2) as n:
                turn(n, 0, 1, 0)
            hidden(NJ - 1, 2 * NJ - 2, 0, 0, 1)
            down(2 * NJ - 3, 0, 1, 0)
            hidden(NJ - 1, 2 * NJ - 1, 0, 1, 1)
            down(2 * NJ - 2, 0, 0, 1)
            down(2 * NJ - 1, 0, 1, 1)


def kernel(**inputs):
    import numpy as np
    import concourse.bacc as bacc
    from concourse.bass_utils import run_bass_kernel_spmd

    g = {k.removeprefix("L0_").removeprefix("attn_").removeprefix("ffn_"): np.asarray(v) for k, v in inputs.items()}
    t = np.ascontiguousarray
    x = g["hidden_states"]
    pad = NJP * P - NHID

    def hidden_tiles(routed, shared):
        w = np.concatenate([routed.transpose(1, 0, 2).reshape(D, E * HE), shared], axis=1)
        w = np.pad(w, ((0, 0), (0, pad)))
        return w.reshape(KF, P, NJP, P).transpose(2, 1, 0, 3)

    w2 = np.pad(np.concatenate([g["w2"].reshape(E * HE, D), g["sw2"]], axis=0), ((0, pad), (0, 0))).reshape(NJP, P, KF, P)
    member = np.zeros((P, NJP * P), np.float32)
    for e in range(E + 1):
        member[e, e * HE:(e + 1) * HE] = 1.0
        member[32 + e, e * HE:(e + 1) * HE] = 1.0
    member = member.reshape(P, NJP, 1, P).transpose(1, 0, 2, 3)
    arrays = {
        "x": t(x),
        "xT": t(x.transpose(2, 0, 1)),
        "wq": t(g["w_q"].T), "wk": t(g["w_k"].T), "wv": t(g["w_v"].T),
        "wr": t(g["w_q_retr"].T), "wl": t(g["w_lmk"].T), "wo": t(g["w_o"].T),
        "gains_d": t(np.stack([g["g_pre"], g["g_chunk_norm"], g["g_pre_retr"]]).reshape(3, KF, P).transpose(2, 0, 1)),
        "gains_hd": t(np.stack([g["g_k_norm"], g["g_q_norm"]], axis=1)),
        "gains_rd": t(np.stack([g["g_q_retr"], g["g_lmk"]], axis=1)),
        "gateT": t(g["gate_w"].T), "cT": t(g["c"].T), "wmod": t(g["wmod"]),
        "wffn": t(np.concatenate([hidden_tiles(g["w1"], g["sw1"]), hidden_tiles(g["w3"], g["sw3"]), w2, member], axis=2)),
    }
    nc = bacc.Bacc("TRN2", target_bir_lowering=False, num_devices=1)
    handles = [nc.dram_tensor(k, a.shape, mybir.dt.from_np(a.dtype), kind="ExternalInput").ap() for k, a in arrays.items()]
    out = nc.dram_tensor("out", (D, B, L), F32, kind="ExternalOutput").ap()
    build(nc, *handles, out)
    r = run_bass_kernel_spmd(nc, [arrays], core_ids=[0])
    return np.ascontiguousarray(r.results[0]["out"].transpose(1, 2, 0))
```
